# Optimizing a Trainium2 kernel written in Bass

```python
import numpy as np
import jax
import jax.numpy as jnp

def _softmax(x, axis=-1):
    return jax.nn.softmax(x, axis=axis)
def _gelu(x):
    return jax.nn.gelu(x, approximate=True)
def _silu(x):
    return jax.nn.silu(x)
def _sigmoid(x):
    return jax.nn.sigmoid(x)
def _layernorm(x, axis=-1, eps=1e-5):
    m = jnp.mean(x, axis=axis, keepdims=True)
    v = jnp.var(x, axis=axis, keepdims=True)
    return (x - m) / jnp.sqrt(v + eps)
def _scatter_add(tgt, idx, src, axis=0):
    return tgt.at[idx].add(src)
def _segment_sum(src, seg, n):
    return jax.ops.segment_sum(src, seg, n)

kernel_name = 'mk_metaformer_d2_conv_nchw384_2a48f6'

def setup_inputs(seed: int = 0):
    np.random.seed(seed)
    _w = jnp.asarray
    def _rec_inputs():
        import jax
        import jax.numpy as jnp
        _gk = jax.random.key(seed)
        x = -0.0005963 + 1.001 * jax.random.normal(jax.random.fold_in(_gk, 1), (8, 384, 32, 32), jnp.float32)
        return x
    x = _rec_inputs()
    def _L0_conv_setup():
        import jax, jax.numpy as jnp
        import numpy as np
        D_MODEL = 384
        D_STATE = 16
        D_CONV = 3
        EXPAND = 2
        D_INNER = EXPAND * D_MODEL
        DT_RANK = (D_MODEL + 15) // 16
        B_, H_, W_ = (8, 32, 32)

        def _mamba(xseq, in_proj_w, conv_w, conv_b, x_proj_w, dt_proj_w, dt_proj_b, A_log, D, out_proj_w):
            B, L, _ = xseq.shape
            xz = xseq @ in_proj_w.T
            xin, z = jnp.split(xz, 2, axis=-1)
            xc = jnp.transpose(xin, (0, 2, 1))
            xc = jnp.pad(xc, ((0, 0), (0, 0), (D_CONV - 1, 0)))
            xc = jax.lax.conv_general_dilated(xc, conv_w[:, None, :], (1,), 'VALID', dimension_numbers=('NCH', 'OIH', 'NCH'), feature_group_count=D_INNER)
            xc = xc + conv_b[None, :, None]
            u = jax.nn.silu(jnp.transpose(xc, (0, 2, 1)))
            dbc = u @ x_proj_w.T
            dt = dbc[..., :DT_RANK]
            Bm = dbc[..., DT_RANK:DT_RANK + D_STATE]
            Cm = dbc[..., DT_RANK + D_STATE:]
            dt = jax.nn.softplus(dt @ dt_proj_w.T + dt_proj_b)
            A = -jnp.exp(A_log)

            def step(h, inp):
                dt_t, B_t, C_t, u_t = inp
                dA = jnp.exp(dt_t[..., None] * A)
                h = dA * h + (dt_t * u_t)[..., None] * B_t[:, None, :]
                y = jnp.einsum('bdn,bn->bd', h, C_t)
                return (h, y)
            h0 = jnp.zeros((B, D_INNER, D_STATE), xseq.dtype)
            _, ys = jax.lax.scan(step, h0, (jnp.swapaxes(dt, 0, 1), jnp.swapaxes(Bm, 0, 1), jnp.swapaxes(Cm, 0, 1), jnp.swapaxes(u, 0, 1)))
            y = jnp.swapaxes(ys, 0, 1) + u * D
            y = y * jax.nn.silu(z)
            return y @ out_proj_w.T
        key = jax.random.key(seed)
        ks = jax.random.split(key, 8)
        s = lambda k, shape, scale: jax.random.normal(k, shape, jnp.float32) * scale
        x = jax.random.normal(ks[0], (B_, D_MODEL, H_, W_), jnp.float32)
        in_proj_w = s(ks[1], (2 * D_INNER, D_MODEL), 0.02)
        conv_w = s(ks[2], (D_INNER, D_CONV), 0.1)
        conv_b = jnp.zeros((D_INNER,), jnp.float32)
        x_proj_w = s(ks[3], (DT_RANK + 2 * D_STATE, D_INNER), 0.02)
        dt_proj_w = s(ks[4], (D_INNER, DT_RANK), 0.1)
        dt_proj_b = jnp.log(jnp.expm1(jnp.full((D_INNER,), 0.01, jnp.float32)))
        A_log = jnp.log(jnp.broadcast_to(jnp.arange(1, D_STATE + 1, dtype=jnp.float32), (D_INNER, D_STATE)))
        D = jnp.ones((D_INNER,), jnp.float32)
        out_proj_w = s(ks[5], (D_MODEL, D_INNER), 0.02)
        return dict(x=x, in_proj_w=in_proj_w, conv_w=conv_w, conv_b=conv_b, x_proj_w=x_proj_w, dt_proj_w=dt_proj_w, dt_proj_b=dt_proj_b, A_log=A_log, D=D, out_proj_w=out_proj_w)
    _L0_conv_all = _L0_conv_setup()
    _L0_conv_in = {k: v for k, v in _L0_conv_all.items() if k in ('in_proj_w', 'conv_w', 'conv_b', 'x_proj_w', 'dt_proj_w', 'dt_proj_b', 'A_log', 'D', 'out_proj_w', )}
    del _L0_conv_all

    def _L0_ffn_setup():
        import jax, jax.numpy as jnp
        import numpy as np
        NUM_GROUPS = 5
        EPS = 1e-05
        QB = 128.0

        def _binarize_weights_groupwise(W):
            n_out = W.shape[0]
            gs = n_out // NUM_GROUPS
            Wb = jnp.zeros_like(W)
            for g in range(NUM_GROUPS):
                wg = W[g * gs:(g + 1) * gs]
                z = wg - wg.mean()
                ste = z + jax.lax.stop_gradient(jnp.sign(z) - z)
                Wb = Wb.at[g * gs:(g + 1) * gs].set(ste)
            return Wb

        def _quantize_activations_groupwise(x):
            n = x.shape[0]
            gs = n // NUM_GROUPS
            xq = jnp.zeros_like(x)
            for g in range(NUM_GROUPS):
                ag = x[g * gs:(g + 1) * gs]
                gamma = jnp.max(jnp.abs(ag))
                xq = xq.at[g * gs:(g + 1) * gs].set(jnp.clip(ag * QB / (gamma + EPS), -QB + EPS, QB - EPS))
            return xq

        def _bitlinear(x, W, b):
            Wb = _binarize_weights_groupwise(W)
            y = jnp.einsum('btc,oc->bto', x, Wb) + b
            return _quantize_activations_groupwise(y)
        key = jax.random.key(seed)
        k1, k2, k3, k4, k5 = jax.random.split(key, 5)
        B, T, C = (10, 2048, 384)
        H = 4 * C
        lim1 = 1.0 / np.sqrt(C)
        lim2 = 1.0 / np.sqrt(H)
        x = jax.random.normal(k1, (B, T, C), dtype=jnp.float32)
        W1 = jax.random.uniform(k2, (H, C), minval=-lim1, maxval=lim1, dtype=jnp.float32)
        b1 = jax.random.uniform(k3, (H,), minval=-lim1, maxval=lim1, dtype=jnp.float32)
        W2 = jax.random.uniform(k4, (C, H), minval=-lim2, maxval=lim2, dtype=jnp.float32)
        b2 = jax.random.uniform(k5, (C,), minval=-lim2, maxval=lim2, dtype=jnp.float32)
        return {'x': x, 'W1': W1, 'b1': b1, 'W2': W2, 'b2': b2}
    _L0_ffn_all = _L0_ffn_setup()
    _L0_ffn_in = {k: v for k, v in _L0_ffn_all.items() if k in ('W1', 'b1', 'W2', 'b2', )}
    del _L0_ffn_all

    def _L1_conv_setup():
        import jax, jax.numpy as jnp
        from jax import lax
        import numpy as np
        H, W = (64, 64)
        K = 5
        SIGMA = 0.5
        CHAN_PER_POS = 8
        INIT_STRIDE = 16
        BATCH = 32

        def _num_offsets(h, w, s):
            ny = (h - s) // s * 2 + 1
            nx = (w - s) // s * 2 + 1
            return (ny, nx, ny * nx - 1)

        def _displace(x, off_int):
            _, _, _, h, w = x.shape

            def shift_one(xp, dxy):
                dx, dy = (dxy[0], dxy[1])
                ys = jnp.arange(h) - dy
                xs = jnp.arange(w) - dx
                ym = (ys >= 0) & (ys < h)
                xm = (xs >= 0) & (xs < w)
                ysc = jnp.clip(ys, 0, h - 1)
                xsc = jnp.clip(xs, 0, w - 1)
                out = xp[:, :, ysc][:, :, :, xsc]
                return out * (ym[:, None] & xm[None, :]).astype(xp.dtype)
            return jax.vmap(shift_one, in_axes=(1, 0), out_axes=1)(x, off_int)
        key = jax.random.key(seed)
        k1, k2 = jax.random.split(key)
        ny, nx, npos = _num_offsets(H, W, INIT_STRIDE)
        C = npos * CHAN_PER_POS
        x = jax.random.normal(k1, (BATCH, C, H, W), dtype=jnp.float32)
        offs = []
        for ih in range(-(ny // 2), ny // 2 + 1):
            for iw in range(-(nx // 2), nx // 2 + 1):
                if ih == 0 and iw == 0:
                    continue
                offs.append([iw * INIT_STRIDE, ih * INIT_STRIDE])
        offset = jnp.asarray(np.array(offs, dtype=np.float32))
        offset = offset + jax.random.uniform(k2, offset.shape, dtype=jnp.float32, minval=-0.4, maxval=0.4)
        return {'x': x, 'offset': offset}
    _L1_conv_all = _L1_conv_setup()
    _L1_conv_in = {k: v for k, v in _L1_conv_all.items() if k in ('offset', )}
    del _L1_conv_all

    def _L1_ffn_setup():
        import jax, jax.numpy as jnp
        import numpy as np
        NUM_GROUPS = 5
        EPS = 1e-05
        QB = 128.0

        def _binarize_weights_groupwise(W):
            n_out = W.shape[0]
            gs = n_out // NUM_GROUPS
            Wb = jnp.zeros_like(W)
            for g in range(NUM_GROUPS):
                wg = W[g * gs:(g + 1) * gs]
                z = wg - wg.mean()
                ste = z + jax.lax.stop_gradient(jnp.sign(z) - z)
                Wb = Wb.at[g * gs:(g + 1) * gs].set(ste)
            return Wb

        def _quantize_activations_groupwise(x):
            n = x.shape[0]
            gs = n // NUM_GROUPS
            xq = jnp.zeros_like(x)
            for g in range(NUM_GROUPS):
                ag = x[g * gs:(g + 1) * gs]
                gamma = jnp.max(jnp.abs(ag))
                xq = xq.at[g * gs:(g + 1) * gs].set(jnp.clip(ag * QB / (gamma + EPS), -QB + EPS, QB - EPS))
            return xq

        def _bitlinear(x, W, b):
            Wb = _binarize_weights_groupwise(W)
            y = jnp.einsum('btc,oc->bto', x, Wb) + b
            return _quantize_activations_groupwise(y)
        key = jax.random.key(seed)
        k1, k2, k3, k4, k5 = jax.random.split(key, 5)
        B, T, C = (10, 2048, 384)
        H = 4 * C
        lim1 = 1.0 / np.sqrt(C)
        lim2 = 1.0 / np.sqrt(H)
        x = jax.random.normal(k1, (B, T, C), dtype=jnp.float32)
        W1 = jax.random.uniform(k2, (H, C), minval=-lim1, maxval=lim1, dtype=jnp.float32)
        b1 = jax.random.uniform(k3, (H,), minval=-lim1, maxval=lim1, dtype=jnp.float32)
        W2 = jax.random.uniform(k4, (C, H), minval=-lim2, maxval=lim2, dtype=jnp.float32)
        b2 = jax.random.uniform(k5, (C,), minval=-lim2, maxval=lim2, dtype=jnp.float32)
        return {'x': x, 'W1': W1, 'b1': b1, 'W2': W2, 'b2': b2}
    _L1_ffn_all = _L1_ffn_setup()
    _L1_ffn_in = {k: v for k, v in _L1_ffn_all.items() if k in ('W1', 'b1', 'W2', 'b2', )}
    del _L1_ffn_all

    return {
        "x": x,
        "L0_conv_in_proj_w": _L0_conv_in["in_proj_w"],
        "L0_conv_conv_w": _L0_conv_in["conv_w"],
        "L0_conv_conv_b": _L0_conv_in["conv_b"],
        "L0_conv_x_proj_w": _L0_conv_in["x_proj_w"],
        "L0_conv_dt_proj_w": _L0_conv_in["dt_proj_w"],
        "L0_conv_dt_proj_b": _L0_conv_in["dt_proj_b"],
        "L0_conv_A_log": _L0_conv_in["A_log"],
        "L0_conv_D": _L0_conv_in["D"],
        "L0_conv_out_proj_w": _L0_conv_in["out_proj_w"],
        "L0_ffn_W1": _L0_ffn_in["W1"],
        "L0_ffn_b1": _L0_ffn_in["b1"],
        "L0_ffn_W2": _L0_ffn_in["W2"],
        "L0_ffn_b2": _L0_ffn_in["b2"],
        "L1_conv_offset": _L1_conv_in["offset"],
        "L1_ffn_W1": _L1_ffn_in["W1"],
        "L1_ffn_b1": _L1_ffn_in["b1"],
        "L1_ffn_W2": _L1_ffn_in["W2"],
        "L1_ffn_b2": _L1_ffn_in["b2"],
    }

def reference(x, L0_conv_in_proj_w, L0_conv_conv_w, L0_conv_conv_b, L0_conv_x_proj_w, L0_conv_dt_proj_w, L0_conv_dt_proj_b, L0_conv_A_log, L0_conv_D, L0_conv_out_proj_w, L0_ffn_W1, L0_ffn_b1, L0_ffn_W2, L0_ffn_b2, L1_conv_offset, L1_ffn_W1, L1_ffn_b1, L1_ffn_W2, L1_ffn_b2):
    import jax
    import jax.numpy as jnp
    def _L0_conv_ref(x, in_proj_w, conv_w, conv_b, x_proj_w, dt_proj_w, dt_proj_b, A_log, D, out_proj_w):
        import jax, jax.numpy as jnp
        import numpy as np
        D_MODEL = 384
        D_STATE = 16
        D_CONV = 3
        EXPAND = 2
        D_INNER = EXPAND * D_MODEL
        DT_RANK = (D_MODEL + 15) // 16
        B_, H_, W_ = (8, 32, 32)

        def _mamba(xseq, in_proj_w, conv_w, conv_b, x_proj_w, dt_proj_w, dt_proj_b, A_log, D, out_proj_w):
            B, L, _ = xseq.shape
            xz = xseq @ in_proj_w.T
            xin, z = jnp.split(xz, 2, axis=-1)
            xc = jnp.transpose(xin, (0, 2, 1))
            xc = jnp.pad(xc, ((0, 0), (0, 0), (D_CONV - 1, 0)))
            xc = jax.lax.conv_general_dilated(xc, conv_w[:, None, :], (1,), 'VALID', dimension_numbers=('NCH', 'OIH', 'NCH'), feature_group_count=D_INNER)
            xc = xc + conv_b[None, :, None]
            u = jax.nn.silu(jnp.transpose(xc, (0, 2, 1)))
            dbc = u @ x_proj_w.T
            dt = dbc[..., :DT_RANK]
            Bm = dbc[..., DT_RANK:DT_RANK + D_STATE]
            Cm = dbc[..., DT_RANK + D_STATE:]
            dt = jax.nn.softplus(dt @ dt_proj_w.T + dt_proj_b)
            A = -jnp.exp(A_log)

            def step(h, inp):
                dt_t, B_t, C_t, u_t = inp
                dA = jnp.exp(dt_t[..., None] * A)
                h = dA * h + (dt_t * u_t)[..., None] * B_t[:, None, :]
                y = jnp.einsum('bdn,bn->bd', h, C_t)
                return (h, y)
            h0 = jnp.zeros((B, D_INNER, D_STATE), xseq.dtype)
            _, ys = jax.lax.scan(step, h0, (jnp.swapaxes(dt, 0, 1), jnp.swapaxes(Bm, 0, 1), jnp.swapaxes(Cm, 0, 1), jnp.swapaxes(u, 0, 1)))
            y = jnp.swapaxes(ys, 0, 1) + u * D
            y = y * jax.nn.silu(z)
            return y @ out_proj_w.T
        B, C, H, W = x.shape
        xseq = jnp.transpose(x, (0, 2, 3, 1)).reshape(B, H * W, C)
        y = _mamba(xseq, in_proj_w, conv_w, conv_b, x_proj_w, dt_proj_w, dt_proj_b, A_log, D, out_proj_w)
        return jnp.transpose(y.reshape(B, H, W, C), (0, 3, 1, 2))

    def _L0_ffn_ref(x, W1, b1, W2, b2):
        import jax, jax.numpy as jnp
        import numpy as np
        NUM_GROUPS = 5
        EPS = 1e-05
        QB = 128.0

        def _binarize_weights_groupwise(W):
            n_out = W.shape[0]
            gs = n_out // NUM_GROUPS
            Wb = jnp.zeros_like(W)
            for g in range(NUM_GROUPS):
                wg = W[g * gs:(g + 1) * gs]
                z = wg - wg.mean()
                ste = z + jax.lax.stop_gradient(jnp.sign(z) - z)
                Wb = Wb.at[g * gs:(g + 1) * gs].set(ste)
            return Wb

        def _quantize_activations_groupwise(x):
            n = x.shape[0]
            gs = n // NUM_GROUPS
            xq = jnp.zeros_like(x)
            for g in range(NUM_GROUPS):
                ag = x[g * gs:(g + 1) * gs]
                gamma = jnp.max(jnp.abs(ag))
                xq = xq.at[g * gs:(g + 1) * gs].set(jnp.clip(ag * QB / (gamma + EPS), -QB + EPS, QB - EPS))
            return xq

        def _bitlinear(x, W, b):
            Wb = _binarize_weights_groupwise(W)
            y = jnp.einsum('btc,oc->bto', x, Wb) + b
            return _quantize_activations_groupwise(y)
        h = _bitlinear(x, W1, b1)
        h = jax.nn.gelu(h, approximate=False)
        out = _bitlinear(h, W2, b2)
        return out

    def _L1_conv_ref(x, offset):
        import jax, jax.numpy as jnp
        from jax import lax
        import numpy as np
        H, W = (64, 64)
        K = 5
        SIGMA = 0.5
        CHAN_PER_POS = 8
        INIT_STRIDE = 16
        BATCH = 32

        def _num_offsets(h, w, s):
            ny = (h - s) // s * 2 + 1
            nx = (w - s) // s * 2 + 1
            return (ny, nx, ny * nx - 1)

        def _displace(x, off_int):
            _, _, _, h, w = x.shape

            def shift_one(xp, dxy):
                dx, dy = (dxy[0], dxy[1])
                ys = jnp.arange(h) - dy
                xs = jnp.arange(w) - dx
                ym = (ys >= 0) & (ys < h)
                xm = (xs >= 0) & (xs < w)
                ysc = jnp.clip(ys, 0, h - 1)
                xsc = jnp.clip(xs, 0, w - 1)
                out = xp[:, :, ysc][:, :, :, xsc]
                return out * (ym[:, None] & xm[None, :]).astype(xp.dtype)
            return jax.vmap(shift_one, in_axes=(1, 0), out_axes=1)(x, off_int)
        B, C, h, w = x.shape
        P = offset.shape[0]
        cpp = C // P
        off_round = jnp.round(offset)
        off_int = off_round.astype(jnp.int32)
        disp = _displace(x.reshape(B, P, cpp, h, w), off_int).reshape(B, C, h, w)
        sub = offset - lax.stop_gradient(off_round)
        c = K // 2
        jj, ii = jnp.meshgrid(jnp.arange(K, dtype=jnp.float32) - c, jnp.arange(K, dtype=jnp.float32) - c, indexing='xy')
        field = jnp.stack([jj, ii], axis=-1)
        d = field[None] + sub[:, None, None, :]
        kernel = jnp.exp(-jnp.sum(d * d, axis=-1) / (2.0 * SIGMA ** 2))
        kernel = kernel / jnp.sum(kernel, axis=(1, 2), keepdims=True)
        kw = jnp.repeat(kernel, cpp, axis=0)[:, None]
        out = lax.conv_general_dilated(disp, kw, window_strides=(1, 1), padding=[(c, c), (c, c)], feature_group_count=C, dimension_numbers=('NCHW', 'OIHW', 'NCHW'))
        return out

    def _L1_ffn_ref(x, W1, b1, W2, b2):
        import jax, jax.numpy as jnp
        import numpy as np
        NUM_GROUPS = 5
        EPS = 1e-05
        QB = 128.0

        def _binarize_weights_groupwise(W):
            n_out = W.shape[0]
            gs = n_out // NUM_GROUPS
            Wb = jnp.zeros_like(W)
            for g in range(NUM_GROUPS):
                wg = W[g * gs:(g + 1) * gs]
                z = wg - wg.mean()
                ste = z + jax.lax.stop_gradient(jnp.sign(z) - z)
                Wb = Wb.at[g * gs:(g + 1) * gs].set(ste)
            return Wb

        def _quantize_activations_groupwise(x):
            n = x.shape[0]
            gs = n // NUM_GROUPS
            xq = jnp.zeros_like(x)
            for g in range(NUM_GROUPS):
                ag = x[g * gs:(g + 1) * gs]
                gamma = jnp.max(jnp.abs(ag))
                xq = xq.at[g * gs:(g + 1) * gs].set(jnp.clip(ag * QB / (gamma + EPS), -QB + EPS, QB - EPS))
            return xq

        def _bitlinear(x, W, b):
            Wb = _binarize_weights_groupwise(W)
            y = jnp.einsum('btc,oc->bto', x, Wb) + b
            return _quantize_activations_groupwise(y)
        h = _bitlinear(x, W1, b1)
        h = jax.nn.gelu(h, approximate=False)
        out = _bitlinear(h, W2, b2)
        return out

    def _gn(v, G=32, eps=1e-5):
        B_, C_, H_, W_ = v.shape
        g = v.reshape(B_, G, C_ // G, H_, W_)
        m = jnp.mean(g, axis=(2, 3, 4), keepdims=True)
        s = jnp.var(g, axis=(2, 3, 4), keepdims=True)
        return ((g - m) / jnp.sqrt(s + eps)).reshape(v.shape)

    def _ln_c(v, eps=1e-6):
        m = jnp.mean(v, axis=1, keepdims=True)
        s = jnp.var(v, axis=1, keepdims=True)
        return (v - m) / jnp.sqrt(s + eps)

    def _ln_t(v, eps=1e-5):
        m = jnp.mean(v, axis=-1, keepdims=True)
        s = jnp.var(v, axis=-1, keepdims=True)
        return (v - m) / jnp.sqrt(s + eps)

    def _to_tokens(v):
        B_, C_, H_, W_ = v.shape
        return v.reshape(B_, C_, H_ * W_).transpose(0, 2, 1)
    def _from_tokens(t, like):
        B_, C_, H_, W_ = like.shape
        return t.transpose(0, 2, 1).reshape(B_, C_, H_, W_)

    x = x + _L0_conv_ref(_ln_c(x), L0_conv_in_proj_w, L0_conv_conv_w, L0_conv_conv_b, L0_conv_x_proj_w, L0_conv_dt_proj_w, L0_conv_dt_proj_b, L0_conv_A_log, L0_conv_D, L0_conv_out_proj_w)
    t = _to_tokens(x)
    t = t + _L0_ffn_ref(_ln_t(t), L0_ffn_W1, L0_ffn_b1, L0_ffn_W2, L0_ffn_b2)
    x = _from_tokens(t, x)
    x = x + _L1_conv_ref(_ln_c(x), L1_conv_offset)
    t = _to_tokens(x)
    t = t + _L1_ffn_ref(_ln_t(t), L1_ffn_W1, L1_ffn_b1, L1_ffn_W2, L1_ffn_b2)
    x = _from_tokens(t, x)
    return x


_drawn_inputs = setup_inputs


def setup_inputs(seed=0):
    import zlib

    import numpy as np

    out = dict(_drawn_inputs(seed))
    spreads = {'L0_conv_conv_b': (0.0, 0.1),
     'L0_conv_dt_proj_b': (-4.600166320800781, 0.2),
     'L0_conv_D': (1.0, 0.2)}
    factors = {}
    for name, (base, spread) in spreads.items():
        noise = np.random.default_rng([zlib.crc32(name.encode()), seed]).standard_normal(out[name].shape)
        drawn = base * np.exp(spread * noise) if base else spread * noise
        out[name] = jnp.asarray(drawn.astype(out[name].dtype))
    for name, factor in factors.items():
        out[name] = (out[name] * factor).astype(out[name].dtype)
    return out
```

```python
import concourse.bass as bass
from concourse import mybir
from contextlib import ExitStack

F32 = mybir.dt.float32
BF16 = mybir.dt.bfloat16
F32R = mybir.dt.float32r
ALU = mybir.AluOpType
ACT = mybir.ActivationFunctionType
AX = mybir.AxisListType

P = 128
B, DM, HW = 8, 384, 1024
CT = DM // P
DI = 2 * DM
KT = DI // P
NS = 16
DTR = (DM + 15) // 16
T = 512
NCHUNK = B * HW // T
STEPS = KT * NS
BC = 2 * NS
DT0 = 3 * BC

OUT_AT = (2, 5, 8)
GATE_AT = (11, 19, 35, 51, 64, 69)
NORM_AT = 16
CONV_AT, CONV_GAP = 32, 5
XP_AT = 66
DT_AT, DT_GAP = 70, 2
SPREAD_AT = 81


def mixer(nc, x, x1, in_wT, conv_w, conv_b, xp_wT, dt_wT, dt_b, A_log, D, out_wT):
    with ExitStack() as ctx:
        def sb(name, shape, dt=F32):
            return ctx.enter_context(nc.sbuf_tensor(name, shape, dt))

        def bank(name):
            return ctx.enter_context(nc.psum_tensor(name, [P, T], F32))

        def sem(name):
            return ctx.enter_context(nc.semaphore(name))

        w_in = sb("w_in", [P, CT, 2 * DI])
        w_out = sb("w_out", [P, KT, DM])
        w_x = sb("w_x", [P, KT, DT0 + DTR])
        w_dt = sb("w_dt", [P, DI])
        cw = sb("cw", [P, KT, 3])
        cb = sb("cb", [P, KT])
        dtb = sb("dtb", [P, KT])
        dskip = sb("dskip", [P, KT])
        aneg = sb("aneg", [P, KT, NS])
        ident = sb("ident", [P, P])
        mean_w = sb("mean_w", [P, P])
        sel3 = sb("sel3", [P, BC], BF16)
        eps_c = sb("eps_c", [P, 1])
        zeros2 = sb("zeros2", [P, 2])
        xs = sb("xs", [P, 2, CT, T])
        xn = sb("xn", [P, 2, CT, T])
        sq = sb("sq", [P, CT, T])
        rstd = sb("rstd", [P, T])
        xin = sb("xin", [P, 2, T + 2])
        halo = sb("halo", [P, KT, 2])
        acc = sb("acc", [P, 2, T])
        th = sb("th", [P, 2, T])
        u = sb("u", [P, 2, KT, T])
        bc3 = sb("bc3", [P, T], BF16)
        bcr = sq[:, 0, :]
        bcm = sb("bcm", [P, T], BF16)
        dtr = sq[:, 1, :]
        rl = th
        sl = acc
        dt = sb("dt", [P, KT, T])
        dtu = sb("dtu", [P, 2, T])
        b_rep = sb("b_rep", [P, NS, T])
        c_rep = sb("c_rep", [P, NS, T])
        dbu = sb("dbu", [P, 3, T])
        hc = sb("hc", [P, 3, T])
        carry = sb("carry", [P, STEPS])
        gate = sb("gate", [P, 2, T])
        yy = sb("yy", [P, T])

        da = [bank("da0"), bank("da1")]
        hs = [bank("hs0"), bank("hs1"), sb("hs2", [P, T])]
        ys = [bank("ys0"), bank("ys1")]
        pp = bank("pp")
        pz = bank("pz")

        weights_in = sem("weights_in")
        consts = sem("consts")
        const_step = sem("const_step")
        halved = sem("halved")
        a_exp = sem("a_exp")
        x_loaded = [sem("x_loaded_first"), sem("x_loaded_second")]
        x_stored = [sem("x_stored_first"), sem("x_stored_second")]
        mean_full, centered, squared, var_full = sem("mean_full"), sem("centered"), sem("squared"), sem("var_full")
        ln_read, rstd_done, normed = sem("ln_read"), sem("rstd_done"), sem("normed")
        in_full, in_read, conv_part, conv_done = sem("in_full"), sem("in_read"), sem("conv_part"), sem("conv_done")
        th_done, u_done = sem("th_done"), sem("u_done")
        xp_full, xp_read, split_step, bc_done = sem("xp_full"), sem("xp_read"), sem("split_step"), sem("bc_done")
        dt_full, dt_read, sp_exp, sp_done, dt_done = sem("dt_full"), sem("dt_read"), sem("sp_exp"), sem("sp_done"), sem("dt_done")
        bb_full, bb_copied = sem("bb_full"), sem("bb_copied")
        cc_full, cc_copied = sem("cc_full"), sem("cc_copied")
        dtu_done, dbu_done = sem("dtu_done"), sem("dbu_done")
        exp_done, scan_done, mult_done, red_done, carried = sem("exp_done"), sem("scan_done"), sem("mult_done"), sem("red_done"), sem("carried")
        z_full, z_tanh, z_read = sem("z_full"), sem("z_tanh"), sem("z_read")
        y_read, gated = sem("y_read"), sem("gated")
        out_full, res_done = sem("out_full"), sem("res_done")
        block = ctx.enter_context(nc.Block())

        XV = x.rearrange("b (t p) s -> b p t s", p=P)
        X1V = x1.rearrange("b (t p) s -> b p t s", p=P)

        @block.sync
        def _(sp):
            for o, i in ((w_in[:], in_wT.rearrange("(t p) n -> p t n", p=P)),
                         (w_out[:], out_wT.rearrange("(t p) n -> p t n", p=P)),
                         (cw[:], conv_w.rearrange("(t p) j -> p t j", p=P)),
                         (aneg[:], A_log.rearrange("(t p) j -> p t j", p=P)),
                         (w_dt[DT0:DT0 + DTR, :], dt_wT)):
                sp.dma_start(o, i).then_inc(weights_in, 16)
            xw = xp_wT.rearrange("(t p) n -> p t n", p=P)
            for r in range(3):
                sp.dma_start(w_x[:, :, r * BC:(r + 1) * BC], xw[:, :, DTR:]).then_inc(weights_in, 16)
            sp.dma_start(w_x[:, :, DT0:], xw[:, :, 0:DTR]).then_inc(weights_in, 16)
            for o, i in ((cb, conv_b), (dtb, dt_b), (dskip, D)):
                sp.dma_start(o[:], i.rearrange("(t p) -> p t", p=P), allow_slow_non_contiguous=True).then_inc(weights_in, 16)

            def load(b, h):
                if not isinstance(b, int) or b > 0:
                    sp.wait_ge(x_stored[h], 16 * b)
                sp.dma_start(xs[:, h], XV[b, :, :, h * T:(h + 1) * T]).then_inc(x_loaded[h], 16)

            def store(b, h):
                sp.wait_ge(res_done, CT * (2 * b + h + 1))
                sp.dma_start(X1V[b, :, :, h * T:(h + 1) * T], xs[:, h]).then_inc(x_stored[h], 16)

            load(0, 0)
            load(0, 1)
            with sp.Fori(0, B - 1) as i:
                for h in range(2):
                    store(i, h)
                    load(i + 1, h)
            store(B - 1, 0)
            store(B - 1, 1)
            for h in range(2):
                sp.wait_ge(x_stored[h], 16 * B)

        @block.tensor
        def _(pe):
            mm = nc.tensor.matmul

            def norm_mean(d, h, image):
                pe.wait_ge(x_loaded[h], 16 * (image + 1))
                if not isinstance(d, int) or d > 0:
                    pe.wait_ge(bb_copied, NS * d)
                for t in range(CT):
                    last = mm(pp[:], mean_w[:], xs[:, h, t], start=t == 0, stop=t == CT - 1)
                last.then_inc(mean_full, 1)

            def norm_var(d):
                pe.wait_ge(squared, d + 1)
                for t in range(CT):
                    last = mm(pp[:], mean_w[:], sq[:, t], start=t == 0, stop=t == CT - 1)
                last.then_inc(var_full, 1)

            def in_proj(d, h, m):
                if m == 0:
                    pe.wait_ge(normed, d + 1)
                else:
                    pe.wait_ge(in_read, KT * d + m)
                for t in range(CT):
                    last = mm(pp[:], w_in[:, t, m * P:(m + 1) * P], xn[:, h, t], start=t == 0, stop=t == CT - 1)
                last.then_inc(in_full, 1)

            def x_proj(d, h):
                pe.wait_ge(u_done, KT * (d + 1))
                for k in range(KT):
                    last = mm(pp[0:DT0 + DTR, :], w_x[:, k], u[:, h, k], start=k == 0, stop=k == KT - 1)
                last.then_inc(xp_full, 1)

            def dt_proj(d, m):
                if m == 0:
                    pe.wait_ge(bc_done, d + 1)
                else:
                    pe.wait_ge(dt_read, KT * d + m)
                mm(pp[:], w_dt[DT0:DT0 + DTR, m * P:(m + 1) * P], dtr[DT0:DT0 + DTR, :],
                   start=True, stop=True).then_inc(dt_full, 1)

            def spread(d, n):
                if n == 0:
                    pe.wait_ge(dt_read, KT * (d + 1))
                    pe.wait_ge(bc_done, d + 1)
                else:
                    pe.wait_ge(bb_copied, NS * d + n)
                    pe.wait_ge(cc_copied, NS * d + n)
                if not isinstance(d, int) or d > 0:
                    if n == 0:
                        pe.wait_ge(z_read, KT * (d - 1) + KT)
                mm(pp[:], sel3[0:DT0, n:n + 1].broadcast_to([DT0, P]), bc3[0:DT0, :], start=True,
                   stop=True).then_inc(bb_full, 1)
                mm(pz[:], sel3[0:DT0, NS + n:NS + n + 1].broadcast_to([DT0, P]), bc3[0:DT0, :], start=True,
                   stop=True).then_inc(cc_full, 1)

            def gate_proj(c, h, k):
                if k > 0:
                    pe.wait_ge(z_read, KT * c + k)
                elif not isinstance(c, int) or c > 0:
                    pe.wait_ge(res_done, CT * c)
                else:
                    pe.wait_ge(cc_copied, NS)
                for t in range(CT):
                    last = mm(pz[:], w_in[:, t, DI + k * P:DI + (k + 1) * P], xn[:, h, t], start=t == 0, stop=t == CT - 1)
                last.then_inc(z_full, 1)

            def out_proj(c, h, m):
                if m == 0:
                    pe.wait_ge(gated, KT * (c + 1))
                    pe.wait_ge(z_read, KT * (c + 1))
                    if isinstance(c, int) and c == NCHUNK - 1:
                        pass
                    else:
                        pe.wait_ge(cc_copied, NS * (c + 2))
                else:
                    pe.wait_ge(res_done, CT * c + m)
                for k in range(KT):
                    last = mm(pz[:], w_out[:, k, m * P:(m + 1) * P], u[:, h, k], start=k == 0, stop=k == KT - 1)
                last.then_inc(out_full, 1)

            def reduce_state(c, k, n):
                s = STEPS * c + NS * k + n
                pe.wait_ge(mult_done, s + 1)
                if n == 0 and (not isinstance(c, int) or KT * c + k >= 2):
                    pe.wait_ge(y_read, KT * c + k - 1)
                mm(ys[k % 2][:], ident[:], hc[:, (NS * k + n) % 3], start=n == 0, stop=n == NS - 1).then_inc(red_done, 1)

            def scan(b, h, before, after):
                c = 2 * b + h
                d = c + 1
                for q in range(STEPS):
                    reduce_state(c, q // NS, q % NS)
                    if before and q < SPREAD_AT + NS - STEPS:
                        spread(c, q + STEPS - SPREAD_AT)
                    if before and q in OUT_AT:
                        out_proj(c - 1, 1 - h, OUT_AT.index(q))
                    if q in GATE_AT:
                        gate_proj(c, h, GATE_AT.index(q))
                    if not after:
                        continue
                    if q == NORM_AT:
                        norm_mean(d, 1 - h, b + h)
                    if q == NORM_AT + 5:
                        norm_var(d)
                    m = (q - CONV_AT) // CONV_GAP
                    if q == CONV_AT + CONV_GAP * m and 0 <= m < KT:
                        in_proj(d, 1 - h, m)
                    if q == XP_AT:
                        x_proj(d, 1 - h)
                    m = (q - DT_AT) // DT_GAP
                    if q == DT_AT + DT_GAP * m and 0 <= m < KT:
                        dt_proj(d, m)
                    if q >= SPREAD_AT:
                        spread(d, q - SPREAD_AT)

            pe.wait_ge(weights_in, 16 * 12)
            pe.wait_ge(consts, 1)
            norm_mean(0, 0, 0)
            norm_var(0)
            for m in range(KT):
                in_proj(0, 0, m)
            x_proj(0, 0)
            for m in range(KT):
                dt_proj(0, m)
            for n in range(NS):
                spread(0, n)
            pe.wait_ge(halved, 1)
            scan(0, 0, False, True)
            with pe.Fori(0, NCHUNK // 2 - 1) as i:
                scan(i, 1, True, True)
                scan(i + 1, 0, True, True)
            scan(B - 1, 1, True, False)
            for m in range(CT):
                out_proj(NCHUNK - 1, 1, m)

        @block.scalar
        def _(act):
            af = nc.scalar.activation

            def norm_square(d, h):
                act.wait_ge(centered, d + 1)
                if not isinstance(d, int) or d > 0:
                    act.wait_ge(dt_full, KT * d)
                af(sq[:], xn[:, h], ACT.Square).then_inc(squared, 1)

            def norm_rstd(d):
                nc.scalar.preload_act_table_set("natural_log_exp_and_others")
                act.wait_ge(var_full, d + 1)
                if not isinstance(d, int) or d > 0:
                    act.wait_ge(normed, d)
                af(rstd[:], pp[:], ACT.Ln, bias=eps_c[:, 0:1]).then_inc(ln_read, 1)
                act.wait_ge(ln_read, d + 1)
                af(rstd[:], rstd[:], ACT.Exp, scale=-0.5).then_inc(rstd_done, 1)

            def conv_in(d, h, m):
                act.wait_ge(in_full, KT * d + m + 1)
                if not isinstance(d, int) or KT * d + m >= 2:
                    act.wait_ge(u_done, KT * d + m - 1)
                if m == 0 and (not isinstance(d, int) or d > 0):
                    act.wait_ge(dt_done, KT * d)
                j = m % 2
                af(xin[:, j, 2:], pp[:], ACT.Copy)
                af(xin[:, j, 0:2], halo[:, m] if h else zeros2[:], ACT.Copy)
                if h == 0:
                    af(halo[:, m], pp[:, T - 2:], ACT.Copy)
                af(acc[:, j], pp[:], ACT.Identity, bias=cb[:, m:m + 1], scale=cw[:, m, 2:3]).then_inc(in_read, 1)

            def conv_tanh(d, m):
                act.wait_ge(conv_done, KT * d + m + 1)
                if not isinstance(d, int) or KT * d + m >= 2:
                    act.wait_ge(u_done, KT * d + m - 1)
                af(th[:, m % 2], acc[:, m % 2], ACT.Tanh).then_inc(th_done, 1)

            def dt_read_tile(d, m):
                act.wait_ge(dt_full, KT * d + m + 1)
                if not isinstance(d, int) or KT * d + m >= 2:
                    act.wait_ge(dt_done, KT * d + m - 1)
                af(sl[:, m % 2], pp[:], ACT.Abs, bias=dtb[:, m:m + 1])
                af(rl[:, m % 2], pp[:], ACT.Relu, bias=dtb[:, m:m + 1]).then_inc(dt_read, 1)

            def softplus(d, m):
                act.wait_ge(dt_read, KT * d + m + 1)
                af(sl[:, m % 2], sl[:, m % 2], ACT.Exp, scale=-1.0).then_inc(sp_exp, 1)
                act.wait_ge(sp_exp, KT * d + m + 1)
                af(sl[:, m % 2], sl[:, m % 2], ACT.Ln, bias=1.0).then_inc(sp_done, 1)

            def spread_copy(d, n):
                act.wait_ge(bb_full, NS * d + n + 1)
                if not isinstance(d, int) or d > 0:
                    act.wait_ge(dbu_done, STEPS * (d - 1) + NS * (KT - 1) + n + 1)
                af(b_rep[:, n], pp[:], ACT.Copy).then_inc(bb_copied, 1)
                act.wait_ge(cc_full, NS * d + n + 1)
                if not isinstance(d, int) or d > 0:
                    act.wait_ge(mult_done, STEPS * (d - 1) + NS * (KT - 1) + n + 1)
                af(c_rep[:, n], pz[:], ACT.Copy).then_inc(cc_copied, 1)

            def gate_tanh(c, k):
                act.wait_ge(z_full, KT * c + k + 1)
                if not isinstance(c, int) or KT * c + k >= 2:
                    act.wait_ge(gated, KT * c + k - 1)
                af(gate[:, k % 2], pz[:], ACT.Tanh, scale=0.5).then_inc(z_tanh, 1)

            def decay(c, k, n):
                s = STEPS * c + NS * k + n
                if n == 0:
                    act.wait_ge(dt_done, KT * c + k + 1)
                if not isinstance(c, int) or s >= 2:
                    act.wait_ge(scan_done, s - 1)
                af(da[(NS * k + n) % 2][:], dt[:, k], ACT.Exp, scale=aneg[:, k, n:n + 1]).then_inc(exp_done, 1)

            def scan(b, h, before, after):
                c = 2 * b + h
                d = c + 1
                for q in range(STEPS):
                    decay(c, q // NS, q % NS)
                    if before and q < SPREAD_AT + 2 + NS - STEPS:
                        spread_copy(c, q + STEPS - SPREAD_AT - 2)
                    if q - 3 in GATE_AT:
                        gate_tanh(c, GATE_AT.index(q - 3))
                    if not after:
                        continue
                    if q == NORM_AT + 5:
                        norm_square(d, 1 - h)
                    if q == NORM_AT + 9:
                        norm_rstd(d)
                    m = (q - CONV_AT - 3) // CONV_GAP
                    if q == CONV_AT + 3 + CONV_GAP * m and 0 <= m < KT:
                        conv_in(d, 1 - h, m)
                    m = (q - CONV_AT - 7) // CONV_GAP
                    if q == CONV_AT + 7 + CONV_GAP * m and 0 <= m < KT:
                        conv_tanh(d, m)
                    m = (q - DT_AT - 3) // DT_GAP
                    if q == DT_AT + 3:
                        nc.scalar.preload_act_table_set("natural_log_exp_and_others")
                    if q == DT_AT + 3 + DT_GAP * m and 0 <= m < KT:
                        dt_read_tile(d, m)
                        softplus(d, m)
                    if q >= SPREAD_AT + 2:
                        spread_copy(d, q - SPREAD_AT - 2)

            act.wait_ge(weights_in, 16 * 12)
            act.wait_ge(consts, 1)
            af(aneg[:], aneg[:], ACT.Exp).then_inc(a_exp, 1)
            act.wait_ge(halved, 1)
            norm_square(0, 0)
            norm_rstd(0)
            for m in range(KT):
                conv_in(0, 0, m)
                conv_tanh(0, m)
            nc.scalar.preload_act_table_set("natural_log_exp_and_others")
            for m in range(KT):
                dt_read_tile(0, m)
                softplus(0, m)
            for n in range(NS):
                spread_copy(0, n)
            scan(0, 0, False, True)
            with act.Fori(0, NCHUNK // 2 - 1) as i:
                scan(i, 1, True, True)
                scan(i + 1, 0, True, True)
            scan(B - 1, 1, True, False)

        @block.gpsimd
        def _(pool):
            tt = nc.gpsimd.tensor_tensor
            nc.gpsimd.memset(ident[:], 0.0)
            nc.gpsimd.memset(sel3[:], 0.0).then_inc(const_step, 1)
            nc.gpsimd.memset(zeros2[:], 0.0)
            nc.gpsimd.memset(eps_c[:], 1e-6)
            nc.gpsimd.memset(mean_w[:], 1.0 / DM)
            pool.wait_ge(const_step, 1)
            nc.gpsimd.affine_select(out=ident[:], in_=ident[:], compare_op=ALU.not_equal, fill=1.0, base=0,
                                    pattern=[[-1, P]], channel_multiplier=1)
            for r in range(3):
                nc.gpsimd.affine_select(out=sel3[:], in_=sel3[:], compare_op=ALU.not_equal, fill=1.0,
                                               base=-BC * r, pattern=[[-1, BC]], channel_multiplier=1).then_inc(const_step, 1)
                pool.wait_ge(const_step, r + 2)
            nc.gpsimd.sem_inc(consts, 1)

            def dt_add(d, m):
                pool.wait_ge(sp_done, KT * d + m + 1)
                if not isinstance(d, int) or d > 0:
                    pool.wait_ge(exp_done, STEPS * (d - 1) + NS * (m + 1))
                tt(dt[:, m], rl[:, m % 2], sl[:, m % 2], ALU.add).then_inc(dt_done, 1)

            def dt_u(c, h, k):
                pool.wait_ge(dt_done, KT * c + k + 1)
                pool.wait_ge(u_done, KT * (c + 1))
                tt(dtu[:, k % 2], dt[:, k], u[:, h, k], ALU.mult).then_inc(dtu_done, 1)
                pool.wait_ge(dtu_done, KT * c + k + 1)

            def drive(c, k, n):
                s = STEPS * c + NS * k + n
                if k == 0:
                    pool.wait_ge(bb_copied, NS * c + n + 1)
                if not isinstance(c, int) or s >= 3:
                    pool.wait_ge(scan_done, s - 2)
                tt(dbu[:, (NS * k + n) % 3], dtu[:, k % 2], b_rep[:, n], ALU.mult).then_inc(dbu_done, 1)

            def gate_y(c, h, k):
                pool.wait_ge(y_read, KT * c + k + 1)
                tt(u[:, h, k], yy[:], gate[:, k % 2], ALU.mult).then_inc(gated, 1)

            def scan(b, h, before, after):
                c = 2 * b + h
                for k in range(KT):
                    dt_u(c, h, k)
                    for n in range(NS):
                        q = NS * k + n
                        drive(c, k, n)
                        if k > 0 and n == 4:
                            gate_y(c, h, k - 1)
                        m = (q - DT_AT - 4) // DT_GAP
                        if after and q == DT_AT + 4 + DT_GAP * m and 0 <= m < KT - 1:
                            dt_add(c + 1, m)
                gate_y(c, h, KT - 1)
                if after:
                    dt_add(c + 1, KT - 1)

            for m in range(KT):
                dt_add(0, m)
            scan(0, 0, False, True)
            with pool.Fori(0, NCHUNK // 2 - 1) as i:
                scan(i, 1, True, True)
                scan(i + 1, 0, True, True)
            scan(B - 1, 1, True, False)

        @block.vector
        def _(dve):
            v = nc.vector
            v.memset(yy[:], 0.0)

            def norm_center(d, h, image):
                dve.wait_ge(mean_full, d + 1)
                if not isinstance(d, int) or d >= 2:
                    dve.wait_ge(z_full, KT * (d - 1))
                dve.wait_ge(x_loaded[h], 16 * (image + 1))
                v.tensor_tensor(xn[:, h], xs[:, h], pp[:].unsqueeze(1).broadcast_to([P, CT, T]), ALU.subtract).then_inc(centered, 1)

            def norm_scale(d, h):
                dve.wait_ge(rstd_done, d + 1)
                v.tensor_tensor(xn[:, h], xn[:, h], rstd[:].unsqueeze(1).broadcast_to([P, CT, T]), ALU.mult).then_inc(normed, 1)

            def conv(d, m):
                j = m % 2
                dve.wait_ge(in_read, KT * d + m + 1)
                v.scalar_tensor_tensor(acc[:, j], xin[:, j, 1:T + 1], cw[:, m, 1:2], acc[:, j], ALU.mult, ALU.add).then_inc(conv_part, 1)
                dve.wait_ge(conv_part, KT * d + m + 1)
                v.scalar_tensor_tensor(acc[:, j], xin[:, j, 0:T], cw[:, m, 0:1], acc[:, j], ALU.mult, ALU.add).then_inc(conv_done, 1)

            def conv_silu(d, h, m):
                dve.wait_ge(th_done, KT * d + m + 1)
                if m == 0 and (not isinstance(d, int) or d >= 2):
                    dve.wait_ge(out_full, CT * (d - 1))
                v.scalar_tensor_tensor(u[:, h, m], th[:, m % 2], 1.0, acc[:, m % 2], ALU.add, ALU.mult).then_inc(u_done, 1)

            def split(d):
                dve.wait_ge(xp_full, d + 1)
                if not isinstance(d, int) or d > 0:
                    dve.wait_ge(cc_full, NS * d)
                v.tensor_copy(bc3[0:DT0, :], pp[0:DT0, :]).then_inc(split_step, 1)
                v.tensor_copy(dtr[DT0:DT0 + DTR, :], pp[DT0:DT0 + DTR, :])
                dve.wait_ge(split_step, 3 * d + 1)
                v.tensor_tensor(bcr[0:DT0, :], pp[0:DT0, :], bc3[0:DT0, :], ALU.subtract).then_inc(split_step, 1)
                dve.wait_ge(split_step, 3 * d + 2)
                v.tensor_copy(bcm[0:DT0, :], bcr[0:DT0, :]).then_inc(split_step, 1)
                dve.wait_ge(split_step, 3 * d + 3)
                v.tensor_copy(bc3[BC:2 * BC, :], bcm[BC:2 * BC, :])
                v.tensor_tensor(bc3[2 * BC:DT0, :], bcr[2 * BC:DT0, :], bcm[2 * BC:DT0, :], ALU.subtract).then_inc(bc_done, 1)

            def recur(b, h, k, n):
                c = 2 * b + h
                q = NS * k + n
                s = STEPS * c + q
                dve.wait_ge(exp_done, s + 1)
                dve.wait_ge(dbu_done, s + 1)
                if h == 1 and q == 0:
                    dve.wait_ge(carried, b + 1)
                if not isinstance(c, int) or s >= 3:
                    dve.wait_ge(mult_done, s - 2)
                v.tensor_tensor_scan(hs[q % 3][:], da[q % 2][:], dbu[:, q % 3],
                                     carry[:, q:q + 1] if h else 0.0, ALU.mult, ALU.add).then_inc(scan_done, 1)

            def times_c(c, h, k, n):
                q = NS * k + n
                s = STEPS * c + q
                dve.wait_ge(scan_done, s + 1)
                if not isinstance(c, int) or s >= 3:
                    dve.wait_ge(red_done, s - 2)
                if k == 0:
                    dve.wait_ge(cc_copied, NS * c + n + 1)
                if h == 0:
                    kept = v.tensor_copy(carry[:, q:q + 1], hs[q % 3][:, T - 1:T])
                    if q == STEPS - 1:
                        kept.then_inc(carried, 1)
                v.tensor_tensor(hc[:, q % 3], hs[q % 3][:], c_rep[:, n], ALU.mult).then_inc(mult_done, 1)

            def gate_z(c, k):
                dve.wait_ge(z_tanh, KT * c + k + 1)
                v.scalar_tensor_tensor(gate[:, k % 2], gate[:, k % 2], 1.0, pz[:], ALU.add, ALU.mult).then_inc(z_read, 1)

            def read_y(c, h, k):
                dve.wait_ge(red_done, STEPS * c + NS * (k + 1))
                if not isinstance(c, int) or KT * c + k > 0:
                    dve.wait_ge(gated, KT * c + k)
                v.scalar_tensor_tensor(yy[:], u[:, h, k], dskip[:, k:k + 1], ys[k % 2][:], ALU.mult, ALU.add).then_inc(y_read, 1)

            def residual(c, h, m):
                dve.wait_ge(out_full, CT * c + m + 1)
                v.tensor_tensor(xs[:, h, m], xs[:, h, m], pz[:], ALU.add).then_inc(res_done, 1)

            def scan(b, h, before, after):
                c = 2 * b + h
                d = c + 1
                recur(b, h, 0, 0)
                for q in range(STEPS):
                    if q + 1 < STEPS:
                        recur(b, h, (q + 1) // NS, (q + 1) % NS)
                    times_c(c, h, q // NS, q % NS)
                    if before and q - 2 in OUT_AT:
                        residual(c - 1, 1 - h, OUT_AT.index(q - 2))
                    if q - 4 in GATE_AT:
                        gate_z(c, GATE_AT.index(q - 4))
                    if q >= NS and q % NS == 1:
                        read_y(c, h, q // NS - 1)
                    if not after:
                        continue
                    if q == NORM_AT + 2:
                        norm_center(d, 1 - h, b + h)
                    if q == NORM_AT + 10:
                        norm_scale(d, 1 - h)
                    m = (q - CONV_AT - 4) // CONV_GAP
                    if q == CONV_AT + 4 + CONV_GAP * m and 0 <= m < KT:
                        conv(d, m)
                    m = (q - CONV_AT - 8) // CONV_GAP
                    if q == CONV_AT + 8 + CONV_GAP * m and 0 <= m < KT:
                        conv_silu(d, 1 - h, m)
                    if q == XP_AT + 2:
                        split(d)
                read_y(c, h, KT - 1)

            dve.wait_ge(weights_in, 16 * 12)
            dve.wait_ge(a_exp, 1)
            v.tensor_scalar(aneg[:], aneg[:], -1.0, None, ALU.mult)
            v.tensor_scalar(cw[:], cw[:], 0.5, None, ALU.mult)
            v.tensor_scalar(cb[:], cb[:], 0.5, None, ALU.mult)
            v.tensor_scalar(w_out[:], w_out[:], 0.5, None, ALU.mult).then_inc(halved, 1)
            dve.wait_ge(halved, 1)
            norm_center(0, 0, 0)
            norm_scale(0, 0)
            for m in range(KT):
                conv(0, m)
                conv_silu(0, 0, m)
            split(0)
            scan(0, 0, False, True)
            with dve.Fori(0, NCHUNK // 2 - 1) as i:
                scan(i, 1, True, True)
                scan(i + 1, 0, True, True)
            scan(B - 1, 1, True, False)
            for m in range(CT):
                residual(NCHUNK - 1, 1, m)


GROUPS = 5
FFN_B = GROUPS * (B // GROUPS)
HID = 4 * DM
MT = HID // P
Q_EPS, Q_BOUND = 1e-5, 128.0
Q_CLIP = Q_BOUND - Q_EPS
HALVES = HW // T
LAG = 5


def ffn(nc, layer, signals, x_in, x_out, W1T, b1, W2T, b2):
    assert B // GROUPS == 1
    with ExitStack() as ctx:
        def sb(name, shape, dt=F32):
            return ctx.enter_context(nc.sbuf_tensor(f"{name}_f{layer}", shape, dt))

        def sem(name):
            if name not in signals:
                signals[name] = nc.alloc_semaphore(f"{name}_f")
            return signals[name]

        def bank(name):
            return ctx.enter_context(nc.psum_tensor(f"{name}_f{layer}", [P, T], F32))

        w1 = sb("w1", [P, CT, HID], F32R)
        w2 = sb("w2", [P, MT, DM], F32R)
        hid = sb("hid", [P, MT, HW])
        raw1 = hid[:, 0:MT // 2, :].rearrange("p m n -> p (m n)")[:, 0:CT * HID].rearrange("p (t n) -> p t n", t=CT)
        raw2 = hid[:, MT // 2:, :].rearrange("p m n -> p (m n)")[:, 0:MT * DM].rearrange("p (t n) -> p t n", t=MT)
        bias1 = sb("bias1", [P, MT])
        bias2 = sb("bias2", [P, CT])
        wsum = sb("wsum", [P, 2, GROUPS])
        wmean = sb("wmean", [P, 2, GROUPS])
        ones = sb("ones", [P, P])
        mean_w = sb("mean_w", [P, P])
        ident = sb("ident", [P, P])
        eps_t = sb("eps_t", [P, 1])
        xn = sb("xn", [P, CT, HW])
        xh = sb("xh", [P, CT, HW], F32R)
        xl = sb("xl", [P, CT, HW], F32R)
        sq = sb("sq", [P, CT, T])
        rstd = sb("rstd", [P, HW])
        xres = sb("xres", [P, CT, HW])
        y2 = sb("y2", [P, CT, HW])
        g = sb("g", [P, 2, HW])
        gh = sb("gh", [P, 3, HW], F32R)
        gl = sb("gl", [P, 3, HW], F32R)
        big = sb("big", [P, 2, MT])
        top = sb("top", [P, 2])
        top1 = sb("top1", [P, 2])
        gain = [sb(f"gain{j}", [P, 1]) for j in range(2)]
        acc = [bank(f"acc{j}") for j in range(CT * HALVES)]
        ph = [bank(f"ph{j}") for j in range(HALVES)]

        weights_in, consts, const_step = sem("weights_in"), sem("consts"), sem("const_step")
        summed, sums_full, means_done, signed = sem("summed"), sem("sums_full"), sem("means_done"), sem("signed")
        x_loaded, xres_loaded, stored = sem("x_loaded"), sem("xres_loaded"), sem("stored")
        mean_full, centered, squared, var_full = sem("mean_full"), sem("centered"), sem("squared"), sem("var_full")
        ln_read, rstd_done, normed, split_hi, split_lo = sem("ln_read"), sem("rstd_done"), sem("normed"), sem("split_hi"), sem("split_lo")
        up_full, up_read, up_max = sem("up_full"), sem("up_read"), sem("up_max")
        gelu_done, g_hi, g_lo, down_full = sem("gelu_done"), sem("g_hi"), sem("g_lo"), sem("down_full")
        down_read, down_max, quant, added = sem("down_read"), sem("down_max"), sem("quant"), sem("added")
        top_col, top_row, top_one, top_all, top_eps, top_inv, gain_done = (
            [sem(f"{n}{j}") for j in range(2)] for n in
            ("top_col", "top_row", "top_one", "top_all", "top_eps", "top_inv", "gain_done"))
        block = ctx.enter_context(nc.Block())
        XIN = x_in.rearrange("b (t p) s -> b p t s", p=P)
        XOUT = x_out.rearrange("b (t p) s -> b p t s", p=P)

        @block.sync
        def _(sp):
            sp.dma_start(raw1, W1T.rearrange("(t p) n -> p t n", p=P)).then_inc(weights_in, 16)
            sp.dma_start(raw2, W2T.rearrange("(t p) n -> p t n", p=P)).then_inc(weights_in, 16)
            sp.dma_start(bias1[:], b1.rearrange("(t p) -> p t", p=P), allow_slow_non_contiguous=True).then_inc(weights_in, 16)
            sp.dma_start(bias2[:], b2.rearrange("(t p) -> p t", p=P), allow_slow_non_contiguous=True).then_inc(weights_in, 16)
            sp.dma_start(xn[:], XIN[0]).then_inc(x_loaded, 16)

            def image(i, more):
                if not isinstance(i, int) or i > 0:
                    sp.wait_ge(added, i)
                sp.dma_start(xres[:], XIN[i]).then_inc(xres_loaded, 16)
                if more:
                    sp.wait_ge(split_lo, HALVES * (i + 1))
                    sp.dma_start(xn[:], XIN[i + 1]).then_inc(x_loaded, 16)
                sp.wait_ge(added, i + 1)
                sp.dma_start(XOUT[i], y2[:]).then_inc(stored, 16)

            image(0, True)
            with sp.Fori(1, FFN_B - 1) as i:
                image(i, True)
            image(FFN_B - 1, False)
            sp.wait_ge(stored, 16 * FFN_B)

        @block.tensor
        def _(pe):
            mm = nc.tensor.matmul

            def norm_mean(i):
                pe.wait_ge(x_loaded, 16 * (i + 1))
                for h in range(HALVES):
                    if not isinstance(i, int) or i > 0:
                        pe.wait_ge(gain_done[0], i)
                    for t in range(CT):
                        last = mm(ph[h][:], mean_w[:], xn[:, t, h * T:(h + 1) * T], start=t == 0, stop=t == CT - 1)
                    last.then_inc(mean_full, 1)

            def norm_var(i, h):
                pe.wait_ge(squared, HALVES * i + h + 1)
                for t in range(CT):
                    last = mm(ph[h][:], mean_w[:], sq[:, t], start=t == 0, stop=t == CT - 1)
                last.then_inc(var_full, 1)

            def up(i, m):
                for h in range(HALVES):
                    if m == 0:
                        pe.wait_ge(split_lo, HALVES * i + h + 1)
                        pe.wait_ge(split_hi, HALVES * i + h + 1)
                    else:
                        pe.wait_ge(up_read, HALVES * (MT * i + m - 1) + h + 1)
                    for part, x in enumerate((xh, xl)):
                        for t in range(CT):
                            last = mm(ph[h][:], w1[:, t, m * P:(m + 1) * P], x[:, t, h * T:(h + 1) * T],
                                      start=part == 0 and t == 0, stop=part == 1 and t == CT - 1)
                    last.then_inc(up_full, 1)

            def down(i, k):
                for part, (x, ready) in enumerate(((gh, g_hi), (gl, g_lo))):
                    pe.wait_ge(ready, MT * i + k + 1)
                    for m in range(CT):
                        for h in range(HALVES):
                            if k == 0 and part == 0 and (not isinstance(i, int) or i > 0):
                                pe.wait_ge(down_read, CT * HALVES * i)
                                pe.wait_ge(gain_done[1], i)
                            last = mm(acc[HALVES * m + h][:], w2[:, k, m * P:(m + 1) * P],
                                      x[:, k % 3, h * T:(h + 1) * T], start=k == 0 and part == 0,
                                      stop=k == MT - 1 and part == 1)
                last.then_inc(down_full, 1)

            def spread_top(i, j, row, col):
                pe.wait_ge(top_col[j], i + 1)
                if j == 1:
                    pe.wait_ge(down_read, CT * HALVES * (i + 1))
                mm(row[0:1, 0:P], top[:, j:j + 1], ident[:], start=True, stop=True).then_inc(top_row[j], 1)
                pe.wait_ge(top_one[j], i + 1)
                mm(col[:, 0:1], ones[0:1, :], top1[0:1, j:j + 1], start=True, stop=True).then_inc(top_all[j], 1)

            def image(i, more):
                spread_top(i, 0, ph[0], ph[1])
                if more:
                    norm_mean(i + 1)
                for k in range(MT):
                    down(i, k)
                    if more and k in (0, 1):
                        norm_var(i + 1, k)
                    if more and k >= LAG:
                        up(i + 1, k - LAG)
                if more:
                    for m in range(MT - LAG, MT):
                        up(i + 1, m)
                spread_top(i, 1, acc[0], acc[1])

            pe.wait_ge(consts, 1)
            pe.wait_ge(summed, 2 * GROUPS)
            mm(ph[0][:, 0:2 * GROUPS], ones[:], wsum[:].rearrange("p a g -> p (a g)"), start=True, stop=True).then_inc(sums_full, 1)
            pe.wait_ge(means_done, 1)
            norm_mean(0)
            for h in range(HALVES):
                norm_var(0, h)
            pe.wait_ge(signed, 1)
            for m in range(MT):
                up(0, m)
            image(0, True)
            with pe.Fori(1, FFN_B - 1) as i:
                image(i, True)
            image(FFN_B - 1, False)

        @block.scalar
        def _(act):
            af = nc.scalar.activation

            def norm_square(i, h):
                act.wait_ge(centered, HALVES * i + h + 1)
                if h > 0 or not isinstance(i, int) or i > 0:
                    act.wait_ge(var_full, HALVES * i + h)
                af(sq[:], xn[:, :, h * T:(h + 1) * T], ACT.Square).then_inc(squared, 1)

            def norm_rstd(i):
                nc.scalar.preload_act_table_set("natural_log_exp_and_others")
                for h in range(HALVES):
                    act.wait_ge(var_full, HALVES * i + h + 1)
                    if not isinstance(i, int) or i > 0:
                        act.wait_ge(normed, HALVES * i)
                    af(rstd[:, h * T:(h + 1) * T], ph[h][:], ACT.Ln, bias=eps_t[:, 0:1]).then_inc(ln_read, 1)
                for h in range(HALVES):
                    act.wait_ge(ln_read, HALVES * i + h + 1)
                    r = rstd[:, h * T:(h + 1) * T]
                    af(r, r, ACT.Exp, scale=-0.5).then_inc(rstd_done, 1)

            def up_bias(i, m):
                for h in range(HALVES):
                    act.wait_ge(up_full, HALVES * (MT * i + m) + h + 1)
                    if h == 0 and (not isinstance(i, int) or i > 0):
                        act.wait_ge(gelu_done, MT * (i - 1) + m + 1)
                        act.wait_ge(up_max, MT * (i - 1) + m + 1)
                    af(hid[:, m, h * T:(h + 1) * T], ph[h][:], ACT.Identity, bias=bias1[:, m:m + 1]).then_inc(up_read, 1)

            def gelu(i, k):
                if k == 0:
                    act.wait_ge(gain_done[0], i + 1)
                if k >= 2 or not isinstance(i, int) or i > 0:
                    act.wait_ge(g_lo, MT * i + k - 1)
                af(g[:, k % 2], hid[:, k], ACT.Gelu, scale=gain[0][:]).then_inc(gelu_done, 1)

            def down_bias(i):
                act.wait_ge(down_full, MT * (i + 1))
                if not isinstance(i, int) or i > 0:
                    act.wait_ge(stored, 16 * i)
                for m in range(CT):
                    for h in range(HALVES):
                        af(y2[:, m, h * T:(h + 1) * T], acc[HALVES * m + h][:], ACT.Identity,
                           bias=bias2[:, m:m + 1]).then_inc(down_read, 1)

            def image(i, more):
                for k in range(MT):
                    gelu(i, k)
                    if more and k in (1, 2):
                        norm_square(i + 1, k - 1)
                    if more and k == 3:
                        norm_rstd(i + 1)
                    if more and k >= LAG + 1:
                        up_bias(i + 1, k - LAG - 1)
                if more:
                    up_bias(i + 1, MT - LAG - 1)
                down_bias(i)
                if more:
                    for m in range(MT - LAG, MT):
                        up_bias(i + 1, m)

            act.wait_ge(means_done, 1)
            for j, (w, raw, n) in enumerate(((w1, raw1, HID), (w2, raw2, DM))):
                size = n // GROUPS
                for q in range(GROUPS):
                    last = af(w[:, :, q * size:(q + 1) * size], raw[:, :, q * size:(q + 1) * size], ACT.Sign,
                              bias=wmean[:, j, q:q + 1])
            last.then_inc(signed, 1)
            norm_square(0, 0)
            norm_square(0, 1)
            norm_rstd(0)
            act.wait_ge(signed, 1)
            for m in range(MT):
                up_bias(0, m)
            image(0, True)
            with act.Fori(1, FFN_B - 1) as i:
                image(i, True)
            image(FFN_B - 1, False)

        @block.vector
        def _(dve):
            v = nc.vector

            def norm_center(i, h):
                dve.wait_ge(mean_full, HALVES * i + h + 1)
                dve.wait_ge(x_loaded, 16 * (i + 1))
                x = xn[:, :, h * T:(h + 1) * T]
                v.tensor_tensor(x, x, ph[h][:].unsqueeze(1).broadcast_to([P, CT, T]), ALU.subtract).then_inc(centered, 1)

            def norm_scale(i, h):
                dve.wait_ge(rstd_done, HALVES * i + h + 1)
                s = slice(h * T, (h + 1) * T)
                v.tensor_tensor(xn[:, :, s], xn[:, :, s], rstd[:, s].unsqueeze(1).broadcast_to([P, CT, T]),
                                ALU.mult).then_inc(normed, 1)
                dve.wait_ge(normed, HALVES * i + h + 1)
                if not isinstance(i, int) or i > 0:
                    dve.wait_ge(up_full, HALVES * MT * i)
                v.tensor_copy(xh[:, :, s], xn[:, :, s]).then_inc(split_hi, 1)
                dve.wait_ge(split_hi, HALVES * i + h + 1)
                v.tensor_tensor(xl[:, :, s], xn[:, :, s], xh[:, :, s], ALU.subtract).then_inc(split_lo, 1)

            def up_largest(i, m):
                dve.wait_ge(up_read, HALVES * (MT * i + m + 1))
                v.tensor_reduce(big[:, 0, m:m + 1], hid[:, m], AX.X, ALU.max, apply_absolute_value=True).then_inc(up_max, 1)

            def gelu_split(i, k):
                dve.wait_ge(gelu_done, MT * i + k + 1)
                if k >= 3 or not isinstance(i, int) or i > 0:
                    dve.wait_ge(down_full, MT * i + k - 2)
                v.tensor_scalar(gh[:, k % 3], g[:, k % 2], Q_CLIP, -Q_CLIP, ALU.min, ALU.max).then_inc(g_hi, 1)
                dve.wait_ge(g_hi, MT * i + k + 1)
                v.scalar_tensor_tensor(gl[:, k % 3], g[:, k % 2], Q_CLIP, gh[:, k % 3], ALU.min, ALU.subtract).then_inc(g_lo, 1)

            def make_gain(i, j, row, col, n, done, total):
                dve.wait_ge(done, total)
                v.tensor_reduce(top[:, j:j + 1], big[:, j, 0:n], AX.X, ALU.max).then_inc(top_col[j], 1)
                dve.wait_ge(top_row[j], i + 1)
                v.tensor_reduce(top1[0:1, j:j + 1], row[0:1, 0:P], AX.X, ALU.max).then_inc(top_one[j], 1)
                dve.wait_ge(top_all[j], i + 1)
                v.tensor_scalar(gain[j][:], col[:, 0:1], Q_EPS, 1.0 / Q_BOUND, ALU.add, ALU.mult).then_inc(top_eps[j], 1)
                dve.wait_ge(top_eps[j], i + 1)
                v.reciprocal(gain[j][:], gain[j][:]).then_inc(gain_done[j], 1)

            def finish(i):
                dve.wait_ge(down_read, CT * HALVES * (i + 1))
                v.tensor_reduce(big[:, 1, 0:CT], y2[:], AX.X, ALU.max, apply_absolute_value=True).then_inc(down_max, 1)
                make_gain(i, 1, acc[0], acc[1], CT, down_max, i + 1)
                dve.wait_ge(gain_done[1], i + 1)
                v.tensor_scalar(y2[:], y2[:], gain[1][:], Q_CLIP, ALU.mult, ALU.min).then_inc(quant, 1)
                dve.wait_ge(quant, i + 1)
                dve.wait_ge(xres_loaded, 16 * (i + 1))
                v.scalar_tensor_tensor(y2[:].rearrange("p t s -> p (t s)"), y2[:].rearrange("p t s -> p (t s)"), -Q_CLIP,
                                       xres[:].rearrange("p t s -> p (t s)"), ALU.max, ALU.add).then_inc(added, 1)

            def image(i, more):
                make_gain(i, 0, ph[0], ph[1], MT, up_max, MT * (i + 1))
                for k in range(MT):
                    gelu_split(i, k)
                    if more and k == 0:
                        norm_center(i + 1, 0)
                        norm_center(i + 1, 1)
                    if more and k == 3:
                        norm_scale(i + 1, 0)
                        norm_scale(i + 1, 1)
                    if more and k >= LAG + 2:
                        up_largest(i + 1, k - LAG - 2)
                if more:
                    for m in range(MT - LAG - 2, MT):
                        up_largest(i + 1, m)
                finish(i)

            dve.wait_ge(weights_in, 16 * 4)
            for j, (raw, n) in enumerate(((raw1, HID), (raw2, DM))):
                size = n // GROUPS
                for q in range(GROUPS):
                    v.tensor_reduce(wsum[:, j, q:q + 1], raw[:, :, q * size:(q + 1) * size], AX.XY, ALU.add).then_inc(summed, 1)
            v.memset(w1[:, :, GROUPS * (HID // GROUPS):].bitcast(F32), 0.0)
            v.memset(w2[:, :, GROUPS * (DM // GROUPS):].bitcast(F32), 0.0)
            dve.wait_ge(sums_full, 1)
            v.tensor_scalar(wmean[:, 0], ph[0][:, 0:GROUPS], -1.0 / (HID // GROUPS * DM), None, ALU.mult)
            v.tensor_scalar(wmean[:, 1], ph[0][:, GROUPS:2 * GROUPS], -1.0 / (DM // GROUPS * HID), None, ALU.mult).then_inc(means_done, 1)
            norm_center(0, 0)
            norm_center(0, 1)
            norm_scale(0, 0)
            norm_scale(0, 1)
            for m in range(MT):
                up_largest(0, m)
            image(0, True)
            with dve.Fori(1, FFN_B - 1) as i:
                image(i, True)
            image(FFN_B - 1, False)

        @block.gpsimd
        def _(pool):
            nc.gpsimd.memset(ident[:], 0.0).then_inc(const_step, 1)
            nc.gpsimd.memset(ones[:], 1.0)
            nc.gpsimd.memset(mean_w[:], 1.0 / DM)
            nc.gpsimd.memset(eps_t[:], 1e-5)
            pool.wait_ge(const_step, 1)
            nc.gpsimd.affine_select(out=ident[:], in_=ident[:], compare_op=ALU.not_equal, fill=1.0, base=0,
                                    pattern=[[-1, P]], channel_multiplier=1).then_inc(consts, 1)


NPOS = 48
CPP = DM // NPOS
SIDE = 32
SIDES = P // SIDE
PPG = SIDE // CPP
MAGIC = 1.5 * 2.0 ** 23
NMAT = 2 * CT * PPG


def displace(nc, signals, x_in, x_mid, x_out, offset):
    with ExitStack() as ctx:
        def sb(name, shape, dt=F32):
            return ctx.enter_context(nc.sbuf_tensor(name + "_d", shape, dt))

        def sem(name):
            return ctx.enter_context(nc.semaphore(name + "_d"))

        def bank(name):
            return ctx.enter_context(nc.psum_tensor(name + "_d", [P, T], F32))

        lag_i = sb("lag_i", [P, P], mybir.dt.int32)
        lag = sb("lag", [P, P])
        diag = sb("diag", [P, P])
        off = sb("off", [P, NMAT])
        whole = sb("whole", [P, NMAT])
        part = sb("part", [P, NMAT])
        scale = sb("scale", [P, NMAT])
        tmp = sb("tmp", [P, 4, NMAT])
        tap = sb("tap", [P, 5, NMAT])
        mats = sb("mats", [P, NMAT, P])
        work = sb("work", [P, NMAT, P])
        mean_w = sb("mean_w", [P, P])
        eps_c = sb("eps_c", [P, 1])
        xn = sb("xn", [P, CT, HW])
        sq = sb("sq", [P, CT, T])
        rstd = sb("rstd", [P, HW])
        xres = sb("xres", [P, CT, HW])
        res = sb("res", [P, CT, HW])
        ta = sb("ta", [P, CT, HW])
        tb = sb("tb", [P, CT, HW])
        tc = sb("tc", [P, CT, HW])
        td = sb("td", [P, CT, HW])
        te = sb("te", [P, CT, HW])
        pc = [bank(f"pc{j}") for j in range(2 * CT)]
        ph = [bank(f"ph{j}") for j in range(HALVES)]

        off_in, iotas, made, lag_done = sem("off_in"), sem("iotas"), sem("made"), sem("lag_done")
        step, tapped, gauss, mats_done = sem("step"), sem("tapped"), sem("gauss"), sem("mats_done")
        x_loaded, xres_loaded = sem("x_loaded"), sem("xres_loaded")
        stored = sem("stored")
        mean_full, centered, squared, var_full = sem("mean_full"), sem("centered"), sem("squared"), sem("var_full")
        ln_read, rstd_done, normed, ta_done = sem("ln_read"), sem("rstd_done"), sem("normed"), sem("ta_done")
        x_full, x_read, tc_done = sem("x_full"), sem("x_read"), sem("tc_done")
        y_full, y_read, te_done, added = sem("y_full"), sem("y_read"), sem("te_done"), sem("added")
        block = ctx.enter_context(nc.Block())
        XIN = x_in.rearrange("b (t p) s -> b p t s", p=P)
        MID = x_mid.rearrange("b (t p) s -> b p t s", p=P)
        OUT = x_out.rearrange("b (t p) s -> b p t s", p=P)

        @block.sync
        def _(sp):
            for g in range(SIDES):
                for a in range(2):
                    for t in range(CT):
                        src = offset[(t * SIDES + g) * PPG:(t * SIDES + g + 1) * PPG, a]
                        j = (a * CT + t) * PPG
                        sp.dma_start(off[g * SIDE:(g + 1) * SIDE, j:j + PPG], src.partition_broadcast(SIDE),
                                     allow_slow_non_contiguous=True).then_inc(off_in, 16)
            sp.dma_start(xn[:], XIN[0]).then_inc(x_loaded, 16)

            def image(i, out, more):
                if not isinstance(i, int) or i > 0:
                    sp.wait_ge(added, i)
                sp.dma_start(xres[:], XIN[i]).then_inc(xres_loaded, 16)
                if more:
                    sp.wait_ge(ta_done, CT * (i + 1))
                    sp.dma_start(xn[:], XIN[i + 1]).then_inc(x_loaded, 16)
                sp.wait_ge(added, i + 1)
                sp.dma_start(out[i], res[:]).then_inc(stored, 16)

            image(0, MID, True)
            with sp.Fori(1, FFN_B) as i:
                image(i, MID, True)
            with sp.Fori(FFN_B, B - 1) as i:
                image(i, OUT, True)
            image(B - 1, OUT, False)
            sp.wait_ge(stored, 16 * B)

        @block.tensor
        def _(pe):
            mm = nc.tensor.matmul

            def norm_mean(i):
                pe.wait_ge(x_loaded, 16 * (i + 1))
                if not isinstance(i, int) or i > 0:
                    pe.wait_ge(ln_read, HALVES * i)
                for h in range(HALVES):
                    for t in range(CT):
                        last = mm(ph[h][:], mean_w[:], xn[:, t, h * T:(h + 1) * T], start=t == 0, stop=t == CT - 1)
                    last.then_inc(mean_full, 1)

            def norm_var(i):
                for h in range(HALVES):
                    pe.wait_ge(squared, HALVES * i + h + 1)
                    for t in range(CT):
                        last = mm(ph[h][:], mean_w[:], sq[:, t], start=t == 0, stop=t == CT - 1)
                    last.then_inc(var_full, 1)

            def axis(i, a, src, ready, full):
                for t in range(CT):
                    pe.wait_ge(ready, CT * i + t + 1)
                    if a == 1:
                        pe.wait_ge(x_read, 2 * CT * i + 2 * t + 2)
                    elif not isinstance(i, int) or i > 0:
                        pe.wait_ge(y_read, 2 * CT * (i - 1) + 2 * t + 2)
                    for q in range(PPG):
                        if a == 0:
                            x = src[:, t].rearrange("p (y c) -> p y c", c=SIDE)[:, :, q * CPP:(q + 1) * CPP]
                        else:
                            x = src[:, t, q * CPP * SIDE:(q + 1) * CPP * SIDE]
                        o = pc[2 * t + q // 2][:, (q % 2) * 256:(q % 2 + 1) * 256]
                        last = mm(o, mats[:, (a * CT + t) * PPG + q], x, start=True, stop=True)
                        if q % 2:
                            last.then_inc(full, 1)

            def image(i, more):
                axis(i, 0, ta, ta_done, x_full)
                if more:
                    norm_mean(i + 1)
                axis(i, 1, tc, tc_done, y_full)
                if more:
                    norm_var(i + 1)

            pe.wait_ge(made, 1)
            norm_mean(0)
            norm_var(0)
            pe.wait_ge(mats_done, 1)
            image(0, True)
            with pe.Fori(1, B - 1) as i:
                image(i, True)
            image(B - 1, False)

        @block.scalar
        def _(act):
            af = nc.scalar.activation

            def norm_square(i):
                for h in range(HALVES):
                    act.wait_ge(centered, HALVES * i + h + 1)
                    if h > 0 or not isinstance(i, int) or i > 0:
                        act.wait_ge(var_full, HALVES * i + h)
                    af(sq[:], xn[:, :, h * T:(h + 1) * T], ACT.Square).then_inc(squared, 1)

            def norm_rstd(i):
                for h in range(HALVES):
                    act.wait_ge(var_full, HALVES * i + h + 1)
                    if not isinstance(i, int) or i > 0:
                        act.wait_ge(normed, HALVES * i)
                    af(rstd[:, h * T:(h + 1) * T], ph[h][:], ACT.Ln, bias=eps_c[:, 0:1]).then_inc(ln_read, 1)
                for h in range(HALVES):
                    act.wait_ge(ln_read, HALVES * i + h + 1)
                    r = rstd[:, h * T:(h + 1) * T]
                    af(r, r, ACT.Exp, scale=-0.5).then_inc(rstd_done, 1)

            def read_x(i):
                for t in range(CT):
                    for j in range(2):
                        act.wait_ge(x_full, 2 * (CT * i + t) + j + 1)
                        if not isinstance(i, int) or i > 0:
                            act.wait_ge(tc_done, CT * (i - 1) + t + 1)
                        o = tb[:, t, j * T:(j + 1) * T].rearrange("p (q c y) -> p q y c", q=2, y=SIDE)
                        for q in range(2):
                            last = af(o[:, q], pc[2 * t + j][:, q * 256:(q + 1) * 256].rearrange("p (y c) -> p y c", c=CPP), ACT.Copy)
                        last.then_inc(x_read, 1)

            def read_y(i):
                for t in range(CT):
                    for j in range(2):
                        act.wait_ge(y_full, 2 * (CT * i + t) + j + 1)
                        if not isinstance(i, int) or i > 0:
                            act.wait_ge(te_done, CT * (i - 1) + t + 1)
                        o = td[:, t].rearrange("p (x c) -> p c x", c=SIDE)[:, j * 16:(j + 1) * 16, :]
                        af(o, pc[2 * t + j][:].rearrange("p (c x) -> p c x", x=SIDE), ACT.Copy).then_inc(y_read, 1)

            def image(i, more):
                read_x(i)
                if more:
                    norm_square(i + 1)
                read_y(i)
                if more:
                    norm_rstd(i + 1)

            nc.scalar.preload_act_table_set("natural_log_exp_and_others")
            act.wait_ge(tapped, 1)
            af(tap[:], tap[:], ACT.Exp, scale=-2.0).then_inc(gauss, 1)
            act.wait_ge(tapped, 2)
            af(mats[:], mats[:], ACT.Exp, scale=-2.0).then_inc(gauss, 1)
            norm_square(0)
            norm_rstd(0)
            image(0, True)
            with act.Fori(1, B - 1) as i:
                image(i, True)
            image(B - 1, False)

        @block.vector
        def _(dve):
            v = nc.vector
            chain = [0]

            def then(instruction):
                chain[0] += 1
                instruction.then_inc(step, 1)
                dve.wait_ge(step, chain[0])

            def over_j(a):
                return a.unsqueeze(1).broadcast_to([P, NMAT, P])

            def over_o(a):
                return a.unsqueeze(2).broadcast_to([P, NMAT, P])

            dve.wait_ge(off_in, 16 * 2 * CT * SIDES)
            dve.wait_ge(made, 1)
            then(v.tensor_copy(lag[:], lag_i[:]))
            then(v.tensor_scalar(whole[:], off[:], MAGIC, None, ALU.add))
            then(v.tensor_scalar(whole[:], whole[:], MAGIC, None, ALU.subtract))
            then(v.tensor_tensor(part[:], off[:], whole[:], ALU.subtract))
            for j in range(5):
                then(v.tensor_scalar(tap[:, j], part[:], float(j - 2), None, ALU.add))
            dve.wait_ge(step, chain[0])
            v.tensor_tensor(tap[:], tap[:], tap[:], ALU.mult).then_inc(tapped, 1)
            then(v.tensor_tensor(work[:], over_j(lag[:]), over_o(whole[:]), ALU.add))
            then(v.tensor_tensor(mats[:], work[:], over_o(part[:]), ALU.add))
            v.tensor_tensor(mats[:], mats[:], mats[:], ALU.mult).then_inc(tapped, 1)
            then(v.tensor_tensor(work[:], work[:], work[:], ALU.mult))
            then(v.tensor_scalar(tmp[:, 0], whole[:], lag[:, 0:1], None, ALU.add))
            then(v.tensor_scalar(tmp[:, 1], tmp[:, 0], 0.0, None, ALU.is_ge))
            then(v.scalar_tensor_tensor(tmp[:, 2], tmp[:, 0], float(SIDE - 1), tmp[:, 1], ALU.is_le, ALU.mult))
            dve.wait_ge(gauss, 1)
            then(v.tensor_tensor(tmp[:, 3], tap[:, 0], tap[:, 1], ALU.add))
            for j in range(2, 5):
                then(v.tensor_tensor(tmp[:, 3], tmp[:, 3], tap[:, j], ALU.add))
            then(v.reciprocal(tmp[:, 3], tmp[:, 3]))
            then(v.tensor_tensor(scale[:], tmp[:, 2], tmp[:, 3], ALU.mult))
            dve.wait_ge(gauss, 2)
            flat = "p j o -> p (j o)"
            then(v.scalar_tensor_tensor(mats[:].rearrange(flat), work[:].rearrange(flat), 4.5, mats[:].rearrange(flat),
                                        ALU.is_le, ALU.mult))
            then(v.tensor_tensor(mats[:], mats[:], over_o(scale[:]), ALU.mult))
            v.tensor_tensor(mats[:], mats[:], over_j(diag[:]), ALU.mult).then_inc(mats_done, 1)

            def norm_center(i):
                dve.wait_ge(x_loaded, 16 * (i + 1))
                for h in range(HALVES):
                    dve.wait_ge(mean_full, HALVES * i + h + 1)
                    x = xn[:, :, h * T:(h + 1) * T]
                    v.tensor_tensor(x, x, ph[h][:].unsqueeze(1).broadcast_to([P, CT, T]), ALU.subtract).then_inc(centered, 1)

            def norm_scale(i):
                for h in range(HALVES):
                    dve.wait_ge(rstd_done, HALVES * i + h + 1)
                    s = slice(h * T, (h + 1) * T)
                    v.tensor_tensor(xn[:, :, s], xn[:, :, s], rstd[:, s].unsqueeze(1).broadcast_to([P, CT, T]),
                                    ALU.mult).then_inc(normed, 1)
                dve.wait_ge(normed, HALVES * (i + 1))
                for t in range(CT):
                    if not isinstance(i, int) or i > 0:
                        dve.wait_ge(x_full, 2 * (CT * (i - 1) + t) + 2)
                    v.transpose(ta[:, t], xn[:, t]).then_inc(ta_done, 1)

            def to_y(i):
                for t in range(CT):
                    dve.wait_ge(x_read, 2 * (CT * i + t) + 2)
                    if not isinstance(i, int) or i > 0:
                        dve.wait_ge(y_full, 2 * (CT * (i - 1) + t) + 2)
                    v.transpose(tc[:, t], tb[:, t]).then_inc(tc_done, 1)

            def finish(i):
                for t in range(CT):
                    dve.wait_ge(y_read, 2 * (CT * i + t) + 2)
                    if not isinstance(i, int) or i > 0:
                        dve.wait_ge(added, i)
                    v.transpose(te[:, t], td[:, t]).then_inc(te_done, 1)
                dve.wait_ge(te_done, CT * (i + 1))
                dve.wait_ge(xres_loaded, 16 * (i + 1))
                if not isinstance(i, int) or i > 0:
                    dve.wait_ge(stored, 16 * i)
                for t in range(CT):
                    last = v.tensor_tensor(res[:, t].rearrange("p (y x) -> p y x", x=SIDE),
                                           te[:, t].rearrange("p (x y) -> p y x", y=SIDE),
                                           xres[:, t].rearrange("p (y x) -> p y x", x=SIDE), ALU.add)
                last.then_inc(added, 1)

            def image(i, more):
                to_y(i)
                if more:
                    norm_center(i + 1)
                finish(i)
                if more:
                    norm_scale(i + 1)

            norm_center(0)
            norm_scale(0)
            image(0, True)
            with dve.Fori(1, B - 1) as i:
                image(i, True)
            image(B - 1, False)

        @block.gpsimd
        def _(pool):
            for s in signals.values():
                nc.gpsimd.sem_clear(s)
            nc.gpsimd.memset(mean_w[:], 1.0 / DM)
            nc.gpsimd.memset(eps_c[:], 1e-6)
            nc.gpsimd.memset(diag[:], 0.0).then_inc(iotas, 1)
            for g in range(SIDES):
                pool.wait_ge(iotas, 2 * g + 1)
                nc.gpsimd.iota(lag_i[g * SIDE:(g + 1) * SIDE, :], pattern=[[0, SIDES], [-1, SIDE]], base=0,
                               channel_multiplier=1).then_inc(iotas, 1)
                pool.wait_ge(iotas, 2 * g + 2)
                nc.gpsimd.memset(diag[g * SIDE:(g + 1) * SIDE, g * SIDE:(g + 1) * SIDE], 1.0).then_inc(iotas, 1)
            pool.wait_ge(iotas, 2 * SIDES + 1)
            nc.gpsimd.sem_inc(made, 1)


def program(nc, x, in_wT, conv_w, conv_b, xp_wT, dt_wT, dt_b, A_log, D, out_wT, W1T_0, b1_0, W2T_0, b2_0,
            offset, W1T_1, b1_1, W2T_1, b2_1, out):
    between = nc.dram_tensor("between_layers", (B, DM, HW), F32).ap()
    mixer(nc, x, between, in_wT, conv_w, conv_b, xp_wT, dt_wT, dt_b, A_log, D, out_wT)
    signals = {}
    ffn(nc, 0, signals, between, between, W1T_0, b1_0, W2T_0, b2_0)
    displace(nc, signals, between, between, out, offset)
    ffn(nc, 1, signals, between, out, W1T_1, b1_1, W2T_1, b2_1)


def kernel(**inputs):
    import numpy as np
    import concourse.bacc as bacc
    from concourse.bass_utils import run_bass_kernel_spmd

    a = {n: np.asarray(v) for n, v in inputs.items()}
    c0 = "L0_conv_"
    arrays = {
        "x": a["x"].reshape(B, DM, HW),
        "in_wT": a[c0 + "in_proj_w"].T, "conv_w": a[c0 + "conv_w"], "conv_b": a[c0 + "conv_b"],
        "xp_wT": a[c0 + "x_proj_w"].T, "dt_wT": a[c0 + "dt_proj_w"].T, "dt_b": a[c0 + "dt_proj_b"],
        "A_log": a[c0 + "A_log"], "D": a[c0 + "D"], "out_wT": a[c0 + "out_proj_w"].T,
        "W1T_0": a["L0_ffn_W1"].T, "b1_0": a["L0_ffn_b1"], "W2T_0": a["L0_ffn_W2"].T, "b2_0": a["L0_ffn_b2"],
        "offset": a["L1_conv_offset"],
        "W1T_1": a["L1_ffn_W1"].T, "b1_1": a["L1_ffn_b1"], "W2T_1": a["L1_ffn_W2"].T, "b2_1": a["L1_ffn_b2"],
    }
    arrays = {f"in_{n}": np.ascontiguousarray(v) for n, v in arrays.items()}
    nc = bacc.Bacc("TRN2", target_bir_lowering=False, num_devices=1)
    args = [nc.dram_tensor(n, v.shape, mybir.dt.from_np(v.dtype), kind="ExternalInput").ap() for n, v in arrays.items()]
    out = nc.dram_tensor("out_dram", (B, DM, HW), F32, kind="ExternalOutput").ap()
    program(nc, *args, out)
    r = run_bass_kernel_spmd(nc, [arrays], core_ids=[0])
    return r.results[0]["out_dram"].reshape(a["x"].shape)
```

```python
import concourse.bass as bass
from concourse import mybir
from contextlib import ExitStack

F32 = mybir.dt.float32
BF16 = mybir.dt.bfloat16
F32R = mybir.dt.float32r
ALU = mybir.AluOpType
ACT = mybir.ActivationFunctionType
AX = mybir.AxisListType

P = 128
B, DM, HW = 8, 384, 1024
CT = DM // P
DI = 2 * DM
KT = DI // P
NS = 16
DTR = (DM + 15) // 16
T = 512
NCHUNK = B * HW // T
STEPS = KT * NS
BC = 2 * NS
DT0 = 3 * BC

SLOTS = 8

PP, PZ, PB = 0, 1, 2
OUT_AT, OUT_IN = (2, 8, 14), (PP, PZ, PP)
GATE_AT, GATE_IN = (20, 26, 36, 59, 70, 84), (PB, PP, PP, PZ, PP, PP)
MEAN_AT, VAR_AT = 23, 30
IN_AT, IN_IN = (40, 43, 47, 50, 53, 56), (PZ, PB, PP, PZ, PB, PP)
XP_AT = 64
DT_AT, DT_IN = (73, 74, 77, 79, 33, 39), (PZ, PB, PZ, PP, PB, PB)
EARLY = 4
SPREAD_AT = 81
GATE_Y_AT = (33, 39, 55, 71, 87, 5)
DT_ADD_AT = (82, 83, 87, 89, 45, 48)
LAG = 5


def mixer(nc, x, x1, in_wT, conv_w, conv_b, xp_wT, dt_wT, dt_b, A_log, D, out_wT):
    with ExitStack() as ctx:
        def sb(name, shape, dt=F32):
            return ctx.enter_context(nc.sbuf_tensor(name, shape, dt))

        def bank(name):
            return ctx.enter_context(nc.psum_tensor(name, [P, T], F32))

        def sem(name):
            return ctx.enter_context(nc.semaphore(name))

        w_in = sb("w_in", [P, CT, 2 * DI])
        w_out = sb("w_out", [P, KT, DM])
        w_x = sb("w_x", [P, KT, DT0 + DTR])
        w_dt = sb("w_dt", [P, DI])
        cw = sb("cw", [P, KT, 3])
        cb = sb("cb", [P, KT])
        dtb = sb("dtb", [P, KT])
        dskip = sb("dskip", [P, KT])
        aneg = sb("aneg", [P, KT, NS])
        ident = sb("ident", [P, P])
        mean_w = sb("mean_w", [P, P])
        sel3 = sb("sel3", [P, BC], BF16)
        eps_c = sb("eps_c", [P, 1])
        zeros2 = sb("zeros2", [P, 2])
        xn = sb("xn", [P, 2, CT, T])
        xres = sb("xres", [P, CT, T])
        sq = sb("sq", [P, CT, T])
        rstd = sb("rstd", [P, T])
        xin = sb("xin", [P, 2, T + 2])
        halo = sb("halo", [P, KT, 2])
        acc = sb("acc", [P, 2, T])
        th = sb("th", [P, 2, T])
        u = sb("u", [P, 2, KT, T])
        bc3 = sb("bc3", [P, T], BF16)
        bcr = sq[:, 0, :]
        bcm = sb("bcm", [P, T], BF16)
        dtr = sb("dtr", [P, T])
        rl = th
        sl = acc
        dt = sb("dt", [P, KT, T])
        dtu = sb("dtu", [P, 2, T])
        b_rep = sb("b_rep", [P, NS, T])
        c_rep = sb("c_rep", [P, NS, T])
        slot = sb("slot", [P, SLOTS, T + 2])
        carry = sb("carry", [P, STEPS])
        gate = sb("gate", [P, 2, T])
        yy = sb("yy", [P, T])

        da = [bank("da0"), bank("da1"), bank("da2")]
        ys = [bank("ys0"), bank("ys1")]
        pg = [bank("pp"), bank("pz"), bank("pb")]
        pp, pz, pb = pg

        weights_in = sem("weights_in")
        consts = sem("consts")
        const_step = sem("const_step")
        halved = sem("halved")
        a_exp = sem("a_exp")
        x_loaded = [sem("x_loaded0"), sem("x_loaded1")]
        xres_loaded, x_stored = sem("xres_loaded"), sem("x_stored")
        mean_full, centered, squared, var_full = sem("mean_full"), sem("centered"), sem("squared"), sem("var_full")
        ln_read, rstd_done, normed = sem("ln_read"), sem("rstd_done"), sem("normed")
        in_full, in_read, conv_part, conv_done = sem("in_full"), sem("in_read"), sem("conv_part"), sem("conv_done")
        th_done, u_done = sem("th_done"), sem("u_done")
        xp_full, xp_read, split_step, bc_done = sem("xp_full"), sem("xp_read"), sem("split_step"), sem("bc_done")
        dt_full, dt_read, sp_exp, sp_done, dt_done = sem("dt_full"), sem("dt_read"), sem("sp_exp"), sem("sp_done"), sem("dt_done")
        bb_full, bb_copied = sem("bb_full"), sem("bb_copied")
        cc_full, cc_copied = sem("cc_full"), sem("cc_copied")
        dtu_done, dbu_done = sem("dtu_done"), sem("dbu_done")
        exp_done, scan_done, mult_done, red_done, carried = sem("exp_done"), sem("scan_done"), sem("mult_done"), sem("red_done"), sem("carried")
        z_full, z_tanh, z_read = sem("z_full"), sem("z_tanh"), sem("z_read")
        y_read, gated = sem("y_read"), sem("gated")
        out_full, res_done = sem("out_full"), sem("res_done")
        block = ctx.enter_context(nc.Block())

        XV = x.rearrange("b (t p) s -> b p t s", p=P)
        X1V = x1.rearrange("b (t p) s -> b p t s", p=P)

        @block.sync
        def _(sp):
            for o, i in ((w_in[:], in_wT.rearrange("(t p) n -> p t n", p=P)),
                         (w_out[:], out_wT.rearrange("(t p) n -> p t n", p=P)),
                         (cw[:], conv_w.rearrange("(t p) j -> p t j", p=P)),
                         (aneg[:], A_log.rearrange("(t p) j -> p t j", p=P)),
                         (w_dt[DT0:DT0 + DTR, :], dt_wT)):
                sp.dma_start(o, i).then_inc(weights_in, 16)
            xw = xp_wT.rearrange("(t p) n -> p t n", p=P)
            for r in range(3):
                sp.dma_start(w_x[:, :, r * BC:(r + 1) * BC], xw[:, :, DTR:]).then_inc(weights_in, 16)
            sp.dma_start(w_x[:, :, DT0:], xw[:, :, 0:DTR]).then_inc(weights_in, 16)
            for o, i in ((cb, conv_b), (dtb, dt_b), (dskip, D)):
                sp.dma_start(o[:], i.rearrange("(t p) -> p t", p=P), allow_slow_non_contiguous=True).then_inc(weights_in, 16)

            def load(b, h):
                d = 2 * b + h
                if not isinstance(d, int) or d >= 2:
                    sp.wait_ge(z_full, KT * (d - 1))
                sp.dma_start(xn[:, h], XV[b, :, :, h * T:(h + 1) * T]).then_inc(x_loaded[h], 16)

            def store(b, h):
                c = 2 * b + h
                if not isinstance(c, int) or c > 0:
                    sp.wait_ge(x_stored, 16 * c)
                sp.dma_start(xres[:], XV[b, :, :, h * T:(h + 1) * T]).then_inc(xres_loaded, 16)
                sp.wait_ge(res_done, CT * (c + 1))
                sp.dma_start(X1V[b, :, :, h * T:(h + 1) * T], xres[:]).then_inc(x_stored, 16)

            load(0, 0)
            load(0, 1)
            load(1, 0)
            store(0, 0)
            load(1, 1)
            store(0, 1)
            with sp.Fori(1, B - 1) as i:
                load(i + 1, 0)
                store(i, 0)
                load(i + 1, 1)
                store(i, 1)
            store(B - 1, 0)
            store(B - 1, 1)
            sp.wait_ge(x_stored, 16 * NCHUNK)

        @block.tensor
        def _(pe):
            mm = nc.tensor.matmul

            def norm_mean(d, h, image, t):
                if t == 0:
                    pe.wait_ge(x_loaded[h], 16 * (image + 1))
                    if not isinstance(d, int) or d > 1:
                        pe.wait_ge(res_done, CT * (d - 2) + 2)
                    elif d == 1:
                        pe.wait_ge(dt_read, EARLY)
                last = mm(pz[:], mean_w[:], xn[:, h, t], start=t == 0, stop=t == CT - 1)
                if t == CT - 1:
                    last.then_inc(mean_full, 1)

            def norm_var(d, t):
                if t == 0:
                    pe.wait_ge(squared, d + 1)
                last = mm(pz[:], mean_w[:], sq[:, t], start=t == 0, stop=t == CT - 1)
                if t == CT - 1:
                    last.then_inc(var_full, 1)

            def in_proj(d, h, m, t):
                if t == 0 and m == 0:
                    pe.wait_ge(normed, d + 1)
                if t == 0 and m == 1 and (not isinstance(d, int) or d > 0):
                    pe.wait_ge(dt_read, KT * d)
                if t == 0 and m == 2 and (not isinstance(d, int) or d > 0):
                    pe.wait_ge(z_read, KT * (d - 1) + 3)
                if t == 0 and m >= 3:
                    pe.wait_ge(in_read, KT * d + m - 2)
                last = mm(pg[IN_IN[m]][:], w_in[:, t, m * P:(m + 1) * P], xn[:, h, t], start=t == 0, stop=t == CT - 1)
                if t == CT - 1:
                    last.then_inc(in_full, 1)

            def x_proj(d, h, k):
                if k == 0:
                    pe.wait_ge(in_read, KT * d + 5)
                pe.wait_ge(u_done, KT * d + k + 1)
                last = mm(pb[0:DT0 + DTR, :], w_x[:, k], u[:, h, k], start=k == 0, stop=k == KT - 1)
                if k == KT - 1:
                    last.then_inc(xp_full, 1)

            def dt_proj(d, m):
                if m == 0:
                    pe.wait_ge(bc_done, d + 1)
                    if not isinstance(d, int) or d > 0:
                        pe.wait_ge(z_read, KT * (d - 1) + 4)
                    else:
                        pe.wait_ge(in_read, KT)
                if m == 1:
                    pe.wait_ge(bc_done, d + 1)
                if m == 2:
                    pe.wait_ge(dt_read, KT * d + 1)
                if m == 3 and (not isinstance(d, int) or d > 0):
                    pe.wait_ge(z_read, KT * (d - 1) + 5)
                if m == 4:
                    pe.wait_ge(z_read, KT * d + 1)
                if m == 5:
                    pe.wait_ge(dt_read, KT * d + 5)
                mm(pg[DT_IN[m]][:], w_dt[DT0:DT0 + DTR, m * P:(m + 1) * P], dtr[DT0:DT0 + DTR, :],
                   start=True, stop=True).then_inc(dt_full, 1)

            def spread(d, n):
                if n == 0:
                    pe.wait_ge(bc_done, d + 1)
                    pe.wait_ge(dt_read, KT * d + 3)
                else:
                    pe.wait_ge(bb_copied, NS * d + n)
                mm(pb[:], sel3[0:DT0, n:n + 1].broadcast_to([DT0, P]), bc3[0:DT0, :], start=True,
                   stop=True).then_inc(bb_full, 1)
                if n > 0:
                    pe.wait_ge(cc_copied, NS * d + n)
                mm(pz[:], sel3[0:DT0, NS + n:NS + n + 1].broadcast_to([DT0, P]), bc3[0:DT0, :], start=True,
                   stop=True).then_inc(cc_full, 1)

            def gate_proj(c, h, k, t):
                if t == 0 and k == 0:
                    pe.wait_ge(bb_copied, NS * (c + 1))
                if t == 0 and k == 1:
                    if not isinstance(c, int) or c > 0:
                        pe.wait_ge(res_done, CT * c)
                    else:
                        pe.wait_ge(dt_read, EARLY)
                if t == 0 and k == 2:
                    pe.wait_ge(z_read, KT * c + 2)
                if t == 0 and k == 3:
                    if not isinstance(c, int) or c < NCHUNK - 1:
                        pe.wait_ge(in_read, KT * (c + 1) + 4)
                    else:
                        pe.wait_ge(res_done, CT * (c - 1) + 2)
                if t == 0 and k == 4:
                    if not isinstance(c, int) or c < NCHUNK - 1:
                        pe.wait_ge(in_read, KT * (c + 1) + 6)
                    else:
                        pe.wait_ge(z_read, KT * c + 3)
                if t == 0 and k == 5:
                    if not isinstance(c, int) or c < NCHUNK - 1:
                        pe.wait_ge(dt_read, KT * (c + 1) + 4)
                    else:
                        pe.wait_ge(z_read, KT * c + 5)
                last = mm(pg[GATE_IN[k]][:], w_in[:, t, DI + k * P:DI + (k + 1) * P], xn[:, h, t], start=t == 0, stop=t == CT - 1)
                if t == CT - 1:
                    last.then_inc(z_full, 1)

            def out_proj(c, h, m, k):
                if k == 0 and m == 0:
                    pe.wait_ge(gated, KT * c + KT - 1)
                    pe.wait_ge(z_read, KT * (c + 1))
                if k == KT - 1 and m == 0:
                    pe.wait_ge(gated, KT * (c + 1))
                if k == 0 and m == 1:
                    if isinstance(c, int) and c == NCHUNK - 1:
                        pe.wait_ge(z_read, KT * c + 4)
                    else:
                        pe.wait_ge(cc_copied, NS * (c + 2))
                if k == 0 and m == 2:
                    pe.wait_ge(res_done, CT * c + 1)
                last = mm(pg[OUT_IN[m]][:], w_out[:, k, m * P:(m + 1) * P], u[:, h, k], start=k == 0, stop=k == KT - 1)
                if k == KT - 1:
                    last.then_inc(out_full, 1)

            def reduce_state(c, k, n):
                s = STEPS * c + NS * k + n
                pe.wait_ge(mult_done, s + 1)
                if n == 0 and (not isinstance(c, int) or KT * c + k >= 2):
                    pe.wait_ge(y_read, KT * c + k - 1)
                mm(ys[k % 2][:], ident[:], slot[:, (NS * k + n) % SLOTS, 0:T], start=n == 0, stop=n == NS - 1).then_inc(red_done, 1)

            def scan(b, h, before, after):
                c = 2 * b + h
                d = c + 1
                for q in range(STEPS):
                    reduce_state(c, q // NS, q % NS)
                    if before and q < SPREAD_AT + NS - STEPS:
                        spread(c, q + STEPS - SPREAD_AT)
                    for m in range(CT):
                        if before and 0 <= q - OUT_AT[m] < KT:
                            out_proj(c - 1, 1 - h, m, q - OUT_AT[m])
                    for k in range(KT):
                        if 0 <= q - GATE_AT[k] < CT:
                            gate_proj(c, h, k, q - GATE_AT[k])
                        if after and 0 <= q - IN_AT[k] < CT:
                            in_proj(d, 1 - h, k, q - IN_AT[k])
                        if q == DT_AT[k] and (after or k >= EARLY):
                            dt_proj(d if k < EARLY else c, k)
                    if after and 0 <= q - MEAN_AT < CT:
                        norm_mean(d, 1 - h, b + h, q - MEAN_AT)
                    if after and 0 <= q - VAR_AT < CT:
                        norm_var(d, q - VAR_AT)
                    if after and 0 <= q - XP_AT < KT:
                        x_proj(d, 1 - h, q - XP_AT)
                    if after and q >= SPREAD_AT:
                        spread(d, q - SPREAD_AT)

            pe.wait_ge(weights_in, 16 * 12)
            pe.wait_ge(consts, 1)
            for t in range(CT):
                norm_mean(0, 0, 0, t)
            for t in range(CT):
                norm_var(0, t)
            for m in range(KT):
                for t in range(CT):
                    in_proj(0, 0, m, t)
            for k in range(KT):
                x_proj(0, 0, k)
            for m in range(EARLY):
                dt_proj(0, m)
            for n in range(NS):
                spread(0, n)
            pe.wait_ge(halved, 1)
            scan(0, 0, False, True)
            with pe.Fori(0, NCHUNK // 2 - 1) as i:
                scan(i, 1, True, True)
                scan(i + 1, 0, True, True)
            scan(B - 1, 1, True, False)
            for m in range(CT):
                for k in range(KT):
                    out_proj(NCHUNK - 1, 1, m, k)

        @block.scalar
        def _(act):
            af = nc.scalar.activation

            def norm_square(d, h):
                act.wait_ge(centered, d + 1)
                af(sq[:], xn[:, h], ACT.Square).then_inc(squared, 1)

            def norm_rstd(d):
                nc.scalar.preload_act_table_set("natural_log_exp_and_others")
                act.wait_ge(var_full, d + 1)
                if not isinstance(d, int) or d > 0:
                    act.wait_ge(normed, d)
                af(rstd[:], pz[:], ACT.Ln, bias=eps_c[:, 0:1]).then_inc(ln_read, 1)
                act.wait_ge(ln_read, d + 1)
                af(rstd[:], rstd[:], ACT.Exp, scale=-0.5).then_inc(rstd_done, 1)

            def conv_in(d, h, m):
                act.wait_ge(in_full, KT * d + m + 1)
                if not isinstance(d, int) or KT * d + m >= 2:
                    act.wait_ge(u_done, KT * d + m - 1)
                if m < 2 and (not isinstance(d, int) or d > 0):
                    act.wait_ge(dt_done, KT * d + m - 1)
                j = m % 2
                ps = pg[IN_IN[m]]
                af(xin[:, j, 2:], ps[:], ACT.Copy)
                af(xin[:, j, 0:2], halo[:, m] if h else zeros2[:], ACT.Copy)
                if h == 0:
                    af(halo[:, m], ps[:, T - 2:], ACT.Copy)
                af(acc[:, j], ps[:], ACT.Identity, bias=cb[:, m:m + 1], scale=cw[:, m, 2:3]).then_inc(in_read, 1)

            def conv_tanh(d, m):
                act.wait_ge(conv_done, KT * d + m + 1)
                if not isinstance(d, int) or KT * d + m >= 2:
                    act.wait_ge(u_done, KT * d + m - 1)
                af(th[:, m % 2], acc[:, m % 2], ACT.Tanh).then_inc(th_done, 1)

            def dt_read_tile(d, m):
                act.wait_ge(dt_full, KT * d + m + 1)
                if not isinstance(d, int) or KT * d + m >= 2:
                    act.wait_ge(dt_done, KT * d + m - 1)
                af(sl[:, m % 2], pg[DT_IN[m]][:], ACT.Abs, bias=dtb[:, m:m + 1])
                af(rl[:, m % 2], pg[DT_IN[m]][:], ACT.Relu, bias=dtb[:, m:m + 1]).then_inc(dt_read, 1)

            def softplus(d, m):
                act.wait_ge(dt_read, KT * d + m + 1)
                af(sl[:, m % 2], sl[:, m % 2], ACT.Exp, scale=-1.0).then_inc(sp_exp, 1)
                act.wait_ge(sp_exp, KT * d + m + 1)
                af(sl[:, m % 2], sl[:, m % 2], ACT.Ln, bias=1.0).then_inc(sp_done, 1)

            def spread_copy(d, n):
                act.wait_ge(bb_full, NS * d + n + 1)
                if not isinstance(d, int) or d > 0:
                    act.wait_ge(dbu_done, STEPS * (d - 1) + NS * (KT - 1) + n + 1)
                af(b_rep[:, n], pb[:], ACT.Copy).then_inc(bb_copied, 1)
                act.wait_ge(cc_full, NS * d + n + 1)
                if not isinstance(d, int) or d > 0:
                    act.wait_ge(mult_done, STEPS * (d - 1) + NS * (KT - 1) + n + 1)
                af(c_rep[:, n], pz[:], ACT.Copy).then_inc(cc_copied, 1)

            def gate_tanh(c, k):
                act.wait_ge(z_full, KT * c + k + 1)
                if not isinstance(c, int) or KT * c + k >= 2:
                    act.wait_ge(gated, KT * c + k - 1)
                af(gate[:, k % 2], pg[GATE_IN[k]][:], ACT.Tanh, scale=0.5).then_inc(z_tanh, 1)

            def decay(c, k, n):
                s = STEPS * c + NS * k + n
                if n == 0:
                    act.wait_ge(dt_done, KT * c + k + 1)
                if not isinstance(c, int) or s >= 3:
                    act.wait_ge(scan_done, s - 2)
                af(da[(NS * k + n) % 3][:], dt[:, k], ACT.Exp, scale=aneg[:, k, n:n + 1]).then_inc(exp_done, 1)

            def keep_state(b, q):
                act.wait_ge(scan_done, STEPS * 2 * b + q + 1)
                af(carry[:, q:q + 1], slot[:, q % SLOTS, T:T + 1], ACT.Copy).then_inc(carried, 1)

            def scan(b, h, before, after):
                c = 2 * b + h
                d = c + 1
                for q in range(STEPS):
                    decay(c, q // NS, q % NS)
                    if h == 0 and q >= 3:
                        keep_state(b, q - 3)
                    for k in range(KT):
                        if q == GATE_AT[k] + CT - 1 + LAG:
                            gate_tanh(c, k)
                        if after and q == IN_AT[k] + CT - 1 + LAG:
                            conv_in(d, 1 - h, k)
                        if after and q == IN_AT[k] + CT - 1 + LAG + 4:
                            conv_tanh(d, k)
                        if q == DT_AT[k] + LAG and (after or k >= EARLY):
                            if k == 0:
                                nc.scalar.preload_act_table_set("natural_log_exp_and_others")
                            dt_read_tile(d if k < EARLY else c, k)
                            softplus(d if k < EARLY else c, k)
                    if after and q == MEAN_AT + CT - 1 + 4:
                        norm_square(d, 1 - h)
                    if after and q == VAR_AT + CT - 1 + LAG:
                        norm_rstd(d)
                    if not after and q == VAR_AT + CT - 1 + LAG:
                        nc.scalar.preload_act_table_set("natural_log_exp_and_others")
                    if before and q < SPREAD_AT + LAG + NS - STEPS:
                        spread_copy(c, q + STEPS - SPREAD_AT - LAG)
                    if after and q >= SPREAD_AT + LAG:
                        spread_copy(d, q - SPREAD_AT - LAG)
                if h == 0:
                    for q in range(STEPS - 3, STEPS):
                        keep_state(b, q)

            act.wait_ge(weights_in, 16 * 12)
            act.wait_ge(consts, 1)
            af(aneg[:], aneg[:], ACT.Exp).then_inc(a_exp, 1)
            act.wait_ge(halved, 1)
            norm_square(0, 0)
            norm_rstd(0)
            for m in range(KT):
                conv_in(0, 0, m)
                conv_tanh(0, m)
            nc.scalar.preload_act_table_set("natural_log_exp_and_others")
            for m in range(EARLY):
                dt_read_tile(0, m)
                softplus(0, m)
            for n in range(NS):
                spread_copy(0, n)
            scan(0, 0, False, True)
            with act.Fori(0, NCHUNK // 2 - 1) as i:
                scan(i, 1, True, True)
                scan(i + 1, 0, True, True)
            scan(B - 1, 1, True, False)

        @block.gpsimd
        def _(pool):
            tt = nc.gpsimd.tensor_tensor
            nc.gpsimd.memset(ident[:], 0.0)
            nc.gpsimd.memset(sel3[:], 0.0).then_inc(const_step, 1)
            nc.gpsimd.memset(zeros2[:], 0.0)
            nc.gpsimd.memset(eps_c[:], 1e-6)
            nc.gpsimd.memset(mean_w[:], 1.0 / DM)
            pool.wait_ge(const_step, 1)
            nc.gpsimd.affine_select(out=ident[:], in_=ident[:], compare_op=ALU.not_equal, fill=1.0, base=0,
                                    pattern=[[-1, P]], channel_multiplier=1)
            for r in range(3):
                nc.gpsimd.affine_select(out=sel3[:], in_=sel3[:], compare_op=ALU.not_equal, fill=1.0,
                                               base=-BC * r, pattern=[[-1, BC]], channel_multiplier=1).then_inc(const_step, 1)
                pool.wait_ge(const_step, r + 2)
            nc.gpsimd.sem_inc(consts, 1)

            def dt_add(d, m):
                pool.wait_ge(sp_done, KT * d + m + 1)
                if not isinstance(d, int) or d > 0:
                    pool.wait_ge(exp_done, STEPS * (d - 1) + NS * (m + 1))
                tt(dt[:, m], rl[:, m % 2], sl[:, m % 2], ALU.add).then_inc(dt_done, 1)

            def dt_u(c, h, k):
                pool.wait_ge(dt_done, KT * c + k + 1)
                pool.wait_ge(u_done, KT * (c + 1))
                tt(dtu[:, k % 2], dt[:, k], u[:, h, k], ALU.mult).then_inc(dtu_done, 1)

            def drive(b, h, k, n):
                c = 2 * b + h
                q = NS * k + n
                s = STEPS * c + q
                if n == 0:
                    pool.wait_ge(dtu_done, KT * c + k + 1)
                if k == 0:
                    pool.wait_ge(bb_copied, NS * c + n + 1)
                if not isinstance(c, int) or s >= SLOTS:
                    pool.wait_ge(red_done, s - SLOTS + 1)
                if h == 0 and q >= SLOTS:
                    pool.wait_ge(carried, STEPS * b + q - SLOTS + 1)
                if h == 1 and q < SLOTS:
                    pool.wait_ge(carried, STEPS * (b + 1) + q - SLOTS + 1)
                tt(slot[:, q % SLOTS, 1:T + 1], dtu[:, k % 2], b_rep[:, n], ALU.mult).then_inc(dbu_done, 1)

            def gate_y(c, h, k):
                pool.wait_ge(y_read, KT * c + k + 1)
                pool.wait_ge(z_read, KT * c + k + 1)
                tt(u[:, h, k], yy[:], gate[:, k % 2], ALU.mult).then_inc(gated, 1)

            def scan(b, h, before, after):
                c = 2 * b + h
                for q in range(STEPS):
                    drive(b, h, q // NS, q % NS)
                    for k in range(KT):
                        if k < KT - 1 and q == GATE_Y_AT[k]:
                            gate_y(c, h, k)
                        if q == DT_ADD_AT[k] and (after or k >= EARLY):
                            dt_add(c + 1 if k < EARLY else c, k)
                    if before and q == GATE_Y_AT[KT - 1]:
                        gate_y(c - 1, 1 - h, KT - 1)
                    if q % NS == NS - 4:
                        if q // NS + 1 < KT:
                            dt_u(c, h, q // NS + 1)
                        elif after:
                            dt_u(c + 1, 1 - h, 0)

            for m in range(EARLY):
                dt_add(0, m)
            dt_u(0, 0, 0)
            scan(0, 0, False, True)
            with pool.Fori(0, NCHUNK // 2 - 1) as i:
                scan(i, 1, True, True)
                scan(i + 1, 0, True, True)
            scan(B - 1, 1, True, False)
            gate_y(NCHUNK - 1, 1, KT - 1)

        @block.vector
        def _(dve):
            v = nc.vector
            v.memset(yy[:], 0.0)

            def norm_center(d, h, image):
                dve.wait_ge(mean_full, d + 1)
                dve.wait_ge(x_loaded[h], 16 * (image + 1))
                v.tensor_tensor(xn[:, h], xn[:, h], pz[:].unsqueeze(1).broadcast_to([P, CT, T]), ALU.subtract).then_inc(centered, 1)

            def norm_scale(d, h):
                dve.wait_ge(rstd_done, d + 1)
                v.tensor_tensor(xn[:, h], xn[:, h], rstd[:].unsqueeze(1).broadcast_to([P, CT, T]), ALU.mult).then_inc(normed, 1)

            def conv(d, m):
                j = m % 2
                dve.wait_ge(in_read, KT * d + m + 1)
                v.scalar_tensor_tensor(acc[:, j], xin[:, j, 1:T + 1], cw[:, m, 1:2], acc[:, j], ALU.mult, ALU.add).then_inc(conv_part, 1)
                dve.wait_ge(conv_part, KT * d + m + 1)
                v.scalar_tensor_tensor(acc[:, j], xin[:, j, 0:T], cw[:, m, 0:1], acc[:, j], ALU.mult, ALU.add).then_inc(conv_done, 1)

            def conv_silu(d, h, m):
                dve.wait_ge(th_done, KT * d + m + 1)
                if m == 0 and (not isinstance(d, int) or d >= 2):
                    dve.wait_ge(out_full, CT * (d - 1))
                v.scalar_tensor_tensor(u[:, h, m], th[:, m % 2], 1.0, acc[:, m % 2], ALU.add, ALU.mult).then_inc(u_done, 1)

            def split(d):
                dve.wait_ge(xp_full, d + 1)
                if not isinstance(d, int) or d > 0:
                    dve.wait_ge(cc_full, NS * d)
                v.tensor_copy(bc3[0:DT0, :], pb[0:DT0, :]).then_inc(split_step, 1)
                v.tensor_copy(dtr[DT0:DT0 + DTR, :], pb[DT0:DT0 + DTR, :])
                dve.wait_ge(split_step, 3 * d + 1)
                v.tensor_tensor(bcr[0:DT0, :], pb[0:DT0, :], bc3[0:DT0, :], ALU.subtract).then_inc(split_step, 1)
                dve.wait_ge(split_step, 3 * d + 2)
                v.tensor_copy(bcm[0:DT0, :], bcr[0:DT0, :]).then_inc(split_step, 1)
                dve.wait_ge(split_step, 3 * d + 3)
                v.tensor_copy(bc3[BC:2 * BC, :], bcm[BC:2 * BC, :])
                v.tensor_tensor(bc3[2 * BC:DT0, :], bcr[2 * BC:DT0, :], bcm[2 * BC:DT0, :], ALU.subtract).then_inc(bc_done, 1)

            def recur(b, h, k, n):
                c = 2 * b + h
                q = NS * k + n
                s = STEPS * c + q
                dve.wait_ge(exp_done, s + 1)
                dve.wait_ge(dbu_done, s + 1)
                if h == 1 and q == 0:
                    dve.wait_ge(carried, STEPS * (b + 1))
                at = slot[:, q % SLOTS, 1:T + 1]
                v.tensor_tensor_scan(at, da[q % 3][:], at, carry[:, q:q + 1] if h else 0.0, ALU.mult,
                                     ALU.add).then_inc(scan_done, 1)

            def times_c(c, h, k, n):
                q = NS * k + n
                s = STEPS * c + q
                dve.wait_ge(scan_done, s + 1)
                if k == 0:
                    dve.wait_ge(cc_copied, NS * c + n + 1)
                v.tensor_tensor(slot[:, q % SLOTS, 0:T], slot[:, q % SLOTS, 1:T + 1], c_rep[:, n],
                                ALU.mult).then_inc(mult_done, 1)

            def gate_z(c, k):
                dve.wait_ge(z_tanh, KT * c + k + 1)
                v.scalar_tensor_tensor(gate[:, k % 2], gate[:, k % 2], 1.0, pg[GATE_IN[k]][:], ALU.add, ALU.mult).then_inc(z_read, 1)

            def read_y(c, h, k):
                dve.wait_ge(red_done, STEPS * c + NS * (k + 1))
                if not isinstance(c, int) or KT * c + k > 0:
                    dve.wait_ge(gated, KT * c + k)
                v.scalar_tensor_tensor(yy[:], u[:, h, k], dskip[:, k:k + 1], ys[k % 2][:], ALU.mult, ALU.add).then_inc(y_read, 1)

            def residual(c, m):
                dve.wait_ge(out_full, CT * c + m + 1)
                dve.wait_ge(xres_loaded, 16 * (c + 1))
                v.tensor_tensor(xres[:, m], xres[:, m], pg[OUT_IN[m]][:], ALU.add).then_inc(res_done, 1)

            def scan(b, h, before, after):
                c = 2 * b + h
                d = c + 1
                recur(b, h, 0, 0)
                for q in range(STEPS):
                    if q + 1 < STEPS:
                        recur(b, h, (q + 1) // NS, (q + 1) % NS)
                    times_c(c, h, q // NS, q % NS)
                    for m in range(CT):
                        if before and q == OUT_AT[m] + KT + 1:
                            residual(c - 1, m)
                    if before and q == 2:
                        read_y(c - 1, 1 - h, KT - 1)
                    if q >= NS and q % NS == 2:
                        read_y(c, h, q // NS - 1)
                    for k in range(KT):
                        if q == GATE_AT[k] + CT + LAG:
                            gate_z(c, k)
                        if after and q == IN_AT[k] + CT + LAG:
                            conv(d, k)
                        if after and q == IN_AT[k] + CT + LAG + 4:
                            conv_silu(d, 1 - h, k)
                    if after and q == MEAN_AT + CT + 1:
                        norm_center(d, 1 - h, b + h)
                    if after and q == VAR_AT + CT + LAG:
                        norm_scale(d, 1 - h)
                    if after and q == XP_AT + KT + 1:
                        split(d)

            dve.wait_ge(weights_in, 16 * 12)
            dve.wait_ge(a_exp, 1)
            v.tensor_scalar(aneg[:], aneg[:], -1.0, None, ALU.mult)
            v.tensor_scalar(cw[:], cw[:], 0.5, None, ALU.mult)
            v.tensor_scalar(cb[:], cb[:], 0.5, None, ALU.mult)
            v.tensor_scalar(w_out[:], w_out[:], 0.5, None, ALU.mult).then_inc(halved, 1)
            dve.wait_ge(halved, 1)
            norm_center(0, 0, 0)
            norm_scale(0, 0)
            for m in range(KT):
                conv(0, m)
                conv_silu(0, 0, m)
            split(0)
            scan(0, 0, False, True)
            with dve.Fori(0, NCHUNK // 2 - 1) as i:
                scan(i, 1, True, True)
                scan(i + 1, 0, True, True)
            scan(B - 1, 1, True, False)
            read_y(NCHUNK - 1, 1, KT - 1)
            for m in range(CT):
                residual(NCHUNK - 1, m)


GROUPS = 5
FFN_B = GROUPS * (B // GROUPS)
HID = 4 * DM
MT = HID // P
Q_EPS, Q_BOUND = 1e-5, 128.0
Q_CLIP = Q_BOUND - Q_EPS
HALVES = HW // T
BEHIND = 4
MEAN_BEFORE = MT - 3


def ffn(nc, layer, signals, x_in, x_out, W1T, b1, W2T, b2):
    assert B // GROUPS == 1
    with ExitStack() as ctx:
        def sb(name, shape, dt=F32):
            return ctx.enter_context(nc.sbuf_tensor(f"{name}_f{layer}", shape, dt))

        def sem(name):
            if name not in signals:
                signals[name] = nc.alloc_semaphore(f"{name}_f")
            return signals[name]

        def bank(name):
            return ctx.enter_context(nc.psum_tensor(f"{name}_f{layer}", [P, T], F32))

        w1 = sb("w1", [P, CT, HID], F32R)
        w2 = sb("w2", [P, MT, DM], F32R)
        hid = sb("hid", [P, MT, HW])
        raw1 = hid[:, 0:MT // 2, :].rearrange("p m n -> p (m n)")[:, 0:CT * HID].rearrange("p (t n) -> p t n", t=CT)
        raw2 = hid[:, MT // 2:, :].rearrange("p m n -> p (m n)")[:, 0:MT * DM].rearrange("p (t n) -> p t n", t=MT)
        bias1 = sb("bias1", [P, MT])
        bias2 = sb("bias2", [P, CT])
        wsum = sb("wsum", [P, 2, GROUPS])
        wmean = sb("wmean", [P, 2, GROUPS])
        ones = sb("ones", [P, P])
        mean_w = sb("mean_w", [P, P])
        ident = sb("ident", [P, P])
        eps_t = sb("eps_t", [P, 1])
        xn = sb("xn", [P, CT, HW])
        xh = sb("xh", [P, CT, HW], F32R)
        xl = sb("xl", [P, CT, HW], F32R)
        sq = sb("sq", [P, HALVES, CT, T])
        rstd = sb("rstd", [P, HW])
        xres = sb("xres", [P, CT, HW])
        y2 = sb("y2", [P, CT, HW])
        g = sb("g", [P, 2, HW])
        gh = sb("gh", [P, 3, HW], F32R)
        gl = sb("gl", [P, 3, HW], F32R)
        big = sb("big", [P, 2, MT])
        top = sb("top", [P, 2])
        top1 = sb("top1", [P, 2])
        gain = [sb(f"gain{j}", [P, 1]) for j in range(2)]
        acc = [bank(f"acc{j}") for j in range(CT * HALVES)]
        ph = [bank(f"ph{j}") for j in range(HALVES)]

        w1_in, w2_in, bias_in, consts, const_step = sem("w1_in"), sem("w2_in"), sem("bias_in"), sem("consts"), sem("const_step")
        summed, sums_full, means_done, signed = sem("summed"), sem("sums_full"), sem("means_done"), sem("signed")
        x_loaded, xres_loaded, stored = sem("x_loaded"), sem("xres_loaded"), sem("stored")
        mean_full, centered, squared, var_full = sem("mean_full"), sem("centered"), sem("squared"), sem("var_full")
        ln_read, rstd_done, normed, split_hi, split_lo = sem("ln_read"), sem("rstd_done"), sem("normed"), sem("split_hi"), sem("split_lo")
        up_full, up_read, up_max = sem("up_full"), sem("up_read"), sem("up_max")
        gelu_done, g_hi, g_lo, down_full = sem("gelu_done"), sem("g_hi"), sem("g_lo"), sem("down_full")
        down_read, down_max, quant, added = sem("down_read"), sem("down_max"), sem("quant"), sem("added")
        top_col, top_row, top_one, top_all, top_eps, top_inv, gain_done = (
            [sem(f"{n}{j}") for j in range(2)] for n in
            ("top_col", "top_row", "top_one", "top_all", "top_eps", "top_inv", "gain_done"))
        block = ctx.enter_context(nc.Block())
        XIN = x_in.rearrange("b (t p) s -> b p t s", p=P)
        XOUT = x_out.rearrange("b (t p) s -> b p t s", p=P)

        @block.sync
        def _(sp):
            sp.dma_start(xn[:], XIN[0]).then_inc(x_loaded, 16)
            sp.dma_start(raw1, W1T.rearrange("(t p) n -> p t n", p=P)).then_inc(w1_in, 16)
            sp.dma_start(raw2, W2T.rearrange("(t p) n -> p t n", p=P)).then_inc(w2_in, 16)
            sp.dma_start(bias1[:], b1.rearrange("(t p) -> p t", p=P), allow_slow_non_contiguous=True).then_inc(bias_in, 16)
            sp.dma_start(bias2[:], b2.rearrange("(t p) -> p t", p=P), allow_slow_non_contiguous=True).then_inc(bias_in, 16)

            def load(i):
                sp.wait_ge(split_lo, HALVES * i)
                sp.dma_start(xn[:], XIN[i]).then_inc(x_loaded, 16)

            def finish(i, more):
                sp.wait_ge(added, i + 1)
                sp.dma_start(XOUT[i], y2[:]).then_inc(stored, 16)
                if more:
                    sp.dma_start(xres[:], XIN[i + 1]).then_inc(xres_loaded, 16)

            sp.dma_start(xres[:], XIN[0]).then_inc(xres_loaded, 16)
            load(1)
            load(2)
            with sp.Fori(0, FFN_B - 3) as i:
                load(i + 3)
                finish(i, True)
            for i in range(FFN_B - 3, FFN_B):
                finish(i, i < FFN_B - 1)
            sp.wait_ge(stored, 16 * FFN_B)

        @block.tensor
        def _(pe):
            mm = nc.tensor.matmul

            def norm_mean(i):
                pe.wait_ge(x_loaded, 16 * (i + 1))
                for h in range(HALVES):
                    if not isinstance(i, int) or i > 0:
                        pe.wait_ge(up_read, HALVES * (MT * (i - 1) + MEAN_BEFORE - 1) + h + 1)
                    for t in range(CT):
                        last = mm(ph[h][:], mean_w[:], xn[:, t, h * T:(h + 1) * T], start=t == 0, stop=t == CT - 1)
                    last.then_inc(mean_full, 1)

            def norm_var(i):
                for h in range(HALVES):
                    pe.wait_ge(squared, HALVES * i + h + 1)
                    if not isinstance(i, int) or i > 0:
                        pe.wait_ge(up_read, HALVES * (MT * i - 1) + h + 1)
                    for t in range(CT):
                        last = mm(ph[h][:], mean_w[:], sq[:, h, t], start=t == 0, stop=t == CT - 1)
                    last.then_inc(var_full, 1)

            def up(i, m, mean_between):
                for h in range(HALVES):
                    if m == 0:
                        pe.wait_ge(split_lo, HALVES * i + h + 1)
                        pe.wait_ge(split_hi, HALVES * i + h + 1)
                    elif m == MEAN_BEFORE and mean_between:
                        pe.wait_ge(centered, HALVES * (i + 1) + h + 1)
                    else:
                        pe.wait_ge(up_read, HALVES * (MT * i + m - 1) + h + 1)
                    for part, x in enumerate((xh, xl)):
                        for t in range(CT):
                            last = mm(ph[h][:], w1[:, t, m * P:(m + 1) * P], x[:, t, h * T:(h + 1) * T],
                                      start=part == 0 and t == 0, stop=part == 1 and t == CT - 1)
                    last.then_inc(up_full, 1)

            def down(i, k):
                for part, (x, ready) in enumerate(((gh, g_hi), (gl, g_lo))):
                    pe.wait_ge(ready, MT * i + k + 1)
                    for m in range(CT):
                        for h in range(HALVES):
                            if k == 0 and part == 0 and (not isinstance(i, int) or i > 0):
                                pe.wait_ge(down_read, CT * HALVES * i)
                                pe.wait_ge(gain_done[1], i)
                            last = mm(acc[HALVES * m + h][:], w2[:, k, m * P:(m + 1) * P],
                                      x[:, k % 3, h * T:(h + 1) * T], start=k == 0 and part == 0,
                                      stop=k == MT - 1 and part == 1)
                last.then_inc(down_full, 1)

            def top_to_row(i, j):
                pe.wait_ge(top_col[j], i + 1)
                mm(acc[2 * j][0:1, 0:P], top[:, j:j + 1], ident[:], start=True, stop=True).then_inc(top_row[j], 1)

            def top_to_all(i, j):
                pe.wait_ge(top_one[j], i + 1)
                mm(acc[2 * j + 1][:, 0:1], ones[0:1, :], top1[0:1, j:j + 1], start=True, stop=True).then_inc(top_all[j], 1)

            def image(i, more, more2):
                if more:
                    norm_var(i + 1)
                top_to_row(i, 0)
                top_to_all(i, 0)
                for k in range(MT):
                    down(i, k)
                    if more and k >= BEHIND:
                        up(i + 1, k - BEHIND, more2)
                if more:
                    for m in range(MT - BEHIND, MT):
                        if m == MEAN_BEFORE and more2:
                            norm_mean(i + 2)
                        up(i + 1, m, more2)
                        if m == MT - 2:
                            top_to_row(i, 1)
                    top_to_all(i, 1)
                else:
                    top_to_row(i, 1)
                    top_to_all(i, 1)

            pe.wait_ge(consts, 1)
            norm_mean(0)
            norm_var(0)
            pe.wait_ge(summed, GROUPS)
            mm(acc[0][:, 0:GROUPS], ones[:], wsum[:, 0], start=True, stop=True).then_inc(sums_full, 1)
            pe.wait_ge(signed, 1)
            for m in range(MT):
                if m == 2:
                    pe.wait_ge(summed, 2 * GROUPS)
                    mm(acc[2][:, 0:GROUPS], ones[:], wsum[:, 1], start=True, stop=True).then_inc(sums_full, 1)
                if m == MEAN_BEFORE:
                    norm_mean(1)
                up(0, m, True)
            pe.wait_ge(signed, 2)
            image(0, True, True)
            with pe.Fori(1, FFN_B - 2) as i:
                image(i, True, True)
            image(FFN_B - 2, True, False)
            image(FFN_B - 1, False, False)

        @block.scalar
        def _(act):
            af = nc.scalar.activation

            def norm_square(i, h):
                act.wait_ge(centered, HALVES * i + h + 1)
                if not isinstance(i, int) or i > 0:
                    act.wait_ge(var_full, HALVES * (i - 1) + h + 1)
                af(sq[:, h], xn[:, :, h * T:(h + 1) * T], ACT.Square).then_inc(squared, 1)

            def norm_rstd(i):
                nc.scalar.preload_act_table_set("natural_log_exp_and_others")
                for h in range(HALVES):
                    act.wait_ge(var_full, HALVES * i + h + 1)
                    if not isinstance(i, int) or i > 0:
                        act.wait_ge(normed, HALVES * i)
                    af(rstd[:, h * T:(h + 1) * T], ph[h][:], ACT.Ln, bias=eps_t[:, 0:1]).then_inc(ln_read, 1)
                for h in range(HALVES):
                    act.wait_ge(ln_read, HALVES * i + h + 1)
                    r = rstd[:, h * T:(h + 1) * T]
                    af(r, r, ACT.Exp, scale=-0.5).then_inc(rstd_done, 1)

            def up_bias(i, m):
                for h in range(HALVES):
                    act.wait_ge(up_full, HALVES * (MT * i + m) + h + 1)
                    if h == 0 and (not isinstance(i, int) or i > 0):
                        act.wait_ge(gelu_done, MT * (i - 1) + m + 1)
                        act.wait_ge(up_max, MT * (i - 1) + m + 1)
                    af(hid[:, m, h * T:(h + 1) * T], ph[h][:], ACT.Identity, bias=bias1[:, m:m + 1]).then_inc(up_read, 1)

            def gelu(i, k):
                if k == 0:
                    act.wait_ge(gain_done[0], i + 1)
                if k >= 2 or not isinstance(i, int) or i > 0:
                    act.wait_ge(g_lo, MT * i + k - 1)
                af(g[:, k % 2], hid[:, k], ACT.Gelu, scale=gain[0][:]).then_inc(gelu_done, 1)

            def down_bias(i):
                act.wait_ge(down_full, MT * (i + 1))
                if not isinstance(i, int) or i > 0:
                    act.wait_ge(stored, 16 * i)
                for m in range(CT):
                    for h in range(HALVES):
                        af(y2[:, m, h * T:(h + 1) * T], acc[HALVES * m + h][:], ACT.Identity,
                           bias=bias2[:, m:m + 1]).then_inc(down_read, 1)

            def image(i, more, more2):
                for k in range(MT):
                    gelu(i, k)
                    if more and k == 1:
                        norm_rstd(i + 1)
                    if more and k >= BEHIND + 1:
                        up_bias(i + 1, k - BEHIND - 1)
                if more:
                    up_bias(i + 1, MT - BEHIND - 1)
                down_bias(i)
                if more:
                    for m in range(MT - BEHIND, MT):
                        up_bias(i + 1, m)
                        if more2 and m >= MT - 2:
                            norm_square(i + 2, m - (MT - 2))

            def sign(j, w, raw, n, q):
                size = n // GROUPS
                last = af(w[:, :, q * size:(q + 1) * size], raw[:, :, q * size:(q + 1) * size], ACT.Sign,
                          bias=wmean[:, j, q:q + 1])
                if q == GROUPS - 1:
                    last.then_inc(signed, 1)

            norm_square(0, 0)
            norm_square(0, 1)
            norm_rstd(0)
            act.wait_ge(means_done, 1)
            for q in range(GROUPS):
                sign(0, w1, raw1, HID, q)
            act.wait_ge(signed, 1)
            act.wait_ge(bias_in, 32)
            for m in range(MT):
                if m == 3:
                    act.wait_ge(means_done, 2)
                    for q in range(GROUPS):
                        sign(1, w2, raw2, DM, q)
                if m == MT // 2:
                    act.wait_ge(signed, 2)
                up_bias(0, m)
                if m >= MT - 2:
                    norm_square(1, m - (MT - 2))
            image(0, True, True)
            with act.Fori(1, FFN_B - 2) as i:
                image(i, True, True)
            image(FFN_B - 2, True, False)
            image(FFN_B - 1, False, False)

        @block.vector
        def _(dve):
            v = nc.vector

            def norm_center(i, h):
                dve.wait_ge(mean_full, HALVES * i + h + 1)
                dve.wait_ge(x_loaded, 16 * (i + 1))
                x = xn[:, :, h * T:(h + 1) * T]
                v.tensor_tensor(x, x, ph[h][:].unsqueeze(1).broadcast_to([P, CT, T]), ALU.subtract).then_inc(centered, 1)

            def norm_scale(i, h):
                dve.wait_ge(rstd_done, HALVES * i + h + 1)
                s = slice(h * T, (h + 1) * T)
                v.tensor_tensor(xn[:, :, s], xn[:, :, s], rstd[:, s].unsqueeze(1).broadcast_to([P, CT, T]),
                                ALU.mult).then_inc(normed, 1)
                dve.wait_ge(normed, HALVES * i + h + 1)
                if not isinstance(i, int) or i > 0:
                    dve.wait_ge(up_full, HALVES * MT * i)
                v.tensor_copy(xh[:, :, s], xn[:, :, s]).then_inc(split_hi, 1)
                dve.wait_ge(split_hi, HALVES * i + h + 1)
                v.tensor_tensor(xl[:, :, s], xn[:, :, s], xh[:, :, s], ALU.subtract).then_inc(split_lo, 1)

            def up_largest(i, m):
                dve.wait_ge(up_read, HALVES * (MT * i + m + 1))
                v.tensor_reduce(big[:, 0, m:m + 1], hid[:, m], AX.X, ALU.max, apply_absolute_value=True).then_inc(up_max, 1)

            def gelu_split(i, k):
                dve.wait_ge(gelu_done, MT * i + k + 1)
                if k >= 3 or not isinstance(i, int) or i > 0:
                    dve.wait_ge(down_full, MT * i + k - 2)
                v.tensor_scalar(gh[:, k % 3], g[:, k % 2], Q_CLIP, -Q_CLIP, ALU.min, ALU.max).then_inc(g_hi, 1)
                dve.wait_ge(g_hi, MT * i + k + 1)
                v.scalar_tensor_tensor(gl[:, k % 3], g[:, k % 2], Q_CLIP, gh[:, k % 3], ALU.min, ALU.subtract).then_inc(g_lo, 1)

            def top_of_tiles(i, j, n, done, total):
                dve.wait_ge(done, total)
                v.tensor_reduce(top[:, j:j + 1], big[:, j, 0:n], AX.X, ALU.max).then_inc(top_col[j], 1)

            def make_gain(i, j):
                dve.wait_ge(top_row[j], i + 1)
                v.tensor_reduce(top1[0:1, j:j + 1], acc[2 * j][0:1, 0:P], AX.X, ALU.max).then_inc(top_one[j], 1)
                dve.wait_ge(top_all[j], i + 1)
                v.tensor_scalar(gain[j][:], acc[2 * j + 1][:, 0:1], Q_EPS, 1.0 / Q_BOUND, ALU.add, ALU.mult).then_inc(top_eps[j], 1)
                dve.wait_ge(top_eps[j], i + 1)
                v.reciprocal(gain[j][:], gain[j][:]).then_inc(gain_done[j], 1)

            def result_largest(i):
                dve.wait_ge(down_read, CT * HALVES * (i + 1))
                v.tensor_reduce(big[:, 1, 0:CT], y2[:], AX.X, ALU.max, apply_absolute_value=True).then_inc(down_max, 1)
                top_of_tiles(i, 1, CT, down_max, i + 1)

            def quantise(i):
                dve.wait_ge(gain_done[1], i + 1)
                v.tensor_scalar(y2[:], y2[:], gain[1][:], Q_CLIP, ALU.mult, ALU.min).then_inc(quant, 1)

            def add_residual(i):
                dve.wait_ge(quant, i + 1)
                dve.wait_ge(xres_loaded, 16 * (i + 1))
                v.scalar_tensor_tensor(y2[:].rearrange("p t s -> p (t s)"), y2[:].rearrange("p t s -> p (t s)"), -Q_CLIP,
                                       xres[:].rearrange("p t s -> p (t s)"), ALU.max, ALU.add).then_inc(added, 1)

            def image(i, more, more2, before):
                top_of_tiles(i, 0, MT, up_max, MT * (i + 1))
                make_gain(i, 0)
                for k in range(MT):
                    gelu_split(i, k)
                    if more and k in (1, 2):
                        norm_scale(i + 1, k - 1)
                    if before and k == BEHIND + 1:
                        quantise(i - 1)
                    if before and k == BEHIND + 2:
                        add_residual(i - 1)
                    if more and k >= BEHIND + 2:
                        up_largest(i + 1, k - BEHIND - 2)
                if more:
                    for m in range(MT - BEHIND - 2, MT):
                        up_largest(i + 1, m)
                        if m == MEAN_BEFORE - 2:
                            result_largest(i)
                        if more2 and m == MEAN_BEFORE - 1:
                            norm_center(i + 2, 0)
                            norm_center(i + 2, 1)
                        if m == MT - 2:
                            make_gain(i, 1)
                else:
                    result_largest(i)
                    make_gain(i, 1)

            norm_center(0, 0)
            norm_center(0, 1)

            def group_sums(j, raw, n):
                size = n // GROUPS
                for q in range(GROUPS):
                    v.tensor_reduce(wsum[:, j, q:q + 1], raw[:, :, q * size:(q + 1) * size], AX.XY, ALU.add).then_inc(summed, 1)

            dve.wait_ge(w1_in, 16)
            group_sums(0, raw1, HID)
            v.memset(w1[:, :, GROUPS * (HID // GROUPS):].bitcast(F32), 0.0)
            v.memset(w2[:, :, GROUPS * (DM // GROUPS):].bitcast(F32), 0.0)
            norm_scale(0, 0)
            norm_scale(0, 1)
            dve.wait_ge(sums_full, 1)
            v.tensor_scalar(wmean[:, 0], acc[0][:, 0:GROUPS], -1.0 / (HID // GROUPS * DM), None, ALU.mult).then_inc(means_done, 1)
            dve.wait_ge(w2_in, 16)
            group_sums(1, raw2, DM)
            dve.wait_ge(sums_full, 2)
            v.tensor_scalar(wmean[:, 1], acc[2][:, 0:GROUPS], -1.0 / (DM // GROUPS * HID), None, ALU.mult).then_inc(means_done, 1)
            for m in range(MT):
                up_largest(0, m)
                if m == MEAN_BEFORE - 1:
                    norm_center(1, 0)
                    norm_center(1, 1)
            image(0, True, True, False)
            with dve.Fori(1, FFN_B - 2) as i:
                image(i, True, True, True)
            image(FFN_B - 2, True, False, True)
            image(FFN_B - 1, False, False, True)
            quantise(FFN_B - 1)
            add_residual(FFN_B - 1)

        @block.gpsimd
        def _(pool):
            nc.gpsimd.memset(ident[:], 0.0).then_inc(const_step, 1)
            nc.gpsimd.memset(ones[:], 1.0)
            nc.gpsimd.memset(mean_w[:], 1.0 / DM)
            nc.gpsimd.memset(eps_t[:], 1e-5)
            pool.wait_ge(const_step, 1)
            nc.gpsimd.affine_select(out=ident[:], in_=ident[:], compare_op=ALU.not_equal, fill=1.0, base=0,
                                    pattern=[[-1, P]], channel_multiplier=1).then_inc(consts, 1)


NPOS = 48
CPP = DM // NPOS
SIDE = 32
SIDES = P // SIDE
PPG = SIDE // CPP
MAGIC = 1.5 * 2.0 ** 23
NMAT = 2 * CT * PPG


def displace(nc, signals, x_in, x_mid, x_out, offset):
    with ExitStack() as ctx:
        def sb(name, shape, dt=F32):
            return ctx.enter_context(nc.sbuf_tensor(name + "_d", shape, dt))

        def sem(name):
            return ctx.enter_context(nc.semaphore(name + "_d"))

        def bank(name):
            return ctx.enter_context(nc.psum_tensor(name + "_d", [P, T], F32))

        lag_i = sb("lag_i", [P, P], mybir.dt.int32)
        lag = sb("lag", [P, P])
        diag = sb("diag", [P, P])
        off = sb("off", [P, NMAT])
        whole = sb("whole", [P, NMAT])
        part = sb("part", [P, NMAT])
        scale = sb("scale", [P, NMAT])
        tmp = sb("tmp", [P, 4, NMAT])
        tap = sb("tap", [P, 5, NMAT])
        mats = sb("mats", [P, NMAT, P])
        work = sb("work", [P, NMAT, P])
        mean_w = sb("mean_w", [P, P])
        eps_c = sb("eps_c", [P, 1])
        xn = sb("xn", [P, CT, HW])
        sq = sb("sq", [P, CT, T])
        rstd = sb("rstd", [P, HW])
        xres = sb("xres", [P, CT, HW])
        res = sb("res", [P, CT, HW])
        ta = sb("ta", [P, CT, HW])
        tb = sb("tb", [P, CT, HW])
        tc = sb("tc", [P, CT, HW])
        td = sb("td", [P, CT, HW])
        te = sb("te", [P, CT, HW])
        pc = [bank(f"pc{j}") for j in range(2 * CT)]
        ph = [bank(f"ph{j}") for j in range(HALVES)]

        off_in, iotas, made, lag_done = sem("off_in"), sem("iotas"), sem("made"), sem("lag_done")
        step, tapped, gauss, mats_done = sem("step"), sem("tapped"), sem("gauss"), sem("mats_done")
        x_loaded, xres_loaded = sem("x_loaded"), sem("xres_loaded")
        stored = sem("stored")
        mean_full, centered, squared, var_full = sem("mean_full"), sem("centered"), sem("squared"), sem("var_full")
        ln_read, rstd_done, normed, ta_done = sem("ln_read"), sem("rstd_done"), sem("normed"), sem("ta_done")
        x_full, x_read, tc_done = sem("x_full"), sem("x_read"), sem("tc_done")
        y_full, y_read, te_done, added = sem("y_full"), sem("y_read"), sem("te_done"), sem("added")
        block = ctx.enter_context(nc.Block())
        XIN = x_in.rearrange("b (t p) s -> b p t s", p=P)
        MID = x_mid.rearrange("b (t p) s -> b p t s", p=P)
        OUT = x_out.rearrange("b (t p) s -> b p t s", p=P)

        @block.sync
        def _(sp):
            for g in range(SIDES):
                for a in range(2):
                    for t in range(CT):
                        src = offset[(t * SIDES + g) * PPG:(t * SIDES + g + 1) * PPG, a]
                        j = (a * CT + t) * PPG
                        sp.dma_start(off[g * SIDE:(g + 1) * SIDE, j:j + PPG], src.partition_broadcast(SIDE),
                                     allow_slow_non_contiguous=True).then_inc(off_in, 16)
            sp.dma_start(xn[:], XIN[0]).then_inc(x_loaded, 16)

            def image(i, out, more):
                if not isinstance(i, int) or i > 0:
                    sp.wait_ge(added, i)
                sp.dma_start(xres[:], XIN[i]).then_inc(xres_loaded, 16)
                if more:
                    sp.wait_ge(ta_done, CT * (i + 1))
                    sp.dma_start(xn[:], XIN[i + 1]).then_inc(x_loaded, 16)
                sp.wait_ge(added, i + 1)
                sp.dma_start(out[i], res[:]).then_inc(stored, 16)

            image(0, MID, True)
            with sp.Fori(1, FFN_B) as i:
                image(i, MID, True)
            with sp.Fori(FFN_B, B - 1) as i:
                image(i, OUT, True)
            image(B - 1, OUT, False)
            sp.wait_ge(stored, 16 * B)

        @block.tensor
        def _(pe):
            mm = nc.tensor.matmul

            def norm_mean(i):
                pe.wait_ge(x_loaded, 16 * (i + 1))
                if not isinstance(i, int) or i > 0:
                    pe.wait_ge(ln_read, HALVES * i)
                for h in range(HALVES):
                    for t in range(CT):
                        last = mm(ph[h][:], mean_w[:], xn[:, t, h * T:(h + 1) * T], start=t == 0, stop=t == CT - 1)
                    last.then_inc(mean_full, 1)

            def norm_var(i):
                for h in range(HALVES):
                    pe.wait_ge(squared, HALVES * i + h + 1)
                    for t in range(CT):
                        last = mm(ph[h][:], mean_w[:], sq[:, t], start=t == 0, stop=t == CT - 1)
                    last.then_inc(var_full, 1)

            def axis(i, a, src, ready, full):
                for t in range(CT):
                    pe.wait_ge(ready, CT * i + t + 1)
                    if a == 1:
                        pe.wait_ge(x_read, 2 * CT * i + 2 * t + 2)
                    elif not isinstance(i, int) or i > 0:
                        pe.wait_ge(y_read, 2 * CT * (i - 1) + 2 * t + 2)
                    for q in range(PPG):
                        if a == 0:
                            x = src[:, t].rearrange("p (y c) -> p y c", c=SIDE)[:, :, q * CPP:(q + 1) * CPP]
                        else:
                            x = src[:, t, q * CPP * SIDE:(q + 1) * CPP * SIDE]
                        o = pc[2 * t + q // 2][:, (q % 2) * 256:(q % 2 + 1) * 256]
                        last = mm(o, mats[:, (a * CT + t) * PPG + q], x, start=True, stop=True)
                        if q % 2:
                            last.then_inc(full, 1)

            def image(i, more):
                axis(i, 0, ta, ta_done, x_full)
                if more:
                    norm_mean(i + 1)
                axis(i, 1, tc, tc_done, y_full)
                if more:
                    norm_var(i + 1)

            pe.wait_ge(made, 1)
            norm_mean(0)
            norm_var(0)
            pe.wait_ge(mats_done, 1)
            image(0, True)
            with pe.Fori(1, B - 1) as i:
                image(i, True)
            image(B - 1, False)

        @block.scalar
        def _(act):
            af = nc.scalar.activation

            def norm_square(i):
                for h in range(HALVES):
                    act.wait_ge(centered, HALVES * i + h + 1)
                    if h > 0 or not isinstance(i, int) or i > 0:
                        act.wait_ge(var_full, HALVES * i + h)
                    af(sq[:], xn[:, :, h * T:(h + 1) * T], ACT.Square).then_inc(squared, 1)

            def norm_rstd(i):
                for h in range(HALVES):
                    act.wait_ge(var_full, HALVES * i + h + 1)
                    if not isinstance(i, int) or i > 0:
                        act.wait_ge(normed, HALVES * i)
                    af(rstd[:, h * T:(h + 1) * T], ph[h][:], ACT.Ln, bias=eps_c[:, 0:1]).then_inc(ln_read, 1)
                for h in range(HALVES):
                    act.wait_ge(ln_read, HALVES * i + h + 1)
                    r = rstd[:, h * T:(h + 1) * T]
                    af(r, r, ACT.Exp, scale=-0.5).then_inc(rstd_done, 1)

            def read_x(i):
                for t in range(CT):
                    for j in range(2):
                        act.wait_ge(x_full, 2 * (CT * i + t) + j + 1)
                        if not isinstance(i, int) or i > 0:
                            act.wait_ge(tc_done, CT * (i - 1) + t + 1)
                        o = tb[:, t, j * T:(j + 1) * T].rearrange("p (q c y) -> p q y c", q=2, y=SIDE)
                        for q in range(2):
                            last = af(o[:, q], pc[2 * t + j][:, q * 256:(q + 1) * 256].rearrange("p (y c) -> p y c", c=CPP), ACT.Copy)
                        last.then_inc(x_read, 1)

            def read_y(i):
                for t in range(CT):
                    for j in range(2):
                        act.wait_ge(y_full, 2 * (CT * i + t) + j + 1)
                        if not isinstance(i, int) or i > 0:
                            act.wait_ge(te_done, CT * (i - 1) + t + 1)
                        o = td[:, t].rearrange("p (x c) -> p c x", c=SIDE)[:, j * 16:(j + 1) * 16, :]
                        af(o, pc[2 * t + j][:].rearrange("p (c x) -> p c x", x=SIDE), ACT.Copy).then_inc(y_read, 1)

            def image(i, more):
                read_x(i)
                if more:
                    norm_square(i + 1)
                read_y(i)
                if more:
                    norm_rstd(i + 1)

            nc.scalar.preload_act_table_set("natural_log_exp_and_others")
            act.wait_ge(tapped, 1)
            af(tap[:], tap[:], ACT.Exp, scale=-2.0).then_inc(gauss, 1)
            act.wait_ge(tapped, 2)
            af(mats[:], mats[:], ACT.Exp, scale=-2.0).then_inc(gauss, 1)
            norm_square(0)
            norm_rstd(0)
            image(0, True)
            with act.Fori(1, B - 1) as i:
                image(i, True)
            image(B - 1, False)

        @block.vector
        def _(dve):
            v = nc.vector
            chain = [0]

            def then(instruction):
                chain[0] += 1
                instruction.then_inc(step, 1)
                dve.wait_ge(step, chain[0])

            def over_j(a):
                return a.unsqueeze(1).broadcast_to([P, NMAT, P])

            def over_o(a):
                return a.unsqueeze(2).broadcast_to([P, NMAT, P])

            dve.wait_ge(off_in, 16 * 2 * CT * SIDES)
            dve.wait_ge(made, 1)
            then(v.tensor_copy(lag[:], lag_i[:]))
            then(v.tensor_scalar(whole[:], off[:], MAGIC, None, ALU.add))
            then(v.tensor_scalar(whole[:], whole[:], MAGIC, None, ALU.subtract))
            then(v.tensor_tensor(part[:], off[:], whole[:], ALU.subtract))
            for j in range(5):
                then(v.tensor_scalar(tap[:, j], part[:], float(j - 2), None, ALU.add))
            dve.wait_ge(step, chain[0])
            v.tensor_tensor(tap[:], tap[:], tap[:], ALU.mult).then_inc(tapped, 1)
            then(v.tensor_tensor(work[:], over_j(lag[:]), over_o(whole[:]), ALU.add))
            then(v.tensor_tensor(mats[:], work[:], over_o(part[:]), ALU.add))
            v.tensor_tensor(mats[:], mats[:], mats[:], ALU.mult).then_inc(tapped, 1)
            then(v.tensor_tensor(work[:], work[:], work[:], ALU.mult))
            then(v.tensor_scalar(tmp[:, 0], whole[:], lag[:, 0:1], None, ALU.add))
            then(v.tensor_scalar(tmp[:, 1], tmp[:, 0], 0.0, None, ALU.is_ge))
            then(v.scalar_tensor_tensor(tmp[:, 2], tmp[:, 0], float(SIDE - 1), tmp[:, 1], ALU.is_le, ALU.mult))
            dve.wait_ge(gauss, 1)
            then(v.tensor_tensor(tmp[:, 3], tap[:, 0], tap[:, 1], ALU.add))
            for j in range(2, 5):
                then(v.tensor_tensor(tmp[:, 3], tmp[:, 3], tap[:, j], ALU.add))
            then(v.reciprocal(tmp[:, 3], tmp[:, 3]))
            then(v.tensor_tensor(scale[:], tmp[:, 2], tmp[:, 3], ALU.mult))
            dve.wait_ge(gauss, 2)
            flat = "p j o -> p (j o)"
            then(v.scalar_tensor_tensor(mats[:].rearrange(flat), work[:].rearrange(flat), 4.5, mats[:].rearrange(flat),
                                        ALU.is_le, ALU.mult))
            then(v.tensor_tensor(mats[:], mats[:], over_o(scale[:]), ALU.mult))
            v.tensor_tensor(mats[:], mats[:], over_j(diag[:]), ALU.mult).then_inc(mats_done, 1)

            def norm_center(i):
                dve.wait_ge(x_loaded, 16 * (i + 1))
                for h in range(HALVES):
                    dve.wait_ge(mean_full, HALVES * i + h + 1)
                    x = xn[:, :, h * T:(h + 1) * T]
                    v.tensor_tensor(x, x, ph[h][:].unsqueeze(1).broadcast_to([P, CT, T]), ALU.subtract).then_inc(centered, 1)

            def norm_scale(i):
                for h in range(HALVES):
                    dve.wait_ge(rstd_done, HALVES * i + h + 1)
                    s = slice(h * T, (h + 1) * T)
                    v.tensor_tensor(xn[:, :, s], xn[:, :, s], rstd[:, s].unsqueeze(1).broadcast_to([P, CT, T]),
                                    ALU.mult).then_inc(normed, 1)
                dve.wait_ge(normed, HALVES * (i + 1))
                for t in range(CT):
                    if not isinstance(i, int) or i > 0:
                        dve.wait_ge(x_full, 2 * (CT * (i - 1) + t) + 2)
                    v.transpose(ta[:, t], xn[:, t]).then_inc(ta_done, 1)

            def to_y(i):
                for t in range(CT):
                    dve.wait_ge(x_read, 2 * (CT * i + t) + 2)
                    if not isinstance(i, int) or i > 0:
                        dve.wait_ge(y_full, 2 * (CT * (i - 1) + t) + 2)
                    v.transpose(tc[:, t], tb[:, t]).then_inc(tc_done, 1)

            def finish(i):
                for t in range(CT):
                    dve.wait_ge(y_read, 2 * (CT * i + t) + 2)
                    if not isinstance(i, int) or i > 0:
                        dve.wait_ge(added, i)
                    v.transpose(te[:, t], td[:, t]).then_inc(te_done, 1)
                dve.wait_ge(te_done, CT * (i + 1))
                dve.wait_ge(xres_loaded, 16 * (i + 1))
                if not isinstance(i, int) or i > 0:
                    dve.wait_ge(stored, 16 * i)
                for t in range(CT):
                    last = v.tensor_tensor(res[:, t].rearrange("p (y x) -> p y x", x=SIDE),
                                           te[:, t].rearrange("p (x y) -> p y x", y=SIDE),
                                           xres[:, t].rearrange("p (y x) -> p y x", x=SIDE), ALU.add)
                last.then_inc(added, 1)

            def image(i, more):
                to_y(i)
                if more:
                    norm_center(i + 1)
                finish(i)
                if more:
                    norm_scale(i + 1)

            norm_center(0)
            norm_scale(0)
            image(0, True)
            with dve.Fori(1, B - 1) as i:
                image(i, True)
            image(B - 1, False)

        @block.gpsimd
        def _(pool):
            for s in signals.values():
                nc.gpsimd.sem_clear(s)
            nc.gpsimd.memset(mean_w[:], 1.0 / DM)
            nc.gpsimd.memset(eps_c[:], 1e-6)
            nc.gpsimd.memset(diag[:], 0.0).then_inc(iotas, 1)
            for g in range(SIDES):
                pool.wait_ge(iotas, 2 * g + 1)
                nc.gpsimd.iota(lag_i[g * SIDE:(g + 1) * SIDE, :], pattern=[[0, SIDES], [-1, SIDE]], base=0,
                               channel_multiplier=1).then_inc(iotas, 1)
                pool.wait_ge(iotas, 2 * g + 2)
                nc.gpsimd.memset(diag[g * SIDE:(g + 1) * SIDE, g * SIDE:(g + 1) * SIDE], 1.0).then_inc(iotas, 1)
            pool.wait_ge(iotas, 2 * SIDES + 1)
            nc.gpsimd.sem_inc(made, 1)


def program(nc, x, in_wT, conv_w, conv_b, xp_wT, dt_wT, dt_b, A_log, D, out_wT, W1T_0, b1_0, W2T_0, b2_0,
            offset, W1T_1, b1_1, W2T_1, b2_1, out):
    between = nc.dram_tensor("between_layers", (B, DM, HW), F32).ap()
    mixer(nc, x, between, in_wT, conv_w, conv_b, xp_wT, dt_wT, dt_b, A_log, D, out_wT)
    signals = {}
    ffn(nc, 0, signals, between, between, W1T_0, b1_0, W2T_0, b2_0)
    displace(nc, signals, between, between, out, offset)
    ffn(nc, 1, signals, between, out, W1T_1, b1_1, W2T_1, b2_1)


def kernel(**inputs):
    import numpy as np
    import concourse.bacc as bacc
    from concourse.bass_utils import run_bass_kernel_spmd

    a = {n: np.asarray(v) for n, v in inputs.items()}
    c0 = "L0_conv_"
    arrays = {
        "x": a["x"].reshape(B, DM, HW),
        "in_wT": a[c0 + "in_proj_w"].T, "conv_w": a[c0 + "conv_w"], "conv_b": a[c0 + "conv_b"],
        "xp_wT": a[c0 + "x_proj_w"].T, "dt_wT": a[c0 + "dt_proj_w"].T, "dt_b": a[c0 + "dt_proj_b"],
        "A_log": a[c0 + "A_log"], "D": a[c0 + "D"], "out_wT": a[c0 + "out_proj_w"].T,
        "W1T_0": a["L0_ffn_W1"].T, "b1_0": a["L0_ffn_b1"], "W2T_0": a["L0_ffn_W2"].T, "b2_0": a["L0_ffn_b2"],
        "offset": a["L1_conv_offset"],
        "W1T_1": a["L1_ffn_W1"].T, "b1_1": a["L1_ffn_b1"], "W2T_1": a["L1_ffn_W2"].T, "b2_1": a["L1_ffn_b2"],
    }
    arrays = {f"in_{n}": np.ascontiguousarray(v) for n, v in arrays.items()}
    nc = bacc.Bacc("TRN2", target_bir_lowering=False, num_devices=1)
    args = [nc.dram_tensor(n, v.shape, mybir.dt.from_np(v.dtype), kind="ExternalInput").ap() for n, v in arrays.items()]
    out = nc.dram_tensor("out_dram", (B, DM, HW), F32, kind="ExternalOutput").ap()
    program(nc, *args, out)
    r = run_bass_kernel_spmd(nc, [arrays], core_ids=[0])
    return r.results[0]["out_dram"].reshape(a["x"].shape)
```

```python
import concourse.bass as bass
from concourse import mybir
from contextlib import ExitStack

F32 = mybir.dt.float32
BF16 = mybir.dt.bfloat16
F32R = mybir.dt.float32r
ALU = mybir.AluOpType
ACT = mybir.ActivationFunctionType
AX = mybir.AxisListType

P = 128
B, DM, HW = 8, 384, 1024
CT = DM // P
DI = 2 * DM
KT = DI // P
NS = 16
DTR = (DM + 15) // 16
T = 512
NCHUNK = B * HW // T
STEPS = KT * NS
BC = 2 * NS
DTH, DTL = 64, 96
ROWS = DTL + DTR

SLOTS = 8

PP, PZ, PB = 0, 1, 2
OUT_AT, OUT_IN = (0, 7, 13), (PP, PZ, PP)
GATE_AT, GATE_IN = (20, 26, 34, 59, 70, 81), (PB, PP, PP, PZ, PP, PP)
LAST_OUT_AT, LAST_OUT_IN = (88, 88, 93), (PZ, PB, PP)
MEAN_AT, VAR_AT = 23, 29
IN_AT, IN_IN = (41, 44, 49, 51, 56, 58), (PZ, PB, PP, PZ, PB, PP)
SUM_AT = (10, 12)
XP_AT = 65
DT_AT, DT_IN = (73, 74, 77, 79, 33, 40), (PZ, PB, PZ, PP, PB, PB)
EARLY = 4
FIRST_ROWS = 5
SPREAD_AT = 86
GATE_Y_AT = (36, 43, 58, 74, 90, 8)
DT_ADD_AT = (83, 84, 85, 90, 46, 49)
LAG = 5
SPREAD_LAG = 5
CONV_LAG = 4
READ_Y_AT = 5
DT_U_AT = 10


def mixer(nc, x, x1, in_wT, conv_w, conv_b, xp_wT, dt_wT, dt_b, A_log, D, out_wT):
    with ExitStack() as ctx:
        def sb(name, shape, dt=F32):
            return ctx.enter_context(nc.sbuf_tensor(name, shape, dt))

        def bank(name):
            return ctx.enter_context(nc.psum_tensor(name, [P, T], F32))

        def sem(name):
            return ctx.enter_context(nc.semaphore(name))

        w_in = sb("w_in", [P, CT, 2 * DI])
        w_out = sb("w_out", [P, KT, DM])
        w_x = sb("w_x", [P, KT, ROWS])
        w_dt_hi = sb("w_dt_hi", [P, DI], F32R)
        w_dt_lo = sb("w_dt_lo", [P, DI], F32R)
        cw = sb("cw", [P, KT, 3])
        cb = sb("cb", [P, KT])
        dtb = sb("dtb", [P, KT])
        dskip = sb("dskip", [P, KT])
        aneg = sb("aneg", [P, KT, NS])
        ident = sb("ident", [P, P])
        mean_w = sb("mean_w", [P, P])
        sel = sb("sel", [P, BC], F32R)
        sel_f = sb("sel_f", [P, BC])
        eps_c = sb("eps_c", [P, 1])
        zeros2 = sb("zeros2", [P, 2])
        xn = sb("xn", [P, 2, CT, T])
        xres = sb("xres", [P, CT, T])
        sq = sb("sq", [P, CT, T])
        xsum = sb("xsum", [P, T])
        rstd = sb("rstd", [P, T])
        xin = sb("xin", [P, 2, T + 2])
        halo = sb("halo", [P, KT, 2])
        acc = sb("acc", [P, 2, T])
        th = sb("th", [P, 2, T])
        u = sb("u", [P, 2, KT, T])
        parts = sb("parts", [P, T], F32R)
        w_dt_raw = u[:, 1].rearrange("p k t -> p (k t)")[:, 0:DI]
        rl = th
        sl = acc
        dt = sb("dt", [P, KT, T])
        dtu = sb("dtu", [P, 2, T])
        b_rep = sb("b_rep", [P, NS, T])
        c_rep = sb("c_rep", [P, NS, T])
        slot = sb("slot", [P, SLOTS, T + 2])
        carry = sb("carry", [P, STEPS])
        gate = sb("gate", [P, 2, T])
        yy = sb("yy", [P, T])

        da = [bank("da0"), bank("da1"), bank("da2")]
        ys = [bank("ys0"), bank("ys1")]
        pg = [bank("pp"), bank("pz"), bank("pb")]
        pp, pz, pb = pg

        in_w_in, params_in, x_w_in, dt_w_in = sem("in_w_in"), sem("params_in"), sem("x_w_in"), sem("dt_w_in")
        w_dt_set, dt_w_step = sem("w_dt_set"), sem("dt_w_step")
        out_w_in, gate_w_in, out_halved = sem("out_w_in"), sem("gate_w_in"), sem("out_halved")
        consts = sem("consts")
        const_step = sem("const_step")
        halved = sem("halved")
        a_exp = sem("a_exp")
        x_loaded = [sem("x_loaded0"), sem("x_loaded1")]
        xres_loaded, x_stored = sem("xres_loaded"), sem("x_stored")
        sum_step, x_summed = sem("sum_step"), sem("x_summed")
        mean_full, centered, squared, var_full = sem("mean_full"), sem("centered"), sem("squared"), sem("var_full")
        ln_read, rstd_done, normed = sem("ln_read"), sem("rstd_done"), sem("normed")
        in_full, in_read, conv_part, conv_done = sem("in_full"), sem("in_read"), sem("conv_part"), sem("conv_done")
        th_done, u_done = sem("th_done"), sem("u_done")
        xp_full, xp_read, split_step, bc_done = sem("xp_full"), sem("xp_read"), sem("split_step"), sem("bc_done")
        dt_full, dt_read, sp_exp, sp_done, dt_done = sem("dt_full"), sem("dt_read"), sem("sp_exp"), sem("sp_done"), sem("dt_done")
        bb_full, bb_copied = sem("bb_full"), sem("bb_copied")
        cc_full, cc_copied = sem("cc_full"), sem("cc_copied")
        dtu_done, dbu_done = sem("dtu_done"), sem("dbu_done")
        exp_done, scan_done, mult_done, red_done, carried = sem("exp_done"), sem("scan_done"), sem("mult_done"), sem("red_done"), sem("carried")
        z_full, z_tanh, z_read = sem("z_full"), sem("z_tanh"), sem("z_read")
        y_read, gated = sem("y_read"), sem("gated")
        out_full, res_done = sem("out_full"), sem("res_done")
        block = ctx.enter_context(nc.Block())

        assert CT == 3
        XV = x.rearrange("b (t p) s -> b p t s", p=P)
        X1V = x1.rearrange("b (t p) s -> b p t s", p=P)

        @block.sync
        def _(sp):
            sp.dma_start(xn[:, 0], XV[0, :, :, 0:T]).then_inc(x_loaded[0], 16)
            sp.dma_start(w_in[:, :, 0:DI], in_wT.rearrange("(t p) n -> p t n", p=P)[:, :, 0:DI]).then_inc(in_w_in, 16)
            for o, i in ((cw, conv_w), (aneg, A_log)):
                sp.dma_start(o[:], i.rearrange("(t p) j -> p t j", p=P)).then_inc(params_in, 16)
            for o, i in ((cb, conv_b), (dtb, dt_b), (dskip, D)):
                sp.dma_start(o[:], i.rearrange("(t p) -> p t", p=P), allow_slow_non_contiguous=True).then_inc(params_in, 16)
            xw = xp_wT.rearrange("(t p) n -> p t n", p=P)
            for r in (0, BC):
                sp.dma_start(w_x[:, :, r:r + BC], xw[:, :, DTR:]).then_inc(x_w_in, 16)
            for r in (DTH, DTL):
                sp.dma_start(w_x[:, :, r:r + DTR], xw[:, :, 0:DTR]).then_inc(x_w_in, 16)
                sp.dma_start(w_dt_raw[r:r + DTR, :], dt_wT).then_inc(dt_w_in, 16)
            sp.dma_start(w_out[:], out_wT.rearrange("(t p) n -> p t n", p=P)).then_inc(out_w_in, 16)
            sp.dma_start(w_in[:, :, DI:], in_wT.rearrange("(t p) n -> p t n", p=P)[:, :, DI:]).then_inc(gate_w_in, 16)

            def load(b, h):
                d = 2 * b + h
                if not isinstance(d, int) or d >= 2:
                    sp.wait_ge(z_full, KT * (d - 1))
                sp.dma_start(xn[:, h], XV[b, :, :, h * T:(h + 1) * T]).then_inc(x_loaded[h], 16)

            def store(b, h):
                c = 2 * b + h
                if not isinstance(c, int) or c > 0:
                    sp.wait_ge(x_stored, 16 * c)
                sp.dma_start(xres[:], XV[b, :, :, h * T:(h + 1) * T]).then_inc(xres_loaded, 16)
                sp.wait_ge(res_done, CT * (c + 1))
                sp.dma_start(X1V[b, :, :, h * T:(h + 1) * T], xres[:]).then_inc(x_stored, 16)

            load(0, 1)
            load(1, 0)
            store(0, 0)
            load(1, 1)
            store(0, 1)
            with sp.Fori(1, B - 1) as i:
                load(i + 1, 0)
                store(i, 0)
                load(i + 1, 1)
                store(i, 1)
            store(B - 1, 0)
            store(B - 1, 1)
            sp.wait_ge(x_stored, 16 * NCHUNK)

        @block.tensor
        def _(pe):
            mm = nc.tensor.matmul

            def norm_mean_first(t):
                if t == 0:
                    pe.wait_ge(x_loaded[0], 16)
                last = mm(pz[:], mean_w[:], xn[:, 0, t], start=t == 0, stop=t == CT - 1)
                if t == CT - 1:
                    last.then_inc(mean_full, 1)

            def norm_mean(d):
                pe.wait_ge(x_summed, d)
                if not isinstance(d, int) or d > 1:
                    pe.wait_ge(res_done, CT * (d - 2) + 2)
                else:
                    pe.wait_ge(dt_read, EARLY)
                mm(pz[:], mean_w[:], xsum[:], start=True, stop=True).then_inc(mean_full, 1)

            def norm_var(d, t):
                if t == 0:
                    pe.wait_ge(squared, d + 1)
                last = mm(pz[:], mean_w[:], sq[:, t], start=t == 0, stop=t == CT - 1)
                if t == CT - 1:
                    last.then_inc(var_full, 1)

            def in_proj(d, h, m, t):
                if t == 0 and m == 0:
                    pe.wait_ge(normed, d + 1)
                if t == 0 and m == 1 and (not isinstance(d, int) or d > 0):
                    pe.wait_ge(dt_read, KT * d)
                if t == 0 and m == 2 and (not isinstance(d, int) or d > 0):
                    pe.wait_ge(z_read, KT * (d - 1) + 3)
                if t == 0 and m >= 3:
                    pe.wait_ge(in_read, KT * d + m - 2)
                last = mm(pg[IN_IN[m]][:], w_in[:, t, m * P:(m + 1) * P], xn[:, h, t], start=t == 0, stop=t == CT - 1)
                if t == CT - 1:
                    last.then_inc(in_full, 1)

            def x_proj(d, h, k):
                if k == 0:
                    pe.wait_ge(in_read, KT * d + 5)
                pe.wait_ge(u_done, KT * d + k + 1)
                last = mm(pb[0:ROWS, :], w_x[:, k], u[:, h, k], start=k == 0, stop=k == KT - 1)
                if k == KT - 1:
                    last.then_inc(xp_full, 1)

            def dt_proj(d, m):
                if m == 0:
                    pe.wait_ge(bc_done, d + 1)
                    if not isinstance(d, int) or d > 0:
                        pe.wait_ge(z_read, KT * (d - 1) + 4)
                    else:
                        pe.wait_ge(in_read, KT)
                if m == 1:
                    pe.wait_ge(bc_done, d + 1)
                if m == 2:
                    pe.wait_ge(dt_read, KT * d + 1)
                if m == 3 and (not isinstance(d, int) or d > 0):
                    pe.wait_ge(z_read, KT * (d - 1) + 5)
                if m == 4:
                    pe.wait_ge(z_read, KT * d + 1)
                if m == 5:
                    pe.wait_ge(dt_read, KT * d + 5)
                mm(pg[DT_IN[m]][:], w_dt_hi[DTH:ROWS, m * P:(m + 1) * P], parts[DTH:ROWS, :], start=True, stop=False)
                mm(pg[DT_IN[m]][:], w_dt_lo[DTH:DTH + DTR, m * P:(m + 1) * P], parts[DTH:DTH + DTR, :],
                   start=False, stop=True).then_inc(dt_full, 1)

            def spread(d, n):
                if n == 0:
                    pe.wait_ge(bc_done, d + 1)
                    pe.wait_ge(dt_read, KT * d + 3)
                else:
                    pe.wait_ge(bb_copied, NS * d + n)
                mm(pb[:], sel[0:2 * BC, n:n + 1].broadcast_to([2 * BC, P]), parts[0:2 * BC, :], start=True,
                   stop=True).then_inc(bb_full, 1)
                if n > 0:
                    pe.wait_ge(cc_copied, NS * d + n)
                mm(pz[:], sel[0:2 * BC, NS + n:NS + n + 1].broadcast_to([2 * BC, P]), parts[0:2 * BC, :], start=True,
                   stop=True).then_inc(cc_full, 1)

            def gate_proj(c, h, k, t):
                if t == 0 and k == 0:
                    pe.wait_ge(bb_copied, NS * (c + 1))
                if t == 0 and k == 1:
                    if not isinstance(c, int) or c > 0:
                        pe.wait_ge(res_done, CT * c)
                    else:
                        pe.wait_ge(dt_read, EARLY)
                if t == 0 and k == 2:
                    pe.wait_ge(z_read, KT * c + 2)
                if t == 0 and k == 3:
                    if not isinstance(c, int) or c < NCHUNK - 1:
                        pe.wait_ge(in_read, KT * (c + 1) + 4)
                    else:
                        pe.wait_ge(res_done, CT * (c - 1) + 2)
                if t == 0 and k == 4:
                    if not isinstance(c, int) or c < NCHUNK - 1:
                        pe.wait_ge(in_read, KT * (c + 1) + 6)
                    else:
                        pe.wait_ge(z_read, KT * c + 3)
                if t == 0 and k == 5:
                    if not isinstance(c, int) or c < NCHUNK - 1:
                        pe.wait_ge(dt_read, KT * (c + 1) + 4)
                    else:
                        pe.wait_ge(z_read, KT * c + 5)
                last = mm(pg[GATE_IN[k]][:], w_in[:, t, DI + k * P:DI + (k + 1) * P], xn[:, h, t], start=t == 0, stop=t == CT - 1)
                if t == CT - 1:
                    last.then_inc(z_full, 1)

            def out_proj(c, h, m, k):
                if k == 0 and m == 0:
                    pe.wait_ge(out_halved, 1)
                    pe.wait_ge(gated, KT * c + KT - 1)
                    pe.wait_ge(z_read, KT * (c + 1))
                if k == KT - 1 and m == 0:
                    pe.wait_ge(gated, KT * (c + 1))
                if k == 0 and m == 1:
                    pe.wait_ge(cc_copied, NS * (c + 2))
                if k == 0 and m == 2:
                    pe.wait_ge(res_done, CT * c + 1)
                last = mm(pg[OUT_IN[m]][:], w_out[:, k, m * P:(m + 1) * P], u[:, h, k], start=k == 0, stop=k == KT - 1)
                if k == KT - 1:
                    last.then_inc(out_full, 1)

            def last_out_proj(m, k):
                c = NCHUNK - 1
                if k == 0:
                    pe.wait_ge(*((z_read, KT * c + 4), (dt_read, KT * NCHUNK), (z_read, KT * NCHUNK))[m])
                    pe.wait_ge(gated, KT * c + KT - 1)
                if k == KT - 1:
                    pe.wait_ge(gated, KT * NCHUNK)
                last = mm(pg[LAST_OUT_IN[m]][:], w_out[:, k, m * P:(m + 1) * P], u[:, 1, k], start=k == 0, stop=k == KT - 1)
                if k == KT - 1:
                    last.then_inc(out_full, 1)

            def reduce_state(c, k, n):
                s = STEPS * c + NS * k + n
                pe.wait_ge(mult_done, s + 1)
                if n == 0 and (not isinstance(c, int) or KT * c + k >= 2):
                    pe.wait_ge(y_read, KT * c + k - 1)
                mm(ys[k % 2][:], ident[:], slot[:, (NS * k + n) % SLOTS, 0:T], start=n == 0, stop=n == NS - 1).then_inc(red_done, 1)

            def scan(b, h, before, after):
                c = 2 * b + h
                d = c + 1
                for q in range(STEPS):
                    reduce_state(c, q // NS, q % NS)
                    if before and q < SPREAD_AT + NS - STEPS:
                        spread(c, q + STEPS - SPREAD_AT)
                    if not before and q < NS - FIRST_ROWS:
                        spread(c, q + FIRST_ROWS)
                    for m in range(CT):
                        if before and 0 <= q - OUT_AT[m] < KT:
                            out_proj(c - 1, 1 - h, m, q - OUT_AT[m])
                    for k in range(KT):
                        if 0 <= q - GATE_AT[k] < CT:
                            gate_proj(c, h, k, q - GATE_AT[k])
                        if after and 0 <= q - IN_AT[k] < CT:
                            in_proj(d, 1 - h, k, q - IN_AT[k])
                        if q == DT_AT[k] and (after or k >= EARLY):
                            dt_proj(d if k < EARLY else c, k)
                    if not after:
                        for m in range(CT):
                            for k in (range(2 * (q - LAST_OUT_AT[m]), 2 * (q - LAST_OUT_AT[m]) + 2)):
                                if 0 <= k < KT - 1:
                                    last_out_proj(m, k)
                    if after and q == MEAN_AT + CT - 1:
                        norm_mean(d)
                    if after and 0 <= q - VAR_AT < CT:
                        norm_var(d, q - VAR_AT)
                    if after and 0 <= q - XP_AT < KT:
                        x_proj(d, 1 - h, q - XP_AT)
                    if after and q >= SPREAD_AT:
                        spread(d, q - SPREAD_AT)

            pe.wait_ge(consts, 1)
            for t in range(CT):
                norm_mean_first(t)
            for t in range(CT):
                norm_var(0, t)
            pe.wait_ge(in_w_in, 16)
            for m in range(KT):
                for t in range(CT):
                    in_proj(0, 0, m, t)
            pe.wait_ge(x_w_in, 16 * 4)
            pe.wait_ge(w_dt_set, 1)
            for k in range(KT):
                x_proj(0, 0, k)
            for m in range(EARLY):
                dt_proj(0, m)
            for n in range(FIRST_ROWS):
                spread(0, n)
            pe.wait_ge(gate_w_in, 16)
            scan(0, 0, False, True)
            with pe.Fori(0, NCHUNK // 2 - 1) as i:
                scan(i, 1, True, True)
                scan(i + 1, 0, True, True)
            scan(B - 1, 1, True, False)
            for m in range(CT):
                last_out_proj(m, KT - 1)

        @block.scalar
        def _(act):
            af = nc.scalar.activation

            def norm_square(d, h):
                act.wait_ge(centered, d + 1)
                af(sq[:], xn[:, h], ACT.Square).then_inc(squared, 1)

            def norm_rstd(d):
                nc.scalar.preload_act_table_set("natural_log_exp_and_others")
                act.wait_ge(var_full, d + 1)
                if not isinstance(d, int) or d > 0:
                    act.wait_ge(normed, d)
                af(rstd[:], pz[:], ACT.Ln, bias=eps_c[:, 0:1]).then_inc(ln_read, 1)
                act.wait_ge(ln_read, d + 1)
                af(rstd[:], rstd[:], ACT.Exp, scale=-0.5).then_inc(rstd_done, 1)

            def conv_in(d, h, m):
                act.wait_ge(in_full, KT * d + m + 1)
                if not isinstance(d, int) or KT * d + m >= 2:
                    act.wait_ge(u_done, KT * d + m - 1)
                if m < 2 and (not isinstance(d, int) or d > 0):
                    act.wait_ge(dt_done, KT * d + m - 1)
                j = m % 2
                ps = pg[IN_IN[m]]
                af(xin[:, j, 2:], ps[:], ACT.Copy)
                af(xin[:, j, 0:2], halo[:, m] if h else zeros2[:], ACT.Copy)
                if h == 0:
                    af(halo[:, m], ps[:, T - 2:], ACT.Copy)
                af(acc[:, j], ps[:], ACT.Identity, bias=cb[:, m:m + 1], scale=cw[:, m, 2:3]).then_inc(in_read, 1)

            def conv_tanh(d, m):
                act.wait_ge(conv_done, KT * d + m + 1)
                if not isinstance(d, int) or KT * d + m >= 2:
                    act.wait_ge(u_done, KT * d + m - 1)
                af(th[:, m % 2], acc[:, m % 2], ACT.Tanh).then_inc(th_done, 1)

            def dt_read_tile(d, m):
                act.wait_ge(dt_full, KT * d + m + 1)
                if not isinstance(d, int) or KT * d + m >= 2:
                    act.wait_ge(dt_done, KT * d + m - 1)
                af(sl[:, m % 2], pg[DT_IN[m]][:], ACT.Abs, bias=dtb[:, m:m + 1])
                af(rl[:, m % 2], pg[DT_IN[m]][:], ACT.Relu, bias=dtb[:, m:m + 1]).then_inc(dt_read, 1)

            def softplus(d, m):
                act.wait_ge(dt_read, KT * d + m + 1)
                af(sl[:, m % 2], sl[:, m % 2], ACT.Exp, scale=-1.0).then_inc(sp_exp, 1)
                act.wait_ge(sp_exp, KT * d + m + 1)
                af(sl[:, m % 2], sl[:, m % 2], ACT.Ln, bias=1.0).then_inc(sp_done, 1)

            def spread_copy(d, n):
                act.wait_ge(bb_full, NS * d + n + 1)
                if not isinstance(d, int) or d > 0:
                    act.wait_ge(dbu_done, STEPS * (d - 1) + NS * (KT - 1) + n + 1)
                af(b_rep[:, n], pb[:], ACT.Copy).then_inc(bb_copied, 1)
                act.wait_ge(cc_full, NS * d + n + 1)
                if not isinstance(d, int) or d > 0:
                    act.wait_ge(mult_done, STEPS * (d - 1) + NS * (KT - 1) + n + 1)
                af(c_rep[:, n], pz[:], ACT.Copy).then_inc(cc_copied, 1)

            def gate_tanh(c, k):
                act.wait_ge(z_full, KT * c + k + 1)
                if not isinstance(c, int) or KT * c + k >= 2:
                    act.wait_ge(gated, KT * c + k - 1)
                af(gate[:, k % 2], pg[GATE_IN[k]][:], ACT.Tanh, scale=0.5).then_inc(z_tanh, 1)

            def decay(c, k, n):
                s = STEPS * c + NS * k + n
                if n == 0:
                    act.wait_ge(dt_done, KT * c + k + 1)
                if not isinstance(c, int) or s >= 3:
                    act.wait_ge(scan_done, s - 2)
                af(da[(NS * k + n) % 3][:], dt[:, k], ACT.Exp, scale=aneg[:, k, n:n + 1]).then_inc(exp_done, 1)

            def keep_state(b, q):
                act.wait_ge(scan_done, STEPS * 2 * b + q + 1)
                af(carry[:, q:q + 1], slot[:, q % SLOTS, T:T + 1], ACT.Copy).then_inc(carried, 1)

            def scan(b, h, before, after):
                c = 2 * b + h
                d = c + 1
                for q in range(STEPS):
                    decay(c, q // NS, q % NS)
                    if h == 0 and q >= 3:
                        keep_state(b, q - 3)
                    for k in range(KT):
                        if q == GATE_AT[k] + CT - 1 + LAG:
                            gate_tanh(c, k)
                        if after and q == IN_AT[k] + CT - 1 + LAG:
                            conv_in(d, 1 - h, k)
                        if after and q == IN_AT[k] + CT - 1 + LAG + CONV_LAG:
                            conv_tanh(d, k)
                        if q == DT_AT[k] + LAG and (after or k >= EARLY):
                            if k == 0:
                                nc.scalar.preload_act_table_set("natural_log_exp_and_others")
                            dt_read_tile(d if k < EARLY else c, k)
                            softplus(d if k < EARLY else c, k)
                    if after and q == MEAN_AT + CT - 1 + 4:
                        norm_square(d, 1 - h)
                    if after and q == VAR_AT + CT - 1 + LAG:
                        norm_rstd(d)
                    if not after and q == VAR_AT + CT - 1 + LAG:
                        nc.scalar.preload_act_table_set("natural_log_exp_and_others")
                    if not before and FIRST_ROWS <= q + 1 < NS:
                        spread_copy(c, q + 1)
                    if before and q < SPREAD_AT + SPREAD_LAG + NS - STEPS:
                        spread_copy(c, q + STEPS - SPREAD_AT - SPREAD_LAG)
                    if after and q >= SPREAD_AT + SPREAD_LAG:
                        spread_copy(d, q - SPREAD_AT - SPREAD_LAG)
                if h == 0:
                    for q in range(STEPS - 3, STEPS):
                        keep_state(b, q)

            act.wait_ge(consts, 1)
            norm_square(0, 0)
            norm_rstd(0)
            act.wait_ge(params_in, 16 * 5)
            af(aneg[:], aneg[:], ACT.Exp).then_inc(a_exp, 1)
            act.wait_ge(halved, 1)
            conv_in(0, 0, 0)
            for m in range(KT):
                if m + 1 < KT:
                    conv_in(0, 0, m + 1)
                conv_tanh(0, m)
            nc.scalar.preload_act_table_set("natural_log_exp_and_others")
            for m in range(EARLY):
                dt_read_tile(0, m)
                softplus(0, m)
            for n in range(FIRST_ROWS):
                spread_copy(0, n)
            scan(0, 0, False, True)
            with act.Fori(0, NCHUNK // 2 - 1) as i:
                scan(i, 1, True, True)
                scan(i + 1, 0, True, True)
            scan(B - 1, 1, True, False)

        @block.gpsimd
        def _(pool):
            tt = nc.gpsimd.tensor_tensor
            nc.gpsimd.memset(ident[:], 0.0)
            nc.gpsimd.memset(sel_f[:], 0.0).then_inc(const_step, 1)
            nc.gpsimd.memset(zeros2[:], 0.0)
            nc.gpsimd.memset(eps_c[:], 1e-6)
            nc.gpsimd.memset(mean_w[:], 1.0 / DM)
            pool.wait_ge(const_step, 1)
            nc.gpsimd.affine_select(out=ident[:], in_=ident[:], compare_op=ALU.not_equal, fill=1.0, base=0,
                                    pattern=[[-1, P]], channel_multiplier=1)
            for r in range(2):
                nc.gpsimd.affine_select(out=sel_f[:], in_=sel_f[:], compare_op=ALU.not_equal, fill=1.0,
                                               base=-BC * r, pattern=[[-1, BC]], channel_multiplier=1).then_inc(const_step, 1)
                pool.wait_ge(const_step, r + 2)
            nc.gpsimd.sem_inc(consts, 1)

            def dt_add(d, m):
                pool.wait_ge(sp_done, KT * d + m + 1)
                if not isinstance(d, int) or d > 0:
                    pool.wait_ge(exp_done, STEPS * (d - 1) + NS * (m + 1))
                tt(dt[:, m], rl[:, m % 2], sl[:, m % 2], ALU.add).then_inc(dt_done, 1)

            def dt_u(c, h, k):
                pool.wait_ge(dt_done, KT * c + k + 1)
                pool.wait_ge(u_done, KT * (c + 1))
                tt(dtu[:, k % 2], dt[:, k], u[:, h, k], ALU.mult).then_inc(dtu_done, 1)

            def drive(b, h, k, n):
                c = 2 * b + h
                q = NS * k + n
                s = STEPS * c + q
                if n == 0:
                    pool.wait_ge(dtu_done, KT * c + k + 1)
                if k == 0:
                    pool.wait_ge(bb_copied, NS * c + n + 1)
                if not isinstance(c, int) or s >= SLOTS:
                    pool.wait_ge(red_done, s - SLOTS + 1)
                if h == 0 and q >= SLOTS:
                    pool.wait_ge(carried, STEPS * b + q - SLOTS + 1)
                if h == 1 and q < SLOTS:
                    pool.wait_ge(carried, STEPS * (b + 1) + q - SLOTS + 1)
                tt(slot[:, q % SLOTS, 1:T + 1], dtu[:, k % 2], b_rep[:, n], ALU.mult).then_inc(dbu_done, 1)

            def sum_tiles(d, h, image, t):
                if t == 0:
                    pool.wait_ge(x_loaded[h], 16 * (image + 1))
                    if not isinstance(d, int) or d > 1:
                        pool.wait_ge(mean_full, d)
                    tt(xsum[:], xn[:, h, 0], xn[:, h, 1], ALU.add).then_inc(sum_step, 1)
                else:
                    pool.wait_ge(sum_step, d)
                    tt(xsum[:], xsum[:], xn[:, h, 2], ALU.add).then_inc(x_summed, 1)

            def gate_y(c, h, k):
                pool.wait_ge(y_read, KT * c + k + 1)
                pool.wait_ge(z_read, KT * c + k + 1)
                tt(u[:, h, k], yy[:], gate[:, k % 2], ALU.mult).then_inc(gated, 1)

            def scan(b, h, before, after):
                c = 2 * b + h
                for q in range(STEPS):
                    drive(b, h, q // NS, q % NS)
                    for t in range(CT - 1):
                        if after and q == SUM_AT[t]:
                            sum_tiles(c + 1, 1 - h, b + h, t)
                    for k in range(KT):
                        if k < KT - 1 and q == GATE_Y_AT[k]:
                            gate_y(c, h, k)
                        if q == DT_ADD_AT[k] and (after or k >= EARLY):
                            dt_add(c + 1 if k < EARLY else c, k)
                    if before and q == GATE_Y_AT[KT - 1]:
                        gate_y(c - 1, 1 - h, KT - 1)
                    if q % NS == DT_U_AT:
                        if q // NS + 1 < KT:
                            dt_u(c, h, q // NS + 1)
                        elif after:
                            dt_u(c + 1, 1 - h, 0)

            for m in range(EARLY):
                dt_add(0, m)
            dt_u(0, 0, 0)
            scan(0, 0, False, True)
            with pool.Fori(0, NCHUNK // 2 - 1) as i:
                scan(i, 1, True, True)
                scan(i + 1, 0, True, True)
            scan(B - 1, 1, True, False)
            gate_y(NCHUNK - 1, 1, KT - 1)

        @block.vector
        def _(dve):
            v = nc.vector
            v.memset(yy[:], 0.0)

            def norm_center(d, h, image):
                dve.wait_ge(mean_full, d + 1)
                dve.wait_ge(x_loaded[h], 16 * (image + 1))
                v.tensor_tensor(xn[:, h], xn[:, h], pz[:].unsqueeze(1).broadcast_to([P, CT, T]), ALU.subtract).then_inc(centered, 1)

            def norm_scale(d, h):
                dve.wait_ge(rstd_done, d + 1)
                v.tensor_tensor(xn[:, h], xn[:, h], rstd[:].unsqueeze(1).broadcast_to([P, CT, T]), ALU.mult).then_inc(normed, 1)

            def conv(d, m):
                j = m % 2
                dve.wait_ge(in_read, KT * d + m + 1)
                v.scalar_tensor_tensor(acc[:, j], xin[:, j, 1:T + 1], cw[:, m, 1:2], acc[:, j], ALU.mult, ALU.add).then_inc(conv_part, 1)
                dve.wait_ge(conv_part, KT * d + m + 1)
                v.scalar_tensor_tensor(acc[:, j], xin[:, j, 0:T], cw[:, m, 0:1], acc[:, j], ALU.mult, ALU.add).then_inc(conv_done, 1)

            def conv_silu(d, h, m):
                dve.wait_ge(th_done, KT * d + m + 1)
                if m == 0 and (not isinstance(d, int) or d >= 2):
                    dve.wait_ge(out_full, CT * (d - 1))
                v.scalar_tensor_tensor(u[:, h, m], th[:, m % 2], 1.0, acc[:, m % 2], ALU.add, ALU.mult).then_inc(u_done, 1)

            def split(d):
                dve.wait_ge(xp_full, d + 1)
                if not isinstance(d, int) or d > 0:
                    dve.wait_ge(cc_full, NS * d)
                    dve.wait_ge(dt_full, KT * d)
                v.tensor_copy(parts[0:ROWS, :], pb[0:ROWS, :]).then_inc(split_step, 1)
                dve.wait_ge(split_step, d + 1)
                v.tensor_tensor(parts[BC:2 * BC, :], pb[BC:2 * BC, :], parts[BC:2 * BC, :], ALU.subtract)
                v.tensor_tensor(parts[DTL:ROWS, :], pb[DTL:ROWS, :], parts[DTL:ROWS, :], ALU.subtract).then_inc(bc_done, 1)

            def recur(b, h, k, n):
                c = 2 * b + h
                q = NS * k + n
                s = STEPS * c + q
                dve.wait_ge(exp_done, s + 1)
                dve.wait_ge(dbu_done, s + 1)
                if h == 1 and q == 0:
                    dve.wait_ge(carried, STEPS * (b + 1))
                at = slot[:, q % SLOTS, 1:T + 1]
                v.tensor_tensor_scan(at, da[q % 3][:], at, carry[:, q:q + 1] if h else 0.0, ALU.mult,
                                     ALU.add).then_inc(scan_done, 1)

            def times_c(c, h, k, n):
                q = NS * k + n
                s = STEPS * c + q
                dve.wait_ge(scan_done, s + 1)
                if k == 0:
                    dve.wait_ge(cc_copied, NS * c + n + 1)
                v.tensor_tensor(slot[:, q % SLOTS, 0:T], slot[:, q % SLOTS, 1:T + 1], c_rep[:, n],
                                ALU.mult).then_inc(mult_done, 1)

            def gate_z(c, k):
                dve.wait_ge(z_tanh, KT * c + k + 1)
                v.scalar_tensor_tensor(gate[:, k % 2], gate[:, k % 2], 1.0, pg[GATE_IN[k]][:], ALU.add, ALU.mult).then_inc(z_read, 1)

            def read_y(c, h, k):
                dve.wait_ge(red_done, STEPS * c + NS * (k + 1))
                if not isinstance(c, int) or KT * c + k > 0:
                    dve.wait_ge(gated, KT * c + k)
                v.scalar_tensor_tensor(yy[:], u[:, h, k], dskip[:, k:k + 1], ys[k % 2][:], ALU.mult, ALU.add).then_inc(y_read, 1)

            def residual(c, m, banks=OUT_IN):
                dve.wait_ge(out_full, CT * c + m + 1)
                dve.wait_ge(xres_loaded, 16 * (c + 1))
                v.tensor_tensor(xres[:, m], xres[:, m], pg[banks[m]][:], ALU.add).then_inc(res_done, 1)

            def scan(b, h, before, after):
                c = 2 * b + h
                d = c + 1
                recur(b, h, 0, 0)
                for q in range(STEPS):
                    if q + 1 < STEPS:
                        recur(b, h, (q + 1) // NS, (q + 1) % NS)
                    times_c(c, h, q // NS, q % NS)
                    for m in range(CT):
                        if before and q == OUT_AT[m] + KT + 1:
                            residual(c - 1, m)
                    if before and q == READ_Y_AT:
                        read_y(c - 1, 1 - h, KT - 1)
                    if q >= NS and q % NS == READ_Y_AT:
                        read_y(c, h, q // NS - 1)
                    for k in range(KT):
                        if q == GATE_AT[k] + CT + LAG:
                            gate_z(c, k)
                        if after and q == IN_AT[k] + CT + LAG:
                            conv(d, k)
                        if after and q == IN_AT[k] + CT + LAG + CONV_LAG:
                            conv_silu(d, 1 - h, k)
                    if after and q == MEAN_AT + CT + 1:
                        norm_center(d, 1 - h, b + h)
                    if after and q == VAR_AT + CT + LAG:
                        norm_scale(d, 1 - h)
                    if after and q == XP_AT + KT + 1:
                        split(d)

            v.memset(w_x[:, :, DTH + DTR:DTL], 0.0)
            v.memset(w_dt_hi[DTH:P, :].bitcast(F32), 0.0).then_inc(dt_w_step, 1)
            dve.wait_ge(consts, 1)
            v.tensor_copy(sel[:], sel_f[:])
            norm_center(0, 0, 0)
            dve.wait_ge(params_in, 16 * 5)
            v.tensor_scalar(cw[:], cw[:], 0.5, None, ALU.mult)
            v.tensor_scalar(cb[:], cb[:], 0.5, None, ALU.mult)
            norm_scale(0, 0)
            dve.wait_ge(dt_w_in, 32)
            dve.wait_ge(dt_w_step, 1)
            for r in (DTH, DTL):
                v.tensor_copy(w_dt_hi[r:r + DTR, :], w_dt_raw[r:r + DTR, :]).then_inc(dt_w_step, 1)
            dve.wait_ge(dt_w_step, 2)
            rows = slice(DTH, DTH + DTR)
            v.tensor_tensor(w_dt_lo[rows, :], w_dt_raw[rows, :], w_dt_hi[rows, :], ALU.subtract).then_inc(w_dt_set, 1)
            dve.wait_ge(a_exp, 1)
            v.tensor_scalar(aneg[:], aneg[:], -1.0, None, ALU.mult).then_inc(halved, 1)
            dve.wait_ge(halved, 1)
            conv(0, 0)
            for m in range(KT):
                if m + 1 < KT:
                    conv(0, m + 1)
                conv_silu(0, 0, m)
            split(0)
            dve.wait_ge(out_w_in, 16)
            v.tensor_scalar(w_out[:], w_out[:], 0.5, None, ALU.mult).then_inc(out_halved, 1)
            scan(0, 0, False, True)
            with dve.Fori(0, NCHUNK // 2 - 1) as i:
                scan(i, 1, True, True)
                scan(i + 1, 0, True, True)
            scan(B - 1, 1, True, False)
            read_y(NCHUNK - 1, 1, KT - 1)
            for m in range(CT):
                residual(NCHUNK - 1, m, LAST_OUT_IN)


GROUPS = 5
FFN_B = GROUPS * (B // GROUPS)
HID = 4 * DM
MT = HID // P
Q_EPS, Q_BOUND = 1e-5, 128.0
Q_CLIP = Q_BOUND - Q_EPS
HALVES = HW // T
BEHIND = 4
MEAN_BEFORE = MT - 2


def ffn(nc, layer, signals, x_in, x_out, W1T, b1, W2T, b2):
    assert B // GROUPS == 1
    with ExitStack() as ctx:
        def sb(name, shape, dt=F32):
            return ctx.enter_context(nc.sbuf_tensor(f"{name}_f{layer}", shape, dt))

        def sem(name):
            if name not in signals:
                signals[name] = nc.alloc_semaphore(f"{name}_f")
            return signals[name]

        def bank(name):
            return ctx.enter_context(nc.psum_tensor(f"{name}_f{layer}", [P, T], F32))

        w1 = sb("w1", [P, CT, HID], F32R)
        w2 = sb("w2", [P, MT, DM], F32R)
        hid = sb("hid", [P, MT, HW])
        raw1 = hid[:, 0:MT // 2, :].rearrange("p m n -> p (m n)")[:, 0:CT * HID].rearrange("p (t n) -> p t n", t=CT)
        raw2 = hid[:, MT // 2:, :].rearrange("p m n -> p (m n)")[:, 0:MT * DM].rearrange("p (t n) -> p t n", t=MT)
        bias1 = sb("bias1", [P, MT])
        bias2 = sb("bias2", [P, CT])
        wsum = sb("wsum", [P, 2, GROUPS])
        wmean = sb("wmean", [P, 2, GROUPS])
        ones = sb("ones", [P, P])
        mean_w = sb("mean_w", [P, P])
        ident = sb("ident", [P, P])
        eps_t = sb("eps_t", [P, 1])
        xn = sb("xn", [P, CT, HW])
        xh = sb("xh", [P, CT, HW], F32R)
        xl = sb("xl", [P, CT, HW], F32R)
        sq = sb("sq", [P, HALVES, CT, T])
        xsum = sb("xsum", [P, HW])
        rstd = sb("rstd", [P, HW])
        xres = sb("xres", [P, CT, HW])
        y2 = sb("y2", [P, CT, HW])
        g = sb("g", [P, 2, HW])
        gh = sb("gh", [P, 3, HW], F32R)
        gl = sb("gl", [P, 3, HW], F32R)
        big = sb("big", [P, 2, MT])
        top = sb("top", [P, 2])
        top1 = sb("top1", [P, 2])
        gain = [sb(f"gain{j}", [P, 1]) for j in range(2)]
        acc = [bank(f"acc{j}") for j in range(CT * HALVES)]
        ph = [bank(f"ph{j}") for j in range(HALVES)]

        w1_in, w2_in, bias_in, consts, const_step = sem("w1_in"), sem("w2_in"), sem("bias_in"), sem("consts"), sem("const_step")
        summed, sums_full, means_done, signed = sem("summed"), sem("sums_full"), sem("means_done"), sem("signed")
        x_loaded, xres_loaded, stored = sem("x_loaded"), sem("xres_loaded"), sem("stored")
        sum_step, x_summed = sem("sum_step"), sem("x_summed")
        mean_full, centered, squared, var_full = sem("mean_full"), sem("centered"), sem("squared"), sem("var_full")
        ln_read, rstd_done, normed, split_hi, split_lo = sem("ln_read"), sem("rstd_done"), sem("normed"), sem("split_hi"), sem("split_lo")
        up_full, up_read, up_max = sem("up_full"), sem("up_read"), sem("up_max")
        gelu_done, g_hi, g_lo, down_full = sem("gelu_done"), sem("g_hi"), sem("g_lo"), sem("down_full")
        down_read, down_max, quant, added = sem("down_read"), sem("down_max"), sem("quant"), sem("added")
        top_col, top_row, top_one, top_all, top_eps, top_inv, gain_done = (
            [sem(f"{n}{j}") for j in range(2)] for n in
            ("top_col", "top_row", "top_one", "top_all", "top_eps", "top_inv", "gain_done"))
        block = ctx.enter_context(nc.Block())
        XIN = x_in.rearrange("b (t p) s -> b p t s", p=P)
        XOUT = x_out.rearrange("b (t p) s -> b p t s", p=P)

        @block.sync
        def _(sp):
            sp.dma_start(xn[:], XIN[0]).then_inc(x_loaded, 16)
            sp.dma_start(raw1, W1T.rearrange("(t p) n -> p t n", p=P)).then_inc(w1_in, 16)
            sp.dma_start(raw2, W2T.rearrange("(t p) n -> p t n", p=P)).then_inc(w2_in, 16)
            sp.dma_start(bias1[:], b1.rearrange("(t p) -> p t", p=P), allow_slow_non_contiguous=True).then_inc(bias_in, 16)
            sp.dma_start(bias2[:], b2.rearrange("(t p) -> p t", p=P), allow_slow_non_contiguous=True).then_inc(bias_in, 16)

            def load(i):
                sp.wait_ge(split_lo, HALVES * i)
                sp.dma_start(xn[:], XIN[i]).then_inc(x_loaded, 16)

            def finish(i, more):
                sp.wait_ge(added, i + 1)
                sp.dma_start(XOUT[i], y2[:]).then_inc(stored, 16)
                if more:
                    sp.dma_start(xres[:], XIN[i + 1]).then_inc(xres_loaded, 16)

            sp.dma_start(xres[:], XIN[0]).then_inc(xres_loaded, 16)
            load(1)
            load(2)
            with sp.Fori(0, FFN_B - 3) as i:
                load(i + 3)
                finish(i, True)
            for i in range(FFN_B - 3, FFN_B):
                finish(i, i < FFN_B - 1)
            sp.wait_ge(stored, 16 * FFN_B)

        @block.tensor
        def _(pe):
            mm = nc.tensor.matmul

            def norm_mean(i):
                if isinstance(i, int) and i == 0:
                    pe.wait_ge(x_loaded, 16)
                else:
                    pe.wait_ge(x_summed, i)
                for h in range(HALVES):
                    if not isinstance(i, int) or i > 0:
                        pe.wait_ge(up_read, HALVES * (MT * (i - 1) + MEAN_BEFORE - 1) + h + 1)
                    if isinstance(i, int) and i == 0:
                        for t in range(CT):
                            last = mm(ph[h][:], mean_w[:], xn[:, t, h * T:(h + 1) * T], start=t == 0, stop=t == CT - 1)
                    else:
                        last = mm(ph[h][:], mean_w[:], xsum[:, h * T:(h + 1) * T], start=True, stop=True)
                    last.then_inc(mean_full, 1)

            def norm_var(i):
                for h in range(HALVES):
                    pe.wait_ge(squared, HALVES * i + h + 1)
                    if not isinstance(i, int) or i > 0:
                        pe.wait_ge(up_read, HALVES * (MT * i - 1) + h + 1)
                    for t in range(CT):
                        last = mm(ph[h][:], mean_w[:], sq[:, h, t], start=t == 0, stop=t == CT - 1)
                    last.then_inc(var_full, 1)

            def up(i, m, mean_between):
                for h in range(HALVES):
                    if m == 0:
                        pe.wait_ge(split_lo, HALVES * i + h + 1)
                        pe.wait_ge(split_hi, HALVES * i + h + 1)
                    elif m == MEAN_BEFORE and mean_between:
                        pe.wait_ge(centered, HALVES * (i + 1) + h + 1)
                    else:
                        pe.wait_ge(up_read, HALVES * (MT * i + m - 1) + h + 1)
                    for part, x in enumerate((xh, xl)):
                        for t in range(CT):
                            last = mm(ph[h][:], w1[:, t, m * P:(m + 1) * P], x[:, t, h * T:(h + 1) * T],
                                      start=part == 0 and t == 0, stop=part == 1 and t == CT - 1)
                    last.then_inc(up_full, 1)

            def down(i, k):
                for part, (x, ready) in enumerate(((gh, g_hi), (gl, g_lo))):
                    pe.wait_ge(ready, MT * i + k + 1)
                    for m in range(CT):
                        for h in range(HALVES):
                            if k == 0 and part == 0 and (not isinstance(i, int) or i > 0):
                                pe.wait_ge(down_read, CT * HALVES * i)
                                pe.wait_ge(gain_done[1], i)
                            last = mm(acc[HALVES * m + h][:], w2[:, k, m * P:(m + 1) * P],
                                      x[:, k % 3, h * T:(h + 1) * T], start=k == 0 and part == 0,
                                      stop=k == MT - 1 and part == 1)
                last.then_inc(down_full, 1)

            def top_to_row(i, j):
                pe.wait_ge(top_col[j], i + 1)
                mm(acc[2 * j][0:1, 0:P], top[:, j:j + 1], ident[:], start=True, stop=True).then_inc(top_row[j], 1)

            def top_to_all(i, j):
                pe.wait_ge(top_one[j], i + 1)
                mm(acc[2 * j + 1][:, 0:1], ones[0:1, :], top1[0:1, j:j + 1], start=True, stop=True).then_inc(top_all[j], 1)

            def image(i, more, more2):
                if more:
                    norm_var(i + 1)
                top_to_row(i, 0)
                top_to_all(i, 0)
                for k in range(MT):
                    down(i, k)
                    if more and k >= BEHIND:
                        up(i + 1, k - BEHIND, more2)
                if more:
                    for m in range(MT - BEHIND, MT):
                        if m == MEAN_BEFORE and more2:
                            norm_mean(i + 2)
                        up(i + 1, m, more2)
                        if m == MT - 2:
                            top_to_row(i, 1)
                    top_to_all(i, 1)
                else:
                    top_to_row(i, 1)
                    top_to_all(i, 1)

            pe.wait_ge(consts, 1)
            norm_mean(0)
            norm_var(0)
            pe.wait_ge(summed, GROUPS)
            mm(acc[0][:, 0:GROUPS], ones[:], wsum[:, 0], start=True, stop=True).then_inc(sums_full, 1)
            pe.wait_ge(signed, 1)
            for m in range(MT):
                if m == 2:
                    pe.wait_ge(summed, 2 * GROUPS)
                    mm(acc[2][:, 0:GROUPS], ones[:], wsum[:, 1], start=True, stop=True).then_inc(sums_full, 1)
                if m == MEAN_BEFORE:
                    norm_mean(1)
                up(0, m, True)
            pe.wait_ge(signed, 2)
            image(0, True, True)
            with pe.Fori(1, FFN_B - 2) as i:
                image(i, True, True)
            image(FFN_B - 2, True, False)
            image(FFN_B - 1, False, False)

        @block.scalar
        def _(act):
            af = nc.scalar.activation

            def norm_square(i, h):
                act.wait_ge(centered, HALVES * i + h + 1)
                if not isinstance(i, int) or i > 0:
                    act.wait_ge(var_full, HALVES * (i - 1) + h + 1)
                af(sq[:, h], xn[:, :, h * T:(h + 1) * T], ACT.Square).then_inc(squared, 1)

            def norm_rstd(i):
                nc.scalar.preload_act_table_set("natural_log_exp_and_others")
                for h in range(HALVES):
                    act.wait_ge(var_full, HALVES * i + h + 1)
                    if not isinstance(i, int) or i > 0:
                        act.wait_ge(normed, HALVES * i)
                    af(rstd[:, h * T:(h + 1) * T], ph[h][:], ACT.Ln, bias=eps_t[:, 0:1]).then_inc(ln_read, 1)
                for h in range(HALVES):
                    act.wait_ge(ln_read, HALVES * i + h + 1)
                    r = rstd[:, h * T:(h + 1) * T]
                    af(r, r, ACT.Exp, scale=-0.5).then_inc(rstd_done, 1)

            def up_bias(i, m):
                for h in range(HALVES):
                    act.wait_ge(up_full, HALVES * (MT * i + m) + h + 1)
                    if h == 0 and (not isinstance(i, int) or i > 0):
                        act.wait_ge(gelu_done, MT * (i - 1) + m + 1)
                        act.wait_ge(up_max, MT * (i - 1) + m + 1)
                    af(hid[:, m, h * T:(h + 1) * T], ph[h][:], ACT.Identity, bias=bias1[:, m:m + 1]).then_inc(up_read, 1)

            def gelu(i, k):
                if k == 0:
                    act.wait_ge(gain_done[0], i + 1)
                if k >= 2 or not isinstance(i, int) or i > 0:
                    act.wait_ge(g_lo, MT * i + k - 1)
                af(g[:, k % 2], hid[:, k], ACT.Gelu, scale=gain[0][:]).then_inc(gelu_done, 1)

            def down_bias(i):
                act.wait_ge(down_full, MT * (i + 1))
                if not isinstance(i, int) or i > 0:
                    act.wait_ge(stored, 16 * i)
                for m in range(CT):
                    for h in range(HALVES):
                        af(y2[:, m, h * T:(h + 1) * T], acc[HALVES * m + h][:], ACT.Identity,
                           bias=bias2[:, m:m + 1]).then_inc(down_read, 1)

            def image(i, more, more2):
                for k in range(MT):
                    gelu(i, k)
                    if more and k == 1:
                        norm_rstd(i + 1)
                    if more and k >= BEHIND + 1:
                        up_bias(i + 1, k - BEHIND - 1)
                if more:
                    up_bias(i + 1, MT - BEHIND - 1)
                down_bias(i)
                if more:
                    for m in range(MT - BEHIND, MT):
                        up_bias(i + 1, m)
                        if more2 and m >= MT - 2:
                            norm_square(i + 2, m - (MT - 2))

            def sign(j, w, raw, n, q):
                size = n // GROUPS
                last = af(w[:, :, q * size:(q + 1) * size], raw[:, :, q * size:(q + 1) * size], ACT.Sign,
                          bias=wmean[:, j, q:q + 1])
                if q == GROUPS - 1:
                    last.then_inc(signed, 1)

            norm_square(0, 0)
            norm_square(0, 1)
            norm_rstd(0)
            act.wait_ge(means_done, 1)
            for q in range(GROUPS):
                sign(0, w1, raw1, HID, q)
            act.wait_ge(signed, 1)
            act.wait_ge(bias_in, 32)
            for m in range(MT):
                if m == 3:
                    act.wait_ge(means_done, 2)
                    for q in range(GROUPS):
                        sign(1, w2, raw2, DM, q)
                if m == MT // 2:
                    act.wait_ge(signed, 2)
                up_bias(0, m)
                if m >= MT - 2:
                    norm_square(1, m - (MT - 2))
            image(0, True, True)
            with act.Fori(1, FFN_B - 2) as i:
                image(i, True, True)
            image(FFN_B - 2, True, False)
            image(FFN_B - 1, False, False)

        @block.vector
        def _(dve):
            v = nc.vector

            def norm_center(i, h):
                dve.wait_ge(mean_full, HALVES * i + h + 1)
                dve.wait_ge(x_loaded, 16 * (i + 1))
                x = xn[:, :, h * T:(h + 1) * T]
                v.tensor_tensor(x, x, ph[h][:].unsqueeze(1).broadcast_to([P, CT, T]), ALU.subtract).then_inc(centered, 1)

            def norm_scale(i, h):
                dve.wait_ge(rstd_done, HALVES * i + h + 1)
                s = slice(h * T, (h + 1) * T)
                v.tensor_tensor(xn[:, :, s], xn[:, :, s], rstd[:, s].unsqueeze(1).broadcast_to([P, CT, T]),
                                ALU.mult).then_inc(normed, 1)
                dve.wait_ge(normed, HALVES * i + h + 1)
                if not isinstance(i, int) or i > 0:
                    dve.wait_ge(up_full, HALVES * MT * i)
                v.tensor_copy(xh[:, :, s], xn[:, :, s]).then_inc(split_hi, 1)

            def up_largest(i, m):
                dve.wait_ge(up_read, HALVES * (MT * i + m + 1))
                v.tensor_reduce(big[:, 0, m:m + 1], hid[:, m], AX.X, ALU.max, apply_absolute_value=True).then_inc(up_max, 1)

            def gelu_split(i, k):
                dve.wait_ge(gelu_done, MT * i + k + 1)
                if k >= 3 or not isinstance(i, int) or i > 0:
                    dve.wait_ge(down_full, MT * i + k - 2)
                v.tensor_scalar(gh[:, k % 3], g[:, k % 2], Q_CLIP, -Q_CLIP, ALU.min, ALU.max).then_inc(g_hi, 1)
                dve.wait_ge(g_hi, MT * i + k + 1)
                v.scalar_tensor_tensor(gl[:, k % 3], g[:, k % 2], Q_CLIP, gh[:, k % 3], ALU.min, ALU.subtract).then_inc(g_lo, 1)

            def top_of_tiles(i, j, n, done, total):
                dve.wait_ge(done, total)
                v.tensor_reduce(top[:, j:j + 1], big[:, j, 0:n], AX.X, ALU.max).then_inc(top_col[j], 1)

            def make_gain(i, j):
                dve.wait_ge(top_row[j], i + 1)
                v.tensor_reduce(top1[0:1, j:j + 1], acc[2 * j][0:1, 0:P], AX.X, ALU.max).then_inc(top_one[j], 1)
                dve.wait_ge(top_all[j], i + 1)
                v.tensor_scalar(gain[j][:], acc[2 * j + 1][:, 0:1], Q_EPS, 1.0 / Q_BOUND, ALU.add, ALU.mult).then_inc(top_eps[j], 1)
                dve.wait_ge(top_eps[j], i + 1)
                v.reciprocal(gain[j][:], gain[j][:]).then_inc(gain_done[j], 1)

            def result_largest(i):
                dve.wait_ge(down_read, CT * HALVES * (i + 1))
                v.tensor_reduce(big[:, 1, 0:CT], y2[:], AX.X, ALU.max, apply_absolute_value=True).then_inc(down_max, 1)
                top_of_tiles(i, 1, CT, down_max, i + 1)

            def quantise(i):
                dve.wait_ge(gain_done[1], i + 1)
                v.tensor_scalar(y2[:], y2[:], gain[1][:], Q_CLIP, ALU.mult, ALU.min).then_inc(quant, 1)

            def add_residual(i):
                dve.wait_ge(quant, i + 1)
                dve.wait_ge(xres_loaded, 16 * (i + 1))
                v.scalar_tensor_tensor(y2[:].rearrange("p t s -> p (t s)"), y2[:].rearrange("p t s -> p (t s)"), -Q_CLIP,
                                       xres[:].rearrange("p t s -> p (t s)"), ALU.max, ALU.add).then_inc(added, 1)

            def image(i, more, more2, before):
                top_of_tiles(i, 0, MT, up_max, MT * (i + 1))
                make_gain(i, 0)
                for k in range(MT):
                    gelu_split(i, k)
                    if more and k in (1, 2):
                        norm_scale(i + 1, k - 1)
                    if before and k == BEHIND + 1:
                        quantise(i - 1)
                    if before and k == BEHIND + 2:
                        add_residual(i - 1)
                    if more and k >= BEHIND + 2:
                        up_largest(i + 1, k - BEHIND - 2)
                if more:
                    for m in range(MT - BEHIND - 2, MT):
                        up_largest(i + 1, m)
                        if m == MT - 5:
                            result_largest(i)
                        if more2 and m == MEAN_BEFORE - 1:
                            norm_center(i + 2, 0)
                            norm_center(i + 2, 1)
                        if m == MT - 2:
                            make_gain(i, 1)
                else:
                    result_largest(i)
                    make_gain(i, 1)

            norm_center(0, 0)
            norm_center(0, 1)

            def group_sums(j, raw, n):
                size = n // GROUPS
                for q in range(GROUPS):
                    v.tensor_reduce(wsum[:, j, q:q + 1], raw[:, :, q * size:(q + 1) * size], AX.XY, ALU.add).then_inc(summed, 1)

            v.memset(w1[:, :, GROUPS * (HID // GROUPS):].bitcast(F32), 0.0)
            v.memset(w2[:, :, GROUPS * (DM // GROUPS):].bitcast(F32), 0.0)
            dve.wait_ge(w1_in, 16)
            group_sums(0, raw1, HID)
            dve.wait_ge(sums_full, 1)
            v.tensor_scalar(wmean[:, 0], acc[0][:, 0:GROUPS], -1.0 / (HID // GROUPS * DM), None, ALU.mult).then_inc(means_done, 1)
            norm_scale(0, 0)
            norm_scale(0, 1)
            dve.wait_ge(w2_in, 16)
            group_sums(1, raw2, DM)
            dve.wait_ge(sums_full, 2)
            v.tensor_scalar(wmean[:, 1], acc[2][:, 0:GROUPS], -1.0 / (DM // GROUPS * HID), None, ALU.mult).then_inc(means_done, 1)
            for m in range(MT):
                up_largest(0, m)
                if m == MEAN_BEFORE - 1:
                    norm_center(1, 0)
                    norm_center(1, 1)
            image(0, True, True, False)
            with dve.Fori(1, FFN_B - 2) as i:
                image(i, True, True, True)
            image(FFN_B - 2, True, False, True)
            image(FFN_B - 1, False, False, True)
            quantise(FFN_B - 1)
            add_residual(FFN_B - 1)

        @block.gpsimd
        def _(pool):
            nc.gpsimd.memset(ident[:], 0.0).then_inc(const_step, 1)
            nc.gpsimd.memset(ones[:], 1.0)
            nc.gpsimd.memset(mean_w[:], 1.0 / DM)
            nc.gpsimd.memset(eps_t[:], 1e-5)
            pool.wait_ge(const_step, 1)
            nc.gpsimd.affine_select(out=ident[:], in_=ident[:], compare_op=ALU.not_equal, fill=1.0, base=0,
                                    pattern=[[-1, P]], channel_multiplier=1).then_inc(consts, 1)

            def split_rest(i):
                for h in range(HALVES):
                    pool.wait_ge(split_hi, HALVES * i + h + 1)
                    s = slice(h * T, (h + 1) * T)
                    nc.gpsimd.tensor_tensor(xl[:, :, s], xn[:, :, s], xh[:, :, s], ALU.subtract).then_inc(split_lo, 1)

            def sum_tiles(i):
                pool.wait_ge(x_loaded, 16 * (i + 1))
                if not isinstance(i, int) or i > 1:
                    pool.wait_ge(mean_full, HALVES * i)
                nc.gpsimd.tensor_tensor(xsum[:], xn[:, 0], xn[:, 1], ALU.add).then_inc(sum_step, 1)
                pool.wait_ge(sum_step, i)
                nc.gpsimd.tensor_tensor(xsum[:], xsum[:], xn[:, 2], ALU.add).then_inc(x_summed, 1)

            assert CT == 3
            split_rest(0)
            sum_tiles(1)
            with pool.Fori(1, FFN_B - 1) as i:
                split_rest(i)
                sum_tiles(i + 1)
            split_rest(FFN_B - 1)


NPOS = 48
CPP = DM // NPOS
SIDE = 32
SIDES = P // SIDE
PPG = SIDE // CPP
MAGIC = 1.5 * 2.0 ** 23
NMAT = 2 * CT * PPG


def displace(nc, signals, x_in, x_mid, x_out, offset):
    with ExitStack() as ctx:
        def sb(name, shape, dt=F32):
            return ctx.enter_context(nc.sbuf_tensor(name + "_d", shape, dt))

        def sem(name):
            return ctx.enter_context(nc.semaphore(name + "_d"))

        def bank(name):
            return ctx.enter_context(nc.psum_tensor(name + "_d", [P, T], F32))

        lag_i = sb("lag_i", [P, SIDE], mybir.dt.int32)
        lag = sb("lag", [P, SIDE])
        blocks = sb("blocks", [P, NMAT, SIDE])
        off = sb("off", [P, NMAT])
        whole = sb("whole", [P, NMAT])
        part = sb("part", [P, NMAT])
        scale = sb("scale", [P, NMAT])
        tmp = sb("tmp", [P, 4, NMAT])
        tap = sb("tap", [P, 5, NMAT])
        mats = sb("mats", [P, NMAT, P])
        work = sb("work", [P, NMAT, SIDE])
        mean_w = sb("mean_w", [P, P])
        eps_c = sb("eps_c", [P, 1])
        xn = sb("xn", [P, CT, HW])
        xc = sb("xc", [P, CT, HW])
        sq = sb("sq", [P, HALVES, CT, T])
        rstd = sb("rstd", [P, HW])
        xres = sb("xres", [P, CT, HW])
        res = sb("res", [P, CT, HW])
        ta = sb("ta", [P, CT, HW])
        tb = sb("tb", [P, CT, HW])
        tc = sb("tc", [P, CT, HW])
        td = sb("td", [P, CT, HW])
        te = sb("te", [P, CT, HW])
        pc = [bank(f"pc{j}") for j in range(2 * CT)]
        ph = [bank(f"ph{j}") for j in range(HALVES)]

        off_in, iotas, made, lag_done = sem("off_in"), sem("iotas"), sem("made"), sem("lag_done")
        step, tapped, gauss, mats_done = sem("step"), sem("tapped"), sem("gauss"), sem("mats_done")
        x_loaded, xres_loaded = sem("x_loaded"), sem("xres_loaded")
        stored = sem("stored")
        mean_full, centered, squared, var_full = sem("mean_full"), sem("centered"), sem("squared"), sem("var_full")
        ln_read, rstd_done, normed, ta_done = sem("ln_read"), sem("rstd_done"), sem("normed"), sem("ta_done")
        x_full, x_read, tc_done = sem("x_full"), sem("x_read"), sem("tc_done")
        y_full, y_read, te_done, added = sem("y_full"), sem("y_read"), sem("te_done"), sem("added")
        block = ctx.enter_context(nc.Block())
        XIN = x_in.rearrange("b (t p) s -> b p t s", p=P)
        MID = x_mid.rearrange("b (t p) s -> b p t s", p=P)
        OUT = x_out.rearrange("b (t p) s -> b p t s", p=P)

        @block.sync
        def _(sp):
            sp.dma_start(xn[:], XIN[0]).then_inc(x_loaded, 16)
            for g in range(SIDES):
                for a in range(2):
                    for t in range(CT):
                        src = offset[(t * SIDES + g) * PPG:(t * SIDES + g + 1) * PPG, a]
                        j = (a * CT + t) * PPG
                        sp.dma_start(off[g * SIDE:(g + 1) * SIDE, j:j + PPG], src.partition_broadcast(SIDE),
                                     allow_slow_non_contiguous=True).then_inc(off_in, 16)
            sp.dma_start(xres[:], XIN[0]).then_inc(xres_loaded, 16)

            def load(i):
                sp.wait_ge(centered, HALVES * i)
                sp.dma_start(xn[:], XIN[i]).then_inc(x_loaded, 16)

            def finish(i, out, more):
                sp.wait_ge(added, CT * (i + 1))
                sp.dma_start(out[i], res[:]).then_inc(stored, 16)
                if more:
                    sp.dma_start(xres[:], XIN[i + 1]).then_inc(xres_loaded, 16)

            load(1)
            load(2)
            with sp.Fori(0, FFN_B) as i:
                load(i + 3)
                finish(i, MID, True)
            for i in range(FFN_B, B):
                finish(i, OUT, i < B - 1)
            sp.wait_ge(stored, 16 * B)

        @block.tensor
        def _(pe):
            mm = nc.tensor.matmul

            def norm_mean(i):
                pe.wait_ge(x_loaded, 16 * (i + 1))
                if not isinstance(i, int) or i > 0:
                    pe.wait_ge(ln_read, HALVES * i)
                for h in range(HALVES):
                    for t in range(CT):
                        last = mm(ph[h][:], mean_w[:], xn[:, t, h * T:(h + 1) * T], start=t == 0, stop=t == CT - 1)
                    last.then_inc(mean_full, 1)

            def norm_var(i):
                for h in range(HALVES):
                    pe.wait_ge(squared, HALVES * i + h + 1)
                    for t in range(CT):
                        last = mm(ph[h][:], mean_w[:], sq[:, h, t], start=t == 0, stop=t == CT - 1)
                    last.then_inc(var_full, 1)

            def axis(i, a, src, ready, full):
                for t in range(CT):
                    pe.wait_ge(ready, CT * i + t + 1)
                    if a == 1:
                        pe.wait_ge(x_read, 2 * CT * i + 2 * t + 2)
                    elif not isinstance(i, int) or i > 0:
                        pe.wait_ge(y_read, 2 * CT * (i - 1) + 2 * t + 2)
                    for q in range(PPG):
                        if a == 0:
                            x = src[:, t].rearrange("p (y c) -> p y c", c=SIDE)[:, :, q * CPP:(q + 1) * CPP]
                        else:
                            x = src[:, t, q * CPP * SIDE:(q + 1) * CPP * SIDE]
                        o = pc[2 * t + q // 2][:, (q % 2) * 256:(q % 2 + 1) * 256]
                        last = mm(o, mats[:, (a * CT + t) * PPG + q], x, start=True, stop=True)
                        if q % 2:
                            last.then_inc(full, 1)

            def image(i, more, more2):
                axis(i, 0, ta, ta_done, x_full)
                if more:
                    norm_var(i + 1)
                axis(i, 1, tc, tc_done, y_full)
                if more2:
                    norm_mean(i + 2)

            pe.wait_ge(made, 1)
            norm_mean(0)
            norm_var(0)
            norm_mean(1)
            pe.wait_ge(mats_done, 1)
            image(0, True, True)
            with pe.Fori(1, B - 2) as i:
                image(i, True, True)
            image(B - 2, True, False)
            image(B - 1, False, False)

        @block.scalar
        def _(act):
            af = nc.scalar.activation

            def norm_square(i, h):
                act.wait_ge(centered, HALVES * i + h + 1)
                if not isinstance(i, int) or i > 0:
                    act.wait_ge(var_full, HALVES * (i - 1) + h + 1)
                af(sq[:, h], xc[:, :, h * T:(h + 1) * T], ACT.Square).then_inc(squared, 1)

            def norm_rstd(i):
                for h in range(HALVES):
                    act.wait_ge(var_full, HALVES * i + h + 1)
                    if not isinstance(i, int) or i > 0:
                        act.wait_ge(normed, HALVES * i)
                    af(rstd[:, h * T:(h + 1) * T], ph[h][:], ACT.Ln, bias=eps_c[:, 0:1]).then_inc(ln_read, 1)
                for h in range(HALVES):
                    act.wait_ge(ln_read, HALVES * i + h + 1)
                    r = rstd[:, h * T:(h + 1) * T]
                    af(r, r, ACT.Exp, scale=-0.5).then_inc(rstd_done, 1)

            def read_x(i, t):
                for j in range(2):
                    act.wait_ge(x_full, 2 * (CT * i + t) + j + 1)
                    if not isinstance(i, int) or i > 0:
                        act.wait_ge(tc_done, CT * (i - 1) + t + 1)
                    o = tb[:, t, j * T:(j + 1) * T].rearrange("p (q c y) -> p q y c", q=2, y=SIDE)
                    for q in range(2):
                        last = af(o[:, q], pc[2 * t + j][:, q * 256:(q + 1) * 256].rearrange("p (y c) -> p y c", c=CPP), ACT.Copy)
                    last.then_inc(x_read, 1)

            def read_y(i):
                for t in range(CT):
                    for j in range(2):
                        act.wait_ge(y_full, 2 * (CT * i + t) + j + 1)
                        if not isinstance(i, int) or i > 0:
                            act.wait_ge(te_done, CT * (i - 1) + t + 1)
                        o = td[:, t].rearrange("p (x c) -> p c x", c=SIDE)[:, j * 16:(j + 1) * 16, :]
                        af(o, pc[2 * t + j][:].rearrange("p (c x) -> p c x", x=SIDE), ACT.Copy).then_inc(y_read, 1)

            def image(i, more):
                for t in range(CT):
                    read_x(i, t)
                    if more and t < HALVES:
                        norm_square(i + 1, t)
                if more:
                    norm_rstd(i + 1)
                read_y(i)

            nc.scalar.preload_act_table_set("natural_log_exp_and_others")
            for h in range(HALVES):
                norm_square(0, h)
            norm_rstd(0)
            act.wait_ge(tapped, 1)
            af(tap[:], tap[:], ACT.Exp, scale=-2.0).then_inc(gauss, 1)
            act.wait_ge(tapped, 2)
            af(blocks[:], blocks[:], ACT.Exp, scale=-2.0).then_inc(gauss, 1)
            image(0, True)
            with act.Fori(1, B - 1) as i:
                image(i, True)
            image(B - 1, False)

        @block.vector
        def _(dve):
            v = nc.vector
            chain = [0]

            def then(instruction):
                chain[0] += 1
                instruction.then_inc(step, 1)
                dve.wait_ge(step, chain[0])

            def over_j(a):
                return a.unsqueeze(1).broadcast_to([P, NMAT, SIDE])

            def over_o(a):
                return a.unsqueeze(2).broadcast_to([P, NMAT, SIDE])

            def norm_center(i):
                dve.wait_ge(x_loaded, 16 * (i + 1))
                for h in range(HALVES):
                    dve.wait_ge(mean_full, HALVES * i + h + 1)
                    if not isinstance(i, int) or i > 0:
                        dve.wait_ge(ta_done, CT * i)
                    v.tensor_tensor(xc[:, :, h * T:(h + 1) * T], xn[:, :, h * T:(h + 1) * T],
                                    ph[h][:].unsqueeze(1).broadcast_to([P, CT, T]), ALU.subtract).then_inc(centered, 1)

            def norm_scale(i):
                for h in range(HALVES):
                    dve.wait_ge(rstd_done, HALVES * i + h + 1)
                    s = slice(h * T, (h + 1) * T)
                    v.tensor_tensor(xc[:, :, s], xc[:, :, s], rstd[:, s].unsqueeze(1).broadcast_to([P, CT, T]),
                                    ALU.mult).then_inc(normed, 1)
                dve.wait_ge(normed, HALVES * (i + 1))
                for t in range(CT):
                    if not isinstance(i, int) or i > 0:
                        dve.wait_ge(x_full, 2 * (CT * (i - 1) + t) + 2)
                    v.transpose(ta[:, t], xc[:, t]).then_inc(ta_done, 1)

            def to_y(i):
                for t in range(CT):
                    dve.wait_ge(x_read, 2 * (CT * i + t) + 2)
                    if not isinstance(i, int) or i > 0:
                        dve.wait_ge(y_full, 2 * (CT * (i - 1) + t) + 2)
                    v.transpose(tc[:, t], tb[:, t]).then_inc(tc_done, 1)

            def to_c(i):
                for t in range(CT):
                    dve.wait_ge(y_read, 2 * (CT * i + t) + 2)
                    if not isinstance(i, int) or i > 0:
                        dve.wait_ge(added, CT * (i - 1) + t + 1)
                    v.transpose(te[:, t], td[:, t]).then_inc(te_done, 1)

            def image(i, before, more, more2):
                to_y(i)
                if before:
                    to_c(i - 1)
                if more:
                    norm_scale(i + 1)
                if more2:
                    norm_center(i + 2)

            norm_center(0)
            dve.wait_ge(off_in, 16 * 2 * CT * SIDES)
            dve.wait_ge(made, 1)
            then(v.tensor_copy(lag[:], lag_i[:]))
            then(v.tensor_scalar(whole[:], off[:], MAGIC, None, ALU.add))
            then(v.tensor_scalar(whole[:], whole[:], MAGIC, None, ALU.subtract))
            then(v.tensor_tensor(part[:], off[:], whole[:], ALU.subtract))
            for j in range(5):
                then(v.tensor_scalar(tap[:, j], part[:], float(j - 2), None, ALU.add))
            dve.wait_ge(step, chain[0])
            v.tensor_tensor(tap[:], tap[:], tap[:], ALU.mult).then_inc(tapped, 1)
            then(v.tensor_tensor(work[:], over_j(lag[:]), over_o(whole[:]), ALU.add))
            then(v.tensor_tensor(blocks[:], work[:], over_o(part[:]), ALU.add))
            v.tensor_tensor(blocks[:], blocks[:], blocks[:], ALU.mult).then_inc(tapped, 1)
            then(v.tensor_tensor(work[:], work[:], work[:], ALU.mult))
            then(v.tensor_scalar(tmp[:, 0], whole[:], lag[:, 0:1], None, ALU.add))
            then(v.tensor_scalar(tmp[:, 1], tmp[:, 0], 0.0, None, ALU.is_ge))
            then(v.scalar_tensor_tensor(tmp[:, 2], tmp[:, 0], float(SIDE - 1), tmp[:, 1], ALU.is_le, ALU.mult))
            dve.wait_ge(gauss, 1)
            then(v.tensor_tensor(tmp[:, 3], tap[:, 0], tap[:, 1], ALU.add))
            for j in range(2, 5):
                then(v.tensor_tensor(tmp[:, 3], tmp[:, 3], tap[:, j], ALU.add))
            then(v.reciprocal(tmp[:, 3], tmp[:, 3]))
            then(v.tensor_tensor(scale[:], tmp[:, 2], tmp[:, 3], ALU.mult))
            dve.wait_ge(gauss, 2)
            flat = "p j o -> p (j o)"
            then(v.scalar_tensor_tensor(blocks[:].rearrange(flat), work[:].rearrange(flat), 4.5, blocks[:].rearrange(flat),
                                        ALU.is_le, ALU.mult))
            then(v.tensor_tensor(blocks[:], blocks[:], over_o(scale[:]), ALU.mult))
            for g in range(SIDES):
                rows = slice(g * SIDE, (g + 1) * SIDE)
                last = v.tensor_copy(mats[rows, :, g * SIDE:(g + 1) * SIDE], blocks[rows])
            last.then_inc(mats_done, 1)

            norm_scale(0)
            norm_center(1)
            image(0, False, True, True)
            image(1, True, True, True)
            with dve.Fori(2, B - 2) as i:
                image(i, True, True, True)
            image(B - 2, True, True, False)
            image(B - 1, True, False, False)
            to_c(B - 1)

        @block.gpsimd
        def _(pool):
            for s in signals.values():
                nc.gpsimd.sem_clear(s)
            nc.gpsimd.memset(mean_w[:], 1.0 / DM)
            nc.gpsimd.memset(eps_c[:], 1e-6)
            nc.gpsimd.memset(mats[:], 0.0).then_inc(iotas, 1)
            for g in range(SIDES):
                pool.wait_ge(iotas, g + 1)
                nc.gpsimd.iota(lag_i[g * SIDE:(g + 1) * SIDE, :], pattern=[[-1, SIDE]], base=0,
                               channel_multiplier=1).then_inc(iotas, 1)
            pool.wait_ge(iotas, SIDES + 1)
            nc.gpsimd.sem_inc(made, 1)

            def add_residual(i):
                pool.wait_ge(xres_loaded, 16 * (i + 1))
                if not isinstance(i, int) or i > 0:
                    pool.wait_ge(stored, 16 * i)
                for t in range(CT):
                    pool.wait_ge(te_done, CT * i + t + 1)
                    nc.gpsimd.tensor_tensor(res[:, t].rearrange("p (y x) -> p y x", x=SIDE),
                                            te[:, t].rearrange("p (x y) -> p y x", y=SIDE),
                                            xres[:, t].rearrange("p (y x) -> p y x", x=SIDE), ALU.add).then_inc(added, 1)

            add_residual(0)
            with pool.Fori(1, B) as i:
                add_residual(i)


def program(nc, x, in_wT, conv_w, conv_b, xp_wT, dt_wT, dt_b, A_log, D, out_wT, W1T_0, b1_0, W2T_0, b2_0,
            offset, W1T_1, b1_1, W2T_1, b2_1, out):
    between = nc.dram_tensor("between_layers", (B, DM, HW), F32).ap()
    mixer(nc, x, between, in_wT, conv_w, conv_b, xp_wT, dt_wT, dt_b, A_log, D, out_wT)
    signals = {}
    ffn(nc, 0, signals, between, between, W1T_0, b1_0, W2T_0, b2_0)
    displace(nc, signals, between, between, out, offset)
    ffn(nc, 1, signals, between, out, W1T_1, b1_1, W2T_1, b2_1)


def kernel(**inputs):
    import numpy as np
    import concourse.bacc as bacc
    from concourse.bass_utils import run_bass_kernel_spmd

    a = {n: np.asarray(v) for n, v in inputs.items()}
    c0 = "L0_conv_"
    arrays = {
        "x": a["x"].reshape(B, DM, HW),
        "in_wT": a[c0 + "in_proj_w"].T, "conv_w": a[c0 + "conv_w"], "conv_b": a[c0 + "conv_b"],
        "xp_wT": a[c0 + "x_proj_w"].T, "dt_wT": a[c0 + "dt_proj_w"].T, "dt_b": a[c0 + "dt_proj_b"],
        "A_log": a[c0 + "A_log"], "D": a[c0 + "D"], "out_wT": a[c0 + "out_proj_w"].T,
        "W1T_0": a["L0_ffn_W1"].T, "b1_0": a["L0_ffn_b1"], "W2T_0": a["L0_ffn_W2"].T, "b2_0": a["L0_ffn_b2"],
        "offset": a["L1_conv_offset"],
        "W1T_1": a["L1_ffn_W1"].T, "b1_1": a["L1_ffn_b1"], "W2T_1": a["L1_ffn_W2"].T, "b2_1": a["L1_ffn_b2"],
    }
    arrays = {f"in_{n}": np.ascontiguousarray(v) for n, v in arrays.items()}
    nc = bacc.Bacc("TRN2", target_bir_lowering=False, num_devices=1)
    args = [nc.dram_tensor(n, v.shape, mybir.dt.from_np(v.dtype), kind="ExternalInput").ap() for n, v in arrays.items()]
    out = nc.dram_tensor("out_dram", (B, DM, HW), F32, kind="ExternalOutput").ap()
    program(nc, *args, out)
    r = run_bass_kernel_spmd(nc, [arrays], core_ids=[0])
    return r.results[0]["out_dram"].reshape(a["x"].shape)
```
